# Optimizing a Trainium2 kernel written in Bass

```python
import numpy as np
import jax
import jax.numpy as jnp

def _softmax(x, axis=-1):
    return jax.nn.softmax(x, axis=axis)

def _gelu(x):
    return jax.nn.gelu(x, approximate=True)

def _silu(x):
    return jax.nn.silu(x)

def _sigmoid(x):
    return jax.nn.sigmoid(x)

def _layernorm(x, axis=-1, eps=1e-05):
    m = jnp.mean(x, axis=axis, keepdims=True)
    v = jnp.var(x, axis=axis, keepdims=True)
    return (x - m) / jnp.sqrt(v + eps)

def _scatter_add(tgt, idx, src, axis=0):
    return tgt.at[idx].add(src)

def _segment_sum(src, seg, n):
    return jax.ops.segment_sum(src, seg, n)
kernel_name = 'mk_gnn_ffn_d2_gnn_r8_b6f683'

def setup_inputs(seed: int=0):
    np.random.seed(seed)
    _w = jnp.asarray

    def _rec_inputs():
        import jax
        import jax.numpy as jnp
        _gk = jax.random.key(seed)
        x = -0.0003713 + 1 * jax.random.normal(jax.random.fold_in(_gk, 1), (6250, 256), jnp.float32)
        _s = jax.random.randint(jax.random.fold_in(_gk, 2), (50000,), 0, 6250, jnp.int32)
        _d = jax.random.randint(jax.random.fold_in(_gk, 3), (50000,), 0, 6250, jnp.int32)
        _loop = jnp.arange(6250, dtype=jnp.int32)
        src = jnp.concatenate([_s, _d, _loop])
        dst = jnp.concatenate([_d, _s, _loop])
        _o = jnp.argsort(dst, stable=True)
        src = src[_o]
        dst = dst[_o]
        edge_attr_256 = -8.513e-05 + 0.999844 * jax.random.normal(jax.random.fold_in(_gk, 12), (106250, 256), jnp.float32)
        edge_weight = jax.random.uniform(jax.random.fold_in(_gk, 13), (106250,), jnp.float32, 0.0, 1)
        node_vec1 = 0.00268188 + 1.0042 * jax.random.normal(jax.random.fold_in(_gk, 14), (6250, 1), jnp.float32)
        return (x, src, dst, edge_attr_256, edge_weight, node_vec1)
    x, src, dst, edge_attr_256, edge_weight, node_vec1 = _rec_inputs()

    def _L0_gnn_setup():
        import jax, jax.numpy as jnp
        import numpy as np
        N = 6250
        E = 200000
        NFEAT = 256
        NHID = 128

        def _graph_conv(x, W, b, edge_src, edge_dst, edge_weight, num_nodes):
            support = x @ W
            msgs = support[edge_src] * edge_weight[:, None]
            agg = jax.ops.segment_sum(msgs, edge_dst, num_segments=num_nodes)
            return agg + b
        key = jax.random.key(seed)
        ks = jax.random.split(key, 8)
        x = jax.random.normal(ks[0], (N, NFEAT), dtype=jnp.float32)
        edge_src = jax.random.randint(ks[1], (E,), 0, N, dtype=jnp.int32)
        edge_dst = jax.random.randint(ks[2], (E,), 0, N, dtype=jnp.int32)
        edge_weight = jax.random.uniform(ks[3], (E,), dtype=jnp.float32)
        W1 = jax.random.normal(ks[4], (NFEAT, NHID), dtype=jnp.float32) / np.sqrt(NFEAT)
        b1 = jax.random.normal(ks[5], (NHID,), dtype=jnp.float32) * 0.01
        W2 = jax.random.normal(ks[6], (NHID, NFEAT), dtype=jnp.float32) / np.sqrt(NHID)
        b2 = jax.random.normal(ks[7], (NFEAT,), dtype=jnp.float32) * 0.01
        return {'x': x, 'edge_src': edge_src, 'edge_dst': edge_dst, 'edge_weight': edge_weight, 'W1': W1, 'b1': b1, 'W2': W2, 'b2': b2}
    _L0_gnn_all = _L0_gnn_setup()
    _L0_gnn_in = {k: v for k, v in _L0_gnn_all.items() if k in ('W1', 'b1', 'W2', 'b2')}
    del _L0_gnn_all

    def _L0_ffn_setup():
        import jax, jax.numpy as jnp
        import numpy as np
        E, D, H, TOP_K = (6, 256, 256, 2)
        ROUTER_H = D // 2
        key = jax.random.key(seed)
        ks = jax.random.split(key, 12)
        s = 1.0 / np.sqrt(D)
        sh = 1.0 / np.sqrt(H)
        sr = 1.0 / np.sqrt(ROUTER_H)
        return {'features': jax.random.normal(ks[0], (8, 512, D), dtype=jnp.float32), 'router_w1': jax.random.uniform(ks[1], (D, ROUTER_H), jnp.float32, -s, s), 'router_b1': jnp.zeros((ROUTER_H,), jnp.float32), 'router_w2': jax.random.uniform(ks[2], (ROUTER_H, E), jnp.float32, -sr, sr), 'router_b2': jnp.zeros((E,), jnp.float32), 'expert_w1': jax.random.uniform(ks[3], (E, D, H), jnp.float32, -s, s), 'expert_b1': jnp.zeros((E, H), jnp.float32), 'expert_w2': jax.random.uniform(ks[4], (E, H, H), jnp.float32, -sh, sh), 'expert_b2': jnp.zeros((E, H), jnp.float32), 'expert_w3': jax.random.uniform(ks[5], (E, H, D), jnp.float32, -sh, sh), 'expert_b3': jnp.zeros((E, D), jnp.float32)}
    _L0_ffn_all = _L0_ffn_setup()
    _L0_ffn_in = {k: v for k, v in _L0_ffn_all.items() if k in ('router_w1', 'router_b1', 'router_w2', 'router_b2', 'expert_w1', 'expert_b1', 'expert_w2', 'expert_b2', 'expert_w3', 'expert_b3')}
    del _L0_ffn_all

    def _L1_gnn_setup():
        import jax, jax.numpy as jnp
        import numpy as np
        N_NODES, N_EDGES, D = (2500, 40000, 256)

        def mish(x):
            return x * jnp.tanh(jax.nn.softplus(x))
        key = jax.random.key(seed)
        ks = jax.random.split(key, 12)
        s = 1.0 / np.sqrt(D)
        return {'node_features': jax.random.normal(ks[0], (N_NODES, D), jnp.float32), 'edge_features': jax.random.normal(ks[1], (N_EDGES, D), jnp.float32), 'targets': jax.random.normal(ks[2], (N_NODES, 1), jnp.float32), 'src': jax.random.randint(ks[3], (N_EDGES,), 0, N_NODES), 'dst': jax.random.randint(ks[4], (N_EDGES,), 0, N_NODES), 'W_dense': jax.random.uniform(ks[5], (D, D), jnp.float32, -s, s), 'b_dense': jax.random.uniform(ks[6], (D,), jnp.float32, -s, s), 'W_edge': jax.random.uniform(ks[7], (D, D), jnp.float32, -s, s), 'b_edge': jax.random.uniform(ks[8], (D,), jnp.float32, -s, s), 'W_out': jax.random.uniform(ks[9], (D, D), jnp.float32, -s, s), 'b_out': jax.random.uniform(ks[10], (D,), jnp.float32, -s, s)}
    _L1_gnn_all = _L1_gnn_setup()
    _L1_gnn_in = {k: v for k, v in _L1_gnn_all.items() if k in ('W_dense', 'b_dense', 'W_edge', 'b_edge', 'W_out', 'b_out')}
    del _L1_gnn_all

    def _L1_ffn_setup():
        import jax, jax.numpy as jnp
        import numpy as np
        E = 8
        K = 2
        D = 256
        H = 512
        DOUT = 256
        EPS = 1e-05
        key = jax.random.key(seed)
        ks = jax.random.split(key, 9)
        s = 0.02
        return {'x': jax.random.normal(ks[0], (4, 1024, D), jnp.float32), 'gamma': 1.0 + 0.05 * jax.random.normal(ks[1], (D,), jnp.float32), 'beta': 0.05 * jax.random.normal(ks[2], (D,), jnp.float32), 'Wr': 0.01 * jax.random.normal(ks[3], (D, E), jnp.float32), 'br': jnp.zeros((E,), jnp.float32), 'W1': s * jax.random.normal(ks[4], (E, D, H), jnp.float32), 'b1': s * jax.random.normal(ks[5], (E, H), jnp.float32), 'W2': s * jax.random.normal(ks[6], (E, H, DOUT), jnp.float32), 'b2': s * jax.random.normal(ks[7], (E, DOUT), jnp.float32)}
    _L1_ffn_all = _L1_ffn_setup()
    _L1_ffn_in = {k: v for k, v in _L1_ffn_all.items() if k in ('gamma', 'beta', 'Wr', 'br', 'W1', 'b1', 'W2', 'b2')}
    del _L1_ffn_all
    return {'x': x, 'src': src, 'dst': dst, 'edge_attr_256': edge_attr_256, 'edge_weight': edge_weight, 'node_vec1': node_vec1, 'L0_gnn_W1': _L0_gnn_in['W1'], 'L0_gnn_b1': _L0_gnn_in['b1'], 'L0_gnn_W2': _L0_gnn_in['W2'], 'L0_gnn_b2': _L0_gnn_in['b2'], 'L0_ffn_router_w1': _L0_ffn_in['router_w1'], 'L0_ffn_router_b1': _L0_ffn_in['router_b1'], 'L0_ffn_router_w2': _L0_ffn_in['router_w2'], 'L0_ffn_router_b2': _L0_ffn_in['router_b2'], 'L0_ffn_expert_w1': _L0_ffn_in['expert_w1'], 'L0_ffn_expert_b1': _L0_ffn_in['expert_b1'], 'L0_ffn_expert_w2': _L0_ffn_in['expert_w2'], 'L0_ffn_expert_b2': _L0_ffn_in['expert_b2'], 'L0_ffn_expert_w3': _L0_ffn_in['expert_w3'], 'L0_ffn_expert_b3': _L0_ffn_in['expert_b3'], 'L1_gnn_W_dense': _L1_gnn_in['W_dense'], 'L1_gnn_b_dense': _L1_gnn_in['b_dense'], 'L1_gnn_W_edge': _L1_gnn_in['W_edge'], 'L1_gnn_b_edge': _L1_gnn_in['b_edge'], 'L1_gnn_W_out': _L1_gnn_in['W_out'], 'L1_gnn_b_out': _L1_gnn_in['b_out'], 'L1_ffn_gamma': _L1_ffn_in['gamma'], 'L1_ffn_beta': _L1_ffn_in['beta'], 'L1_ffn_Wr': _L1_ffn_in['Wr'], 'L1_ffn_br': _L1_ffn_in['br'], 'L1_ffn_W1': _L1_ffn_in['W1'], 'L1_ffn_b1': _L1_ffn_in['b1'], 'L1_ffn_W2': _L1_ffn_in['W2'], 'L1_ffn_b2': _L1_ffn_in['b2']}

def reference(x, src, dst, edge_attr_256, edge_weight, node_vec1, L0_gnn_W1, L0_gnn_b1, L0_gnn_W2, L0_gnn_b2, L0_ffn_router_w1, L0_ffn_router_b1, L0_ffn_router_w2, L0_ffn_router_b2, L0_ffn_expert_w1, L0_ffn_expert_b1, L0_ffn_expert_w2, L0_ffn_expert_b2, L0_ffn_expert_w3, L0_ffn_expert_b3, L1_gnn_W_dense, L1_gnn_b_dense, L1_gnn_W_edge, L1_gnn_b_edge, L1_gnn_W_out, L1_gnn_b_out, L1_ffn_gamma, L1_ffn_beta, L1_ffn_Wr, L1_ffn_br, L1_ffn_W1, L1_ffn_b1, L1_ffn_W2, L1_ffn_b2):
    import jax
    import jax.numpy as jnp

    def _L0_gnn_ref(x, edge_src, edge_dst, edge_weight, W1, b1, W2, b2):
        import jax, jax.numpy as jnp
        import numpy as np
        N = 6250
        E = 200000
        NFEAT = 256
        NHID = 128

        def _graph_conv(x, W, b, edge_src, edge_dst, edge_weight, num_nodes):
            support = x @ W
            msgs = support[edge_src] * edge_weight[:, None]
            agg = jax.ops.segment_sum(msgs, edge_dst, num_segments=num_nodes)
            return agg + b
        n = x.shape[0]
        h = _graph_conv(x, W1, b1, edge_src, edge_dst, edge_weight, n)
        h = jax.nn.relu(h)
        out = _graph_conv(h, W2, b2, edge_src, edge_dst, edge_weight, n)
        return out

    def _L0_ffn_ref(features, router_w1, router_b1, router_w2, router_b2, expert_w1, expert_b1, expert_w2, expert_b2, expert_w3, expert_b3):
        import jax, jax.numpy as jnp
        import numpy as np
        E, D, H, TOP_K = (6, 256, 256, 2)
        ROUTER_H = D // 2
        rh = jax.nn.relu(features @ router_w1 + router_b1)
        expert_logits = jax.nn.softmax(rh @ router_w2 + router_b2, axis=-1)
        top_w, top_i = jax.lax.top_k(expert_logits, TOP_K)
        routing_weights = jax.nn.softmax(top_w, axis=-1)
        h1 = jax.nn.relu(jnp.einsum('bsd,edh->bseh', features, expert_w1) + expert_b1)
        h2 = jax.nn.relu(jnp.einsum('bseh,ehf->bsef', h1, expert_w2) + expert_b2)
        expert_out = jnp.einsum('bsef,efo->bseo', h2, expert_w3) + expert_b3
        sel = jnp.take_along_axis(expert_out, top_i[:, :, :, None], axis=2)
        combined = jnp.sum(sel * routing_weights[..., None], axis=2)
        return combined

    def _L1_gnn_ref(node_features, edge_features, targets, src, dst, W_dense, b_dense, W_edge, b_edge, W_out, b_out):
        import jax, jax.numpy as jnp
        import numpy as np
        N_NODES, N_EDGES, D = (2500, 40000, 256)

        def mish(x):
            return x * jnp.tanh(jax.nn.softplus(x))
        x = mish(node_features @ W_dense.T + b_dense)
        y = mish(edge_features @ W_edge.T + b_edge)
        msg = jax.nn.relu(x[src] + y)
        agg = jax.ops.segment_sum(msg, dst, num_segments=node_features.shape[0])
        rst = x + agg
        return mish(rst @ W_out.T + b_out)

    def _L1_ffn_ref(x, gamma, beta, Wr, br, W1, b1, W2, b2):
        import jax, jax.numpy as jnp
        import numpy as np
        E = 8
        K = 2
        D = 256
        H = 512
        DOUT = 256
        EPS = 1e-05
        mu = jnp.mean(x, axis=-1, keepdims=True)
        var = jnp.mean(jnp.square(x - mu), axis=-1, keepdims=True)
        xn = (x - mu) * jax.lax.rsqrt(var + EPS) * gamma + beta
        logits = jnp.einsum('bsd,de->bse', xn, Wr) + br
        top_vals, top_idx = jax.lax.top_k(logits, K)
        w = jax.nn.softmax(top_vals, axis=-1)
        w_full = jnp.einsum('bsk,bske->bse', w, jax.nn.one_hot(top_idx, E, dtype=w.dtype))
        y = jnp.zeros(x.shape[:-1] + (DOUT,), x.dtype)
        for e in range(E):
            h = jax.nn.gelu(jnp.einsum('bsd,dh->bsh', xn, W1[e]) + b1[e], approximate=False)
            y_e = jnp.einsum('bsh,hd->bsd', h, W2[e]) + b2[e]
            y = y + y_e * w_full[..., e, None]
        return y
    x = x + _L0_gnn_ref(_layernorm(x, axis=-1), src, dst, edge_weight, L0_gnn_W1, L0_gnn_b1, L0_gnn_W2, L0_gnn_b2)
    x = x + _L0_ffn_ref(_layernorm(x, axis=-1)[None], L0_ffn_router_w1, L0_ffn_router_b1, L0_ffn_router_w2, L0_ffn_router_b2, L0_ffn_expert_w1, L0_ffn_expert_b1, L0_ffn_expert_w2, L0_ffn_expert_b2, L0_ffn_expert_w3, L0_ffn_expert_b3)[0]
    x = x + _L1_gnn_ref(_layernorm(x, axis=-1), edge_attr_256, node_vec1, src, dst, L1_gnn_W_dense, L1_gnn_b_dense, L1_gnn_W_edge, L1_gnn_b_edge, L1_gnn_W_out, L1_gnn_b_out)
    x = x + _L1_ffn_ref(_layernorm(x, axis=-1)[None], L1_ffn_gamma, L1_ffn_beta, L1_ffn_Wr, L1_ffn_br, L1_ffn_W1, L1_ffn_b1, L1_ffn_W2, L1_ffn_b2)[0]
    return x

_drawn_inputs = setup_inputs


def setup_inputs(seed=0):
    import zlib

    import numpy as np

    out = dict(_drawn_inputs(seed))
    spreads = {'L0_ffn_router_b1': (0.0, 0.8),
     'L0_ffn_router_b2': (0.0, 0.8),
     'L0_ffn_expert_b1': (0.0, 0.8),
     'L0_ffn_expert_b2': (0.0, 0.8),
     'L0_ffn_expert_b3': (0.0, 2.0),
     'L1_ffn_br': (0.0, 0.8)}
    factors = {'L0_gnn_b1': 8.0,
     'L0_gnn_b2': 8.0,
     'L0_ffn_router_w1': 6.074,
     'L0_ffn_router_w2': 6.162,
     'L0_ffn_expert_w1': 8.0,
     'L0_ffn_expert_w2': 8.0,
     'L0_ffn_expert_w3': 6.847,
     'L1_gnn_b_dense': 3.591,
     'L1_gnn_b_edge': 4.951,
     'L1_gnn_b_out': 30.902,
     'L1_ffn_gamma': 8.0,
     'L1_ffn_beta': 8.0,
     'L1_ffn_Wr': 8.0,
     'L1_ffn_W1': 8.0,
     'L1_ffn_b1': 64.0,
     'L1_ffn_W2': 8.0,
     'L1_ffn_b2': 187.185}
    for name, (base, spread) in spreads.items():
        noise = np.random.default_rng([zlib.crc32(name.encode()), seed]).standard_normal(out[name].shape)
        drawn = base * np.exp(spread * noise) if base else spread * noise
        out[name] = jnp.asarray(drawn.astype(out[name].dtype))
    for name, factor in factors.items():
        out[name] = (out[name] * factor).astype(out[name].dtype)
    return out
```

```python
import concourse.bass as bass
from concourse import mybir
from contextlib import ExitStack
import numpy as np

FP32 = mybir.dt.float32
BF16 = mybir.dt.bfloat16
I32 = mybir.dt.int32
U32 = mybir.dt.uint32
ALU = mybir.AluOpType
ACT = mybir.ActivationFunctionType
AX = mybir.AxisListType

P = 128
D = 256
KD = D // P
HID = 128
N = 6250
T = 52
NP = T * P
TG = 4
G = T // TG
GN = TG * P
E = 106250
C = 840
CG = 4
EG = C // CG
EGP = EG // 2
SLOTS = 6
IT = EG // SLOTS
MISH = SLOTS // 2
W = 64
TW = NP + W
EPS = 1e-5
E0 = 6
E1 = 8
H1 = 512
HM = H1 // P
ZMAX = 20.0
LN2 = 0.6931471805599453


def take(eng, semaphore, n=1):
    eng.wait_ge(semaphore, n)
    eng.sem_inc(semaphore, -n)


def link(eng, ins, semaphore):
    ins.then_inc(semaphore, 1)
    take(eng, semaphore)


class Signals:

    def __init__(self, nc, prefix=""):
        self.nc, self.prefix, self.made = nc, prefix, []

    def __enter__(self):
        return self

    def __call__(self, name):
        self.made.append(self.nc.alloc_semaphore(self.prefix + name))
        return self.made[-1]

    def __exit__(self, *_):
        self.nc.clear_and_free_semaphores(self.made)
        self.nc.all_engine_barrier()


class Chip:

    def __init__(self, nc, ctx, io):
        self.nc, self.io = nc, io
        sb = lambda name, shape, dt=FP32: ctx.enter_context(nc.sbuf_tensor(name, shape, dt))
        self.x = sb("x_sb", [P, T, D])
        self.feat = sb("feat", [P, KD, TW])
        self.src = sb("src_sb", [P, C], I32)
        self.dstrel = sb("dstrel", [P, C])
        self.weight = sb("weight_sb", [P, C])
        self.base = sb("base_row", [1, EG], I32)
        self.window = sb("window_row", [1, EG], I32)
        self.passes = sb("passes", [1, 1], I32)
        self.iota = sb("iota_sb", [P, W])
        self.ident = sb("ident_sb", [P, P])
        self.mv = sb("mv", [P, T, 2])
        self.rstd = sb("rstd", [P, T])
        self.route = sb("route", [P, T, 8])
        self.eps = sb("eps_sb", [P, 1])
        dram = lambda name, shape, dt=FP32: nc.dram_tensor(name, shape, dt, kind="Internal").ap()
        self.t1 = dram("support_table", (NP, HID))
        self.t2 = dram("hidden_table", (NP, HID))
        self.t3 = dram("node_table", (NP, D))
        self.mish_d = dram("edge_mish_table", (EG, P, CG, D))
        self.base_d = dram("base_dram", (EG,))
        self.span_d = dram("span_dram", (EG,))


def stage_setup(nc, c):
    io = c.io
    with ExitStack() as ctx:
        sb = lambda name, shape, dt=FP32: ctx.enter_context(nc.sbuf_tensor(name, shape, dt))
        sem = ctx.enter_context(Signals(nc))
        dst_g = sb("dst_g", [EGP, 2, CG * P], I32)
        dst_gf = sb("dst_gf", [EGP, 2, CG * P])
        low = sb("low", [EGP, 2])
        high = sb("high", [EGP, 2])
        span = sb("span", [EGP, 2])
        dst_t = sb("dst_t", [P, C], I32)
        dst_tf = sb("dst_tf", [P, C])
        base_bc = sb("base_bc", [P, EG])
        base_1 = sb("base_1", [1, EG])
        span_1 = sb("span_1", [1, EG])
        widest = sb("widest", [1, 1])
        widest_i = sb("widest_i", [1, 1], I32)
        shifted = sb("shifted", [1, 1], I32)
        x_in, dst_in, edges_in = sem("x_in"), sem("dst_in"), sem("edges_in")
        own, spans_ready, spans_out, spans_in = sem("su_own"), sem("spans_ready"), sem("spans_out"), sem("spans_in")
        block = ctx.enter_context(nc.Block())

        @block.sync
        def _(sp):
            sp.dma_start(dst_g[:], io["dst_g"]).then_inc(dst_in, 16)
            sp.dma_start(dst_t[:], io["dst_t"]).then_inc(edges_in, 16)
            sp.dma_start(c.src[:], io["src_t"]).then_inc(x_in, 16)
            sp.dma_start(c.weight[:], io["weight_t"]).then_inc(x_in, 16)
            sp.dma_start(c.iota[:], io["iota"]).then_inc(x_in, 16)
            sp.dma_start(c.ident[:], io["ident"]).then_inc(x_in, 16)
            sp.dma_start(c.x[:], io["x"].rearrange("(t p) d -> p t d", p=P)).then_inc(x_in, 16)
            sp.wait_ge(spans_ready, 2)
            with nc.allow_non_contiguous_dma(reason="208 words"):
                sp.dma_start(c.base_d.rearrange("(a p) -> p a", p=EGP), low[:]).then_inc(spans_out, 16)
                sp.dma_start(c.span_d.rearrange("(a p) -> p a", p=EGP), span[:]).then_inc(spans_out, 16)
            sp.wait_ge(spans_out, 32)
            sp.dma_start(base_bc[:], c.base_d.partition_broadcast(P)).then_inc(spans_in, 16)
            sp.dma_start(base_1[:], c.base_d.rearrange("(a g) -> a g", a=1)).then_inc(spans_in, 16)
            sp.dma_start(span_1[:], c.span_d.rearrange("(a g) -> a g", a=1)).then_inc(spans_in, 16)
            sp.wait_ge(x_in, 5 * 16)

        @block.vector
        def _(dve):
            nc.vector.memset(c.eps[:], EPS)
            dve.wait_ge(dst_in, 16)
            link(dve, nc.vector.tensor_copy(dst_gf[:], dst_g[:]), own)
            nc.vector.tensor_reduce(low[:], dst_gf[:], AX.X, ALU.min).then_inc(spans_ready, 1)
            link(dve, nc.vector.tensor_reduce(high[:], dst_gf[:], AX.X, ALU.max), own)
            dve.wait_ge(spans_ready, 1)
            nc.vector.tensor_tensor(span[:], high[:], low[:], ALU.subtract).then_inc(spans_ready, 1)
            dve.wait_ge(edges_in, 16)
            link(dve, nc.vector.tensor_copy(dst_tf[:], dst_t[:]), own)
            dve.wait_ge(spans_in, 48)
            by_chunk = lambda a, j: a[:].rearrange("p (g j) -> p j g", j=CG)[:, j, :]
            for j in range(CG):
                nc.vector.tensor_tensor(by_chunk(c.dstrel, j), by_chunk(dst_tf, j), base_bc[:], ALU.subtract)
            nc.vector.tensor_copy(c.base[:], base_1[:])
            link(dve, nc.vector.tensor_reduce(widest[:], span_1[:], AX.X, ALU.max), own)
            link(dve, nc.vector.tensor_copy(widest_i[:], widest[:]), own)
            link(dve, nc.vector.tensor_single_scalar(shifted[:], widest_i[:], W.bit_length() - 1,
                                                     ALU.arith_shift_right), own)
            nc.vector.tensor_scalar_add(c.passes[:], shifted[:], 1.0)


def stage_stats(nc, c, name):
    with ExitStack() as ctx:
        stats = ctx.enter_context(nc.sbuf_tensor(f"{name}_stats", [P, TG, 6], FP32))
        mv4 = ctx.enter_context(nc.sbuf_tensor(f"{name}_mv4", [P, TG, 2], FP32))
        dev = ctx.enter_context(nc.sbuf_tensor(f"{name}_dev", [P, T], FP32))
        sem = ctx.enter_context(Signals(nc, name + "_"))
        stats_done = sem("stats_done")
        mv_done = sem("mv_done")
        all_done = sem("all_done")
        dev_done = sem("dev_done")
        block = ctx.enter_context(nc.Block())

        @block.vector
        def _(dve):
            with dve.Fori(0, G) as g:
                for s in range(TG):
                    nc.vector.bn_stats(stats[:, s, :], c.x[:, bass.ds(g * TG + s, 1), :].rearrange("p a d -> p (a d)")).then_inc(stats_done, 1)
                take(dve, stats_done, TG)
                for s in range(TG):
                    nc.vector.bn_aggr(mv4[:, s, :], stats[:, s, :]).then_inc(mv_done, 1)
                take(dve, mv_done, TG)
                link(dve, nc.vector.tensor_copy(c.mv[:, bass.ds(g * TG, TG), :], mv4[:]), mv_done)
            dve.sem_inc(all_done, 1)
            dve.wait_ge(dev_done, 1)
            link(dve, nc.vector.reciprocal(c.rstd[:], dev[:]), mv_done)
            link(dve, nc.vector.tensor_tensor(dev[:], c.rstd[:], c.rstd[:], ALU.mult), mv_done)
            link(dve, nc.vector.scalar_tensor_tensor(dev[:], c.mv[:, :, 1], EPS, dev[:], ALU.add, ALU.mult), mv_done)
            link(dve, nc.vector.tensor_scalar(dev[:], dev[:], -0.5, 1.5, ALU.mult, ALU.add), mv_done)
            nc.vector.tensor_tensor(c.rstd[:], c.rstd[:], dev[:], ALU.mult)

        @block.scalar
        def _(act):
            act.wait_ge(all_done, 1)
            act.activation(dev[:], c.mv[:, :, 1], ACT.Sqrt, bias=c.eps[:]).then_inc(dev_done, 1)


def tokens(a, g, h):
    return a[..., bass.ds(g * GN + h * (GN // 2), GN // 2)]


def normalise(dve, nc, c, xn, g, h, xn_ready):
    for s in range(2):
        tile = bass.ds(g * TG + 2 * h + s, 1)
        last = nc.vector.tensor_scalar(xn[:, s, :], c.x[:, tile, :].rearrange("p a d -> p (a d)"),
                                       c.mv[:, tile, 0], c.rstd[:, tile], ALU.subtract, ALU.mult)
    last.then_inc(xn_ready, 1)


def transpose_half(nc, c, out, xn):
    for k in range(KD):
        for s in range(2):
            last = nc.tensor.transpose(out[:, k, s * P:(s + 1) * P], xn[:, s, k * P:(k + 1) * P], c.ident[:])
    return last


def store_rows(sp, table, g, h, rows, rows_ready, rows_out, rows_free):
    take(sp, rows_ready[h])
    sp.dma_start(table[bass.ds(g * GN + h * (GN // 2), GN // 2), :].rearrange("(s p) d -> p s d", p=P),
                 rows[h][:]).then_inc(rows_out[h], 16)


def stage_support(nc, c):
    io = c.io
    with ExitStack() as ctx:
        sb = lambda name, shape, dt=FP32: ctx.enter_context(nc.sbuf_tensor(name, shape, dt))
        pb = lambda name, shape: ctx.enter_context(nc.psum_tensor(name, shape, FP32))
        sem = ctx.enter_context(Signals(nc))
        sem2 = lambda name: [sem(f"{name}{h}") for h in range(2)]
        w1 = sb("gw1", [P, KD, HID])
        xn = [sb(f"s_xn{h}", [P, 2, D]) for h in range(2)]
        xt = [sb(f"s_xt{h}", [P, KD, 2 * P]) for h in range(2)]
        rows = [sb(f"s_rows{h}", [P, 2, HID]) for h in range(2)]
        ps_t = [pb(f"s_pt{h}", [P, KD, 2 * P]) for h in range(2)]
        ps_y = [pb(f"s_py{h}", [P, 2, HID]) for h in range(2)]
        w_in = sem("s_w_in")
        xn_ready, pt_ready, xt_ready = sem2("s_xn_ready"), sem2("s_pt_ready"), sem2("s_xt_ready")
        py_ready, rows_ready = sem2("s_py_ready"), sem2("s_rows_ready")
        rows_out, rows_free = sem2("s_rows_out"), sem2("s_rows_free")
        block = ctx.enter_context(nc.Block())

        @block.sync
        def _(sp):
            sp.dma_start(w1[:], io["g_w1"]).then_inc(w_in, 16)
            with sp.Fori(0, G) as g:
                for h in range(2):
                    store_rows(sp, c.t1, g, h, rows, rows_ready, rows_out, rows_free)
                for h in range(2):
                    take(sp, rows_out[h], 16)
                    sp.sem_inc(rows_free[h], 1)

        @block.vector
        def _(dve):
            dve.sem_inc(rows_free[0], 1)
            dve.sem_inc(rows_free[1], 1)
            with dve.Fori(0, G) as g:
                for h in range(2):
                    normalise(dve, nc, c, xn[h], g, h, xn_ready[h])
                for h in range(2):
                    take(dve, py_ready[h])
                    take(dve, rows_free[h])
                    nc.vector.tensor_copy(rows[h][:], ps_y[h][:]).then_inc(rows_ready[h], 1)

        @block.scalar
        def _(act):
            with act.Fori(0, G) as g:
                for h in range(2):
                    take(act, pt_ready[h])
                    act.copy(xt[h][:], ps_t[h][:]).then_inc(xt_ready[h], 1)

        @block.tensor
        def _(pe):
            pe.wait_ge(w_in, 16)
            with pe.Fori(0, G) as g:
                for h in range(2):
                    take(pe, xn_ready[h])
                    transpose_half(nc, c, ps_t[h], xn[h]).then_inc(pt_ready[h], 1)
                for h in range(2):
                    take(pe, xt_ready[h])
                    for s in range(2):
                        for k in range(KD):
                            last = pe.matmul(ps_y[h][:, s, :], xt[h][:, k, s * P:(s + 1) * P], w1[:, k, :],
                                             start=k == 0, stop=k == KD - 1)
                    last.then_inc(py_ready[h], 1)


def stage_conv(nc, c, part, table):
    io, name = c.io, f"conv{part}"
    with ExitStack() as ctx:
        sb = lambda n, shape, dt=FP32: ctx.enter_context(nc.sbuf_tensor(f"{name}_{n}", shape, dt))
        pb = lambda n, shape: ctx.enter_context(nc.psum_tensor(f"{name}_{n}", shape, FP32))
        sem = ctx.enter_context(Signals(nc, name + "_"))
        idx = sb("idx", [P, 2, SLOTS // 2 * CG], I32)
        rel = sb("rel", [P, C])
        window = sb("window", [1, EG], I32)
        gath = [sb(f"gath{s}", [P, CG, HID]) for s in range(SLOTS)]
        hot = [sb(f"hot{s}", [P, CG, W]) for s in range(SLOTS)]
        we = sb("we", [P, KD, D])
        bias, parts, ones = bias_buffers(sb)
        ln2 = sb("ln2", [P, 1])
        edge = [sb(f"edge{r}", [P, KD, CG * P]) for r in range(MISH)]
        q = [sb(f"q{r}", [P, CG, D]) for r in range(MISH)]
        neg = [sb(f"neg{r}", [P, CG, D]) for r in range(MISH)]
        ps = [pb(f"ps{n}", [P, W]) for n in range(2)]
        ps_z = [pb(f"pz{r}", [P, CG, D]) for r in range(MISH)]
        sums = c.feat[:, 0, :]
        gathered = [nc.alloc_semaphore(f"{name}_gathered{s}") for s in range(SLOTS)]
        slot_free = [sem(f"slot_free{s}") for s in range(SLOTS)]
        hot_ready = [sem(f"hot_ready{s}") for s in range(SLOTS)]
        ps_ready = [sem(f"ps_ready{n}") for n in range(2)]
        ps_free = [sem(f"ps_free{n}") for n in range(2)]
        idx_ready, own, act_own, neg_own = sem("idx_ready"), sem("own"), sem("act_own"), sem("neg_own")
        w_in, parts_ready = sem("w_in"), sem("parts_ready")
        per_r = lambda n: [sem(f"{n}{r}") for r in range(MISH)]
        edge_in, edge_free, z_done, z_free = per_r("edge_in"), per_r("edge_free"), per_r("z_done"), per_r("z_free")
        z_ready, q_ready, neg_ready, neg_out = per_r("z_ready"), per_r("q_ready"), per_r("neg_ready"), per_r("neg_out")
        block = ctx.enter_context(nc.Block())

        def load_passes(eng):
            return eng.value_load(c.passes[0:1, 0:1], min_val=1, max_val=TW // W)

        @block.sync
        def _(sp):
            group = lambda i, r: bass.ds(i * MISH + (part * IT * MISH + r), 1)

            def load(i, r):
                take(sp, edge_free[r])
                sp.dma_start(edge[r][:], io["edge_t"][group(i, r)].rearrange("a p k e -> p (a k) e")).then_inc(edge_in[r], 16)

            def store(i, r):
                take(sp, neg_ready[r])
                sp.dma_start(c.mish_d[group(i, r)].rearrange("a p j d -> p (a j) d"), neg[r][:]).then_inc(neg_out[r], 16)

            sp.dma_start(we[:], io["l_we"]).then_inc(w_in, 16)
            sp.dma_start(bias[0][:], io["l_be"]).then_inc(w_in, 16)
            for r in range(MISH):
                sp.sem_inc(edge_free[r], 1)
            with sp.Fori(0, load_passes(sp)) as k:
                for r in range(MISH):
                    load(0, r)
                with sp.Fori(0, IT - 1) as i:
                    for r in range(MISH):
                        load(i + 1, r)
                        store(i, r)
                for r in range(MISH):
                    store(IT - 1, r)
            for r in range(MISH):
                sp.wait_ge(neg_out[r], 16)

        @block.gpsimd
        def _(pool):
            for s in range(SLOTS):
                pool.sem_inc(slot_free[s], 1)
            with pool.Fori(0, load_passes(pool)) as k:
                with pool.Fori(0, IT) as i:
                    for half in range(2):
                        for s in range(half * 3, half * 3 + 3):
                            take(pool, slot_free[s])
                        nc.gpsimd.tensor_copy(idx[:, half, :], c.src[:, bass.ds(i * (SLOTS * CG) + half * (SLOTS // 2 * CG), SLOTS // 2 * CG)]).then_inc(idx_ready, 1)
                        take(pool, idx_ready)
                        for s in range(half * 3, half * 3 + 3):
                            for j in range(CG):
                                col = (s - half * 3) * CG + j
                                pool.indirect_dma_start(
                                    gath[s][:, j, :], None, table[:, :],
                                    bass.IndirectOffsetOnAxis(ap=idx[:, half, col:col + 1], axis=0),
                                ).then_inc(gathered[s], 16)

        @block.vector
        def _(dve):
            def mish_begin(r):
                take(dve, z_done[r])
                dve.sem_inc(edge_free[r], 1)
                nc.vector.tensor_scalar(q[r][:], ps_z[r][:], ZMAX, None, ALU.min).then_inc(z_ready[r], 1)

            def mish_end(r):
                take(dve, q_ready[r])
                take(dve, neg_out[r], 16)
                link(dve, nc.vector.scalar_tensor_tensor(neg[r][:], q[r][:], -1.0, ps_z[r][:], ALU.add, ALU.mult), neg_own)
                dve.sem_inc(z_free[r], 1)
                dve.sem_inc(neg_ready[r], 1)

            def add(i, s):
                at = dve.value_load(window[0:1, bass.ds(i * SLOTS + s, 1)], min_val=0, max_val=NP)
                take(dve, ps_ready[s % 2])
                here = sums[:, bass.ds(at, W)]
                link(dve, nc.vector.tensor_tensor(here, here, ps[s % 2][:], ALU.add), own)
                dve.sem_inc(ps_free[s % 2], 1)
                dve.sem_inc(slot_free[s], 1)

            def step(i, first):
                for s in range(SLOTS):
                    for j in range(CG):
                        col = bass.ds(i * (SLOTS * CG) + s * CG + j, 1)
                        last = nc.vector.tensor_scalar(hot[s][:, j, :], c.iota[:], rel[:, col], c.weight[:, col],
                                                       ALU.is_equal, ALU.mult)
                    last.then_inc(hot_ready[s], 1)
                for r in range(MISH):
                    add(i, 2 * r)
                    add(i, 2 * r + 1)
                    mish_begin(r)
                    if r or not first:
                        mish_end((r - 1) % MISH)

            for n in range(2):
                dve.sem_inc(ps_free[n], 1)
            for r in range(MISH):
                dve.sem_inc(z_free[r], 1)
                dve.sem_inc(neg_out[r], 16)
            nc.vector.memset(ln2[:], LN2)
            nc.vector.memset(ones[:], 1.0)
            nc.vector.memset(sums, 0.0)
            nc.vector.tensor_copy(rel[:], c.dstrel[:])
            link(dve, nc.vector.tensor_copy(window[:], c.base[:]), own)
            dve.wait_ge(w_in, 32)
            split_bias(dve, nc, c, bias, parts, own)
            dve.sem_inc(parts_ready, 2)
            with dve.Fori(0, load_passes(dve)) as k:
                step(0, True)
                with dve.Fori(1, IT) as i:
                    step(i, False)
                mish_end(MISH - 1)
                nc.vector.tensor_scalar(rel[:], rel[:], -float(W), None, ALU.add)
                link(dve, nc.vector.tensor_scalar(window[:], window[:], float(W), float(NP), ALU.add, ALU.min), own)

        @block.scalar
        def _(act):
            act.wait_ge(parts_ready, 1)
            log_exp_table(act)
            with act.Fori(0, load_passes(act)) as k:
                with act.Fori(0, IT) as i:
                    for r in range(MISH):
                        take(act, z_ready[r])
                        mish_factor(act, q[r][:], ln2, act_own, q_ready[r])

        @block.tensor
        def _(pe):
            def segment(k, i, s):
                take(pe, hot_ready[s])
                take(pe, ps_free[s % 2])
                pe.wait_ge(gathered[s], k * (IT * CG * 16) + i * (CG * 16) + CG * 16)
                for j in range(CG):
                    last = pe.matmul(ps[s % 2][:], gath[s][:, j, :], hot[s][:, j, :], start=j == 0, stop=j == CG - 1)
                last.then_inc(ps_ready[s % 2], 1)

            def product(r):
                take(pe, edge_in[r], 16)
                take(pe, z_free[r])
                for j in range(CG):
                    for m in range(KD):
                        pe.matmul(ps_z[r][:, j, :], edge[r][:, m, j * P:(j + 1) * P], we[:, m, :], start=m == 0, stop=False)
                    last = pe.matmul(ps_z[r][:, j, :], ones[:], parts[:], start=False, stop=True)
                last.then_inc(z_done[r], 1)

            pe.wait_ge(parts_ready, 1)
            with pe.Fori(0, load_passes(pe)) as k:
                with pe.Fori(0, IT) as i:
                    for r in range(MISH):
                        segment(k, i, 2 * r)
                        segment(k, i, 2 * r + 1)
                        product(r)


def stage_hidden(nc, c):
    io = c.io
    with ExitStack() as ctx:
        sb = lambda name, shape, dt=FP32: ctx.enter_context(nc.sbuf_tensor(name, shape, dt))
        sem = ctx.enter_context(Signals(nc))
        sem2 = lambda name: [sem(f"{name}{h}") for h in range(2)]
        b1 = sb("gb1", [P, 1])
        hid = [sb(f"h_hid{h}", [P, 2 * P]) for h in range(2)]
        rows = [sb(f"h_rows{h}", [P, 2, HID]) for h in range(2)]
        ps = [ctx.enter_context(nc.psum_tensor(f"h_ps{h}", [P, 2, HID], FP32)) for h in range(2)]
        b_in, own = sem("h_b_in"), sem("h_own")
        hid_ready, ps_ready, ps_free = sem2("h_hid_ready"), sem2("h_ps_ready"), sem2("h_ps_free")
        rows_ready, rows_out, rows_free = sem2("h_rows_ready"), sem2("h_rows_out"), sem2("h_rows_free")
        block = ctx.enter_context(nc.Block())

        @block.sync
        def _(sp):
            sp.dma_start(b1[:], io["g_b1"]).then_inc(b_in, 16)
            with sp.Fori(0, G) as g:
                for h in range(2):
                    store_rows(sp, c.t2, g, h, rows, rows_ready, rows_out, rows_free)
                for h in range(2):
                    take(sp, rows_out[h], 16)
                    sp.sem_inc(rows_free[h], 1)

        @block.scalar
        def _(act):
            act.wait_ge(b_in, 16)
            act.sem_inc(ps_free[0], 1)
            act.sem_inc(ps_free[1], 1)
            with act.Fori(0, G) as g:
                for h in range(2):
                    take(act, ps_free[h])
                    act.activation(hid[h][:], tokens(c.feat[:, 0, :], g, h), ACT.Relu, bias=b1[:]).then_inc(hid_ready[h], 1)

        @block.tensor
        def _(pe):
            with pe.Fori(0, G) as g:
                for h in range(2):
                    take(pe, hid_ready[h])
                    for s in range(2):
                        last = pe.transpose(ps[h][:, s, :], hid[h][:, s * P:(s + 1) * P], c.ident[:])
                    last.then_inc(ps_ready[h], 1)

        @block.vector
        def _(dve):
            dve.sem_inc(rows_free[0], 1)
            dve.sem_inc(rows_free[1], 1)
            with dve.Fori(0, G) as g:
                for h in range(2):
                    take(dve, ps_ready[h])
                    take(dve, rows_free[h])
                    link(dve, nc.vector.tensor_copy(rows[h][:], ps[h][:]), own)
                    dve.sem_inc(rows_ready[h], 1)
                    dve.sem_inc(ps_free[h], 1)


def stage_convolved(nc, c):
    io = c.io
    with ExitStack() as ctx:
        sb = lambda name, shape, dt=FP32: ctx.enter_context(nc.sbuf_tensor(name, shape, dt))
        sem = ctx.enter_context(Signals(nc))
        sem2 = lambda name: [sem(f"{name}{h}") for h in range(2)]
        w2, b2 = sb("gw2", [P, D]), sb("gb2", [P, D])
        sums = [sb(f"c_sums{h}", [P, 2 * P]) for h in range(2)]
        ps = [ctx.enter_context(nc.psum_tensor(f"c_ps{h}", [P, 2, D], FP32)) for h in range(2)]
        w_in = sem("c_w_in")
        own = sem("c_own")
        sums_ready, ps_ready, ps_free = sem2("c_sums_ready"), sem2("c_ps_ready"), sem2("c_ps_free")
        block = ctx.enter_context(nc.Block())

        @block.sync
        def _(sp):
            sp.dma_start(w2[:], io["g_w2"]).then_inc(w_in, 16)
            sp.dma_start(b2[:], io["g_b2"]).then_inc(w_in, 16)

        @block.scalar
        def _(act):
            act.sem_inc(ps_free[0], 1)
            act.sem_inc(ps_free[1], 1)
            with act.Fori(0, G) as g:
                for h in range(2):
                    take(act, ps_free[h])
                    act.copy(sums[h][:], tokens(c.feat[:, 0, :], g, h)).then_inc(sums_ready[h], 1)

        @block.tensor
        def _(pe):
            pe.wait_ge(w_in, 32)
            with pe.Fori(0, G) as g:
                for h in range(2):
                    take(pe, sums_ready[h])
                    for s in range(2):
                        last = pe.matmul(ps[h][:, s, :], sums[h][:, s * P:(s + 1) * P], w2[:], start=True, stop=True)
                    last.then_inc(ps_ready[h], 1)

        @block.vector
        def _(dve):
            dve.wait_ge(w_in, 32)
            with dve.Fori(0, G) as g:
                for h in range(2):
                    x = c.x[:, bass.ds(g * TG + 2 * h, 2), :]
                    link(dve, nc.vector.tensor_tensor(x, x, b2[:].unsqueeze(1).to_broadcast([P, 2, D]), ALU.add), own)
                    take(dve, ps_ready[h])
                    link(dve, nc.vector.tensor_tensor(x, x, ps[h][:], ALU.add), own)
                    dve.sem_inc(ps_free[h], 1)


def stage_route(nc, c, mix):
    io, name = c.io, f"r{mix}"
    experts = (E0, E1)[mix]
    with ExitStack() as ctx:
        sb = lambda n, shape, dt=FP32: ctx.enter_context(nc.sbuf_tensor(f"{name}_{n}", shape, dt))
        pb = lambda n, shape: ctx.enter_context(nc.psum_tensor(f"{name}_{n}", shape, FP32))
        sem = ctx.enter_context(Signals(nc, name + "_"))
        sem2 = lambda n: [sem(f"{n}{h}") for h in range(2)]
        if mix == 0:
            w1, b1 = sb("w1", [P, KD, P]), sb("b1", [P, 1])
            hid = [sb(f"hid{h}", [P, 2 * P]) for h in range(2)]
            w2 = sb("w2", [P, E0])
        else:
            gamma, beta, w2 = sb("gamma", [P, KD]), sb("beta", [P, KD]), sb("w2", [P, KD, E1])
            xt = [sb(f"xt{h}", [P, KD, 2 * P]) for h in range(2)]
        b2 = sb("b2", [P, experts])
        iota8 = sb("iota8", [P, 8])
        xn = [sb(f"xn{h}", [P, 2, D]) for h in range(2)]
        logit = sb("logit", [P, T, 8])
        top = sb("top", [P, T])
        total = sb("total", [P, T])
        best = sb("best", [P, T, 8])
        best_at = sb("best_at", [P, T, 8], U32)
        at = sb("at", [P, T, 2])
        second = sb("second", [P, T])
        w_0, w_1 = sb("w_0", [P, T]), sb("w_1", [P, T])
        mask = sb("mask", [P, T, 8])
        ps_t = [pb(f"pt{h}", [P, KD, 2 * P]) for h in range(2)]
        ps_h = [pb(f"ph{h}", [P, 2 * P]) for h in range(2)]
        ps_l = [pb(f"pl{h}", [P, 2, 8]) for h in range(2)]
        w_in, own, act_own = sem("w_in"), sem("own"), sem("act_own")
        xn_ready, pt_ready, ft_ready = sem2("xn_ready"), sem2("pt_ready"), sem2("ft_ready")
        ph_ready, hid_ready, pl_ready = sem2("ph_ready"), sem2("hid_ready"), sem2("pl_ready")
        shifted_ready, exp_ready, gap_ready, gap_exp = sem("shifted_ready"), sem("exp_ready"), sem("gap_ready"), sem("gap_exp")
        xt_ready, xt_free = sem2("xt_ready"), sem2("xt_free")
        block = ctx.enter_context(nc.Block())
        loads = ([(w1, "r0_w1"), (b1, "r0_b1"), (w2, "r0_w2"), (b2, "r0_b2")] if mix == 0 else
                 [(gamma, "r1_gamma"), (beta, "r1_beta"), (w2, "r1_w2"), (b2, "r1_b2")]) + [(iota8, "iota8")]

        @block.sync
        def _(sp):
            for tile, key in loads:
                sp.dma_start(tile[:], io[key]).then_inc(w_in, 16)

        def over(ap):
            return ap.unsqueeze(2).to_broadcast([P, T, 8])

        @block.vector
        def _(dve):
            nc.vector.memset(logit[:], -1e30)
            dve.wait_ge(w_in, 16 * len(loads))
            with dve.Fori(0, G) as g:
                for h in range(2):
                    normalise(dve, nc, c, xn[h], g, h, xn_ready[h])
                for h in range(2):
                    take(dve, pl_ready[h])
                    link(dve, nc.vector.tensor_tensor(logit[:, bass.ds(g * TG + 2 * h, 2), 0:experts], ps_l[h][:, :, 0:experts],
                                                      b2[:].unsqueeze(1).to_broadcast([P, 2, experts]), ALU.add), own)
            if mix == 0:
                some = logit[:, :, 0:experts]
                wide = lambda ap: ap.unsqueeze(2).to_broadcast([P, T, experts])
                link(dve, nc.vector.tensor_reduce(top[:], some, AX.X, ALU.max), own)
                nc.vector.tensor_tensor(some, some, wide(top[:]), ALU.subtract).then_inc(shifted_ready, 1)
                take(dve, exp_ready)
                link(dve, nc.vector.tensor_reduce(total[:], some, AX.X, ALU.add), own)
                link(dve, nc.vector.reciprocal(total[:], total[:]), own)
                link(dve, nc.vector.tensor_tensor(some, some, wide(total[:]), ALU.mult), own)
            for t in range(T):
                last = nc.vector.max(best[:, t, :], logit[:, t, :])
            link(dve, last, own)
            for t in range(T):
                last = nc.vector.max_index(best_at[:, t, :], best[:, t, :], logit[:, t, :])
            nc.vector.tensor_tensor(second[:], best[:, :, 1], best[:, :, 0], ALU.subtract).then_inc(gap_ready, 1)
            last.then_inc(own, 1)
            take(dve, own)
            link(dve, nc.vector.tensor_copy(at[:], best_at[:, :, 0:2]), own)
            take(dve, gap_exp)
            link(dve, nc.vector.tensor_scalar_add(total[:], second[:], 1.0), own)
            link(dve, nc.vector.reciprocal(w_0[:], total[:]), own)
            link(dve, nc.vector.tensor_tensor(w_1[:], second[:], w_0[:], ALU.mult), own)
            every = iota8[:].unsqueeze(1).to_broadcast([P, T, 8])
            for n, w_n in enumerate((w_0, w_1)):
                link(dve, nc.vector.tensor_tensor(mask[:], every, over(at[:, :, n]), ALU.is_equal), own)
                out = (c.route, mask)[n]
                link(dve, nc.vector.tensor_tensor(out[:], mask[:], over(w_n[:]), ALU.mult), own)
            nc.vector.tensor_tensor(c.route[:], c.route[:], mask[:], ALU.add)

        @block.scalar
        def _(act):
            act.wait_ge(w_in, 16 * len(loads))
            if mix == 1:
                act.sem_inc(xt_free[0], 1)
                act.sem_inc(xt_free[1], 1)
            with act.Fori(0, G) as g:
                for h in range(2):
                    take(act, pt_ready[h])
                    if mix == 1:
                        take(act, xt_free[h])
                    if mix == 0:
                        act.copy(tokens(c.feat[:, :, :], g, h), ps_t[h][:]).then_inc(ft_ready[h], 1)
                    else:
                        for k in range(KD):
                            last = act.activation(xt[h][:, k, :], ps_t[h][:, k, :], ACT.Identity,
                                                  scale=gamma[:, k:k + 1], bias=beta[:, k:k + 1])
                        link(act, last, act_own)
                        act.sem_inc(ft_ready[h], 1)
                        act.sem_inc(xt_ready[h], 1)
                if mix == 0:
                    for h in range(2):
                        take(act, ph_ready[h])
                        act.activation(hid[h][:], ps_h[h][:], ACT.Relu, bias=b1[:]).then_inc(hid_ready[h], 1)
            if mix == 0:
                take(act, shifted_ready)
                act.activation(logit[:, :, 0:experts], logit[:, :, 0:experts], ACT.Exp).then_inc(exp_ready, 1)
            take(act, gap_ready)
            act.activation(second[:], second[:], ACT.Exp).then_inc(gap_exp, 1)

        @block.tensor
        def _(pe):
            pe.wait_ge(w_in, 16 * len(loads))
            with pe.Fori(0, G) as g:
                for h in range(2):
                    take(pe, xn_ready[h])
                    transpose_half(nc, c, ps_t[h], xn[h]).then_inc(pt_ready[h], 1)
                if mix == 0:
                    for h in range(2):
                        take(pe, ft_ready[h])
                        for k in range(KD):
                            last = pe.matmul(ps_h[h][:], w1[:, k, :], tokens(c.feat[:, k, :], g, h),
                                             start=k == 0, stop=k == KD - 1)
                        last.then_inc(ph_ready[h], 1)
                    for h in range(2):
                        take(pe, hid_ready[h])
                        for s in range(2):
                            last = pe.matmul(ps_l[h][:, s, 0:E0], hid[h][:, s * P:(s + 1) * P], w2[:], start=True, stop=True)
                        last.then_inc(pl_ready[h], 1)
                else:
                    for h in range(2):
                        take(pe, ft_ready[h])
                        for s in range(2):
                            for k in range(KD):
                                last = pe.matmul(ps_l[h][:, s, 0:E1], xt[h][:, k, s * P:(s + 1) * P], w2[:, k, :],
                                                 start=k == 0, stop=k == KD - 1)
                        last.then_inc(pl_ready[h], 1)

        if mix == 1:
            @block.gpsimd
            def _(pool):
                with pool.Fori(0, G) as g:
                    for h in range(2):
                        take(pool, xt_ready[h])
                        nc.gpsimd.tensor_copy(tokens(c.feat[:, :, :], g, h), xt[h][:]).then_inc(xt_free[h], 1)


def stage_last_bias(nc, c, mix):
    io, name = c.io, f"lb{mix}"
    experts = (E0, E1)[mix]
    with ExitStack() as ctx:
        sb = lambda n, shape, dt=FP32: ctx.enter_context(nc.sbuf_tensor(f"{name}_{n}", shape, dt))
        sem = ctx.enter_context(Signals(nc, name + "_"))
        sem2 = lambda n: [sem(f"{n}{h}") for h in range(2)]
        bias = sb("bias", [experts, D])
        route = [sb(f"route{h}", [P, 2, 8]) for h in range(2)]
        rt = [sb(f"rt{h}", [8, 2 * P]) for h in range(2)]
        ps_r = [ctx.enter_context(nc.psum_tensor(f"{name}_pr{h}", [8, 2 * P], FP32)) for h in range(2)]
        ps_y = [ctx.enter_context(nc.psum_tensor(f"{name}_py{h}", [P, 2, D], FP32)) for h in range(2)]
        b_in, own = sem("b_in"), sem("own")
        route_ready, pr_ready, rt_ready, py_ready = sem2("route_ready"), sem2("pr_ready"), sem2("rt_ready"), sem2("py_ready")
        block = ctx.enter_context(nc.Block())

        @block.sync
        def _(sp):
            sp.dma_start(bias[:], io[f"m{mix}_blast"]).then_inc(b_in, 16)

        @block.vector
        def _(dve):
            with dve.Fori(0, G) as g:
                for h in range(2):
                    nc.vector.tensor_copy(route[h][:], c.route[:, bass.ds(g * TG + 2 * h, 2), :]).then_inc(route_ready[h], 1)
                for h in range(2):
                    x = c.x[:, bass.ds(g * TG + 2 * h, 2), :]
                    take(dve, py_ready[h])
                    nc.vector.tensor_tensor(x, x, ps_y[h][:], ALU.add)

        @block.scalar
        def _(act):
            with act.Fori(0, G) as g:
                for h in range(2):
                    take(act, pr_ready[h])
                    act.copy(rt[h][:], ps_r[h][:]).then_inc(rt_ready[h], 1)

        @block.tensor
        def _(pe):
            pe.wait_ge(b_in, 16)
            with pe.Fori(0, G) as g:
                for h in range(2):
                    take(pe, route_ready[h])
                    for s in range(2):
                        last = pe.transpose(ps_r[h][:, s * P:(s + 1) * P], route[h][:, s, :], c.ident[:])
                    last.then_inc(pr_ready[h], 1)
                for h in range(2):
                    take(pe, rt_ready[h])
                    for s in range(2):
                        last = pe.matmul(ps_y[h][:, s, :], rt[h][0:experts, s * P:(s + 1) * P], bias[:], start=True, stop=True)
                    last.then_inc(py_ready[h], 1)


def stage_experts0(nc, c):
    io = c.io
    with ExitStack() as ctx:
        sb = lambda n, shape, dt=FP32: ctx.enter_context(nc.sbuf_tensor(f"e0_{n}", shape, dt))
        sem = ctx.enter_context(Signals(nc, "e0_"))
        w = [[sb(f"w{layer}_{e}", [P, KD, D]) for e in range(E0)] for layer in range(3)]
        b = [sb(f"b{layer}", [P, E0, KD]) for layer in range(2)]
        h1 = [sb(f"h1_{n}", [P, KD, GN]) for n in range(2)]
        h2 = [sb(f"h2_{n}", [P, KD, GN]) for n in range(2)]
        ps_1 = [ctx.enter_context(nc.psum_tensor(f"e0_p1_{m}", [P, GN], FP32)) for m in range(KD)]
        ps_2 = [ctx.enter_context(nc.psum_tensor(f"e0_p2_{m}", [P, GN], FP32)) for m in range(KD)]
        ps_3 = ctx.enter_context(nc.psum_tensor("e0_p3", [P, TG, D], FP32))
        b_in = sem("b_in")
        w_in = [sem(f"w_in{e}") for e in range(E0)]
        p1_ready, h1_ready, p2_ready, h2_ready = sem("p1_ready"), sem("h1_ready"), sem("p2_ready"), sem("h2_ready")
        p3_ready, p3_free, own = sem("p3_ready"), sem("p3_free"), sem("own")
        block = ctx.enter_context(nc.Block())

        @block.sync
        def _(sp):
            sp.dma_start(b[0][:], io["m0_b1"]).then_inc(b_in, 16)
            sp.dma_start(b[1][:], io["m0_b2"]).then_inc(b_in, 16)
            for e in range(E0):
                for layer in range(3):
                    sp.dma_start(w[layer][e][:], io[f"m0_w{layer + 1}"][e]).then_inc(w_in[e], 16)

        @block.tensor
        def _(pe):
            def first(g, e):
                for m in range(KD):
                    for k in range(KD):
                        last = pe.matmul(ps_1[m][:], w[0][e][:, k, m * P:(m + 1) * P], c.feat[:, k, bass.ds(g * GN, GN)],
                                         start=k == 0, stop=k == KD - 1)
                    last.then_inc(p1_ready, 1)

            def second(e):
                for m in range(KD):
                    for k in range(KD):
                        last = pe.matmul(ps_2[m][:], w[1][e][:, k, m * P:(m + 1) * P], h1[e % 2][:, k, :],
                                         start=k == 0, stop=k == KD - 1)
                    last.then_inc(p2_ready, 1)

            def third(e):
                take(pe, p3_free)
                for s in range(TG):
                    for k in range(KD):
                        last = pe.matmul(ps_3[:, s, :], h2[e % 2][:, k, s * P:(s + 1) * P], w[2][e][:, k, :],
                                         start=k == 0, stop=k == KD - 1)
                last.then_inc(p3_ready, 1)

            for e in range(E0):
                pe.wait_ge(w_in[e], 48)
            with pe.Fori(0, G) as g:
                first(g, 0)
                for e in range(E0):
                    take(pe, h1_ready, KD)
                    if e + 1 < E0:
                        first(g, e + 1)
                    if e > 0:
                        take(pe, h2_ready, KD)
                    second(e)
                    if e > 0:
                        third(e - 1)
                take(pe, h2_ready, KD)
                third(E0 - 1)

        @block.scalar
        def _(act):
            act.wait_ge(b_in, 32)
            with act.Fori(0, G) as g:
                for e in range(E0):
                    for m in range(KD):
                        take(act, p1_ready)
                        act.activation(h1[e % 2][:, m, :], ps_1[m][:], ACT.Relu, bias=b[0][:, e, m:m + 1]).then_inc(h1_ready, 1)

        @block.vector
        def _(dve):
            def add(g, e):
                take(dve, p3_ready)
                for s in range(TG):
                    tile = bass.ds(g * TG + s, 1)
                    x = c.x[:, tile, :].rearrange("p a d -> p (a d)")
                    last = nc.vector.scalar_tensor_tensor(x, ps_3[:, s, :], c.route[:, tile, e], x, ALU.mult, ALU.add)
                link(dve, last, own)
                dve.sem_inc(p3_free, 1)

            dve.sem_inc(p3_free, 1)
            dve.wait_ge(b_in, 32)
            with dve.Fori(0, G) as g:
                for e in range(E0):
                    for m in range(KD):
                        take(dve, p2_ready)
                        nc.vector.tensor_scalar(h2[e % 2][:, m, :], ps_2[m][:], b[1][:, e, m:m + 1], 0.0,
                                                ALU.add, ALU.max).then_inc(h2_ready, 1)
                    if e > 0:
                        add(g, e - 1)
                add(g, E0 - 1)


def stage_experts1(nc, c):
    io = c.io
    with ExitStack() as ctx:
        sb = lambda n, shape, dt=FP32: ctx.enter_context(nc.sbuf_tensor(f"e1_{n}", shape, dt))
        sem = ctx.enter_context(Signals(nc, "e1_"))
        w1 = [sb(f"w1_{n}", [P, KD, H1]) for n in range(E1)]
        w2 = [sb(f"w2_{n}", [P, HM, D]) for n in range(E1)]
        b1 = sb("b1", [P, E1, HM])
        hid = sb("hid", [P, HM, GN])
        ps_1 = [ctx.enter_context(nc.psum_tensor(f"e1_p1_{m}", [P, GN], FP32)) for m in range(HM)]
        ps_2 = [ctx.enter_context(nc.psum_tensor(f"e1_p2_{n}", [P, TG, D], FP32)) for n in range(2)]
        b_in = sem("b_in")
        w_in = [sem(f"w_in{e}") for e in range(E1)]
        p1_ready = [sem(f"p1_ready{m}") for m in range(HM)]
        hid_ready = [sem(f"hid_ready{m}") for m in range(HM)]
        p2_ready, p2_free, own = sem("p2_ready"), sem("p2_free"), sem("own")
        block = ctx.enter_context(nc.Block())

        @block.sync
        def _(sp):
            sp.dma_start(b1[:], io["m1_b1"]).then_inc(b_in, 16)
            for e in range(E1):
                sp.dma_start(w1[e][:], io["m1_w1"][e]).then_inc(w_in[e], 16)
                sp.dma_start(w2[e][:], io["m1_w2"][e]).then_inc(w_in[e], 16)

        @block.tensor
        def _(pe):
            for e in range(E1):
                pe.wait_ge(w_in[e], 32)
            with pe.Fori(0, G) as g:
                for e in range(E1):
                    for m in range(HM):
                        for k in range(KD):
                            last = pe.matmul(ps_1[m][:], w1[e][:, k, m * P:(m + 1) * P], c.feat[:, k, bass.ds(g * GN, GN)],
                                             start=k == 0, stop=k == KD - 1)
                        last.then_inc(p1_ready[m], 1)
                    take(pe, p2_free)
                    for m in range(HM):
                        take(pe, hid_ready[m])
                    for s in range(TG):
                        for m in range(HM):
                            last = pe.matmul(ps_2[e % 2][:, s, :], hid[:, m, s * P:(s + 1) * P], w2[e][:, m, :],
                                             start=m == 0, stop=m == HM - 1)
                    last.then_inc(p2_ready, 1)

        @block.scalar
        def _(act):
            act.wait_ge(b_in, 16)
            with act.Fori(0, G) as g:
                for e in range(E1):
                    for m in range(HM):
                        take(act, p1_ready[m])
                        act.activation(hid[:, m, :], ps_1[m][:], ACT.Gelu, bias=b1[:, e, m:m + 1]).then_inc(hid_ready[m], 1)

        @block.vector
        def _(dve):
            dve.sem_inc(p2_free, 2)
            with dve.Fori(0, G) as g:
                for e in range(E1):
                    take(dve, p2_ready)
                    for s in range(TG):
                        tile = bass.ds(g * TG + s, 1)
                        x = c.x[:, tile, :].rearrange("p a d -> p (a d)")
                        last = nc.vector.scalar_tensor_tensor(x, ps_2[e % 2][:, s, :], c.route[:, tile, e], x, ALU.mult, ALU.add)
                    link(dve, last, own)
                    dve.sem_inc(p2_free, 1)


def split_bias(dve, nc, c, bias, parts, own):
    b, high, rest, total = bias
    link(dve, nc.vector.tensor_copy(high[:], b[:]), own)
    link(dve, nc.vector.tensor_scalar(total[:], high[:], c.ident[0:3, 0:1], None, ALU.mult), own)
    link(dve, nc.vector.tensor_tensor(rest[:], b[:], high[:], ALU.subtract), own)
    for row in (1, 2):
        link(dve, nc.vector.tensor_copy(high[:], rest[:]), own)
        link(dve, nc.vector.scalar_tensor_tensor(total[:], high[:], c.ident[0:3, row:row + 1], total[:], ALU.mult, ALU.add), own)
        link(dve, nc.vector.tensor_tensor(rest[:], rest[:], high[:], ALU.subtract), own)
    link(dve, nc.vector.tensor_copy(parts[:], total[:]), own)


def bias_buffers(sb):
    return ((sb("bias", [3, D]), sb("bias_high", [3, D], BF16), sb("bias_rest", [3, D]), sb("bias_total", [3, D])),
            sb("bias_parts", [3, D], BF16), sb("ones3", [3, P], BF16))


def mish_factor(act, q, ln2, own, ready):
    link(act, act.activation(q, q, ACT.Exp), own)
    link(act, act.activation(q, q, ACT.Square, bias=1.0), own)
    link(act, act.activation(q, q, ACT.Ln, bias=1.0), own)
    act.activation(q, q, ACT.Exp, scale=-1.0, bias=ln2[:]).then_inc(ready, 1)


def log_exp_table(act):
    act.preload_act_table_set("natural_log_exp_and_others")


def stage_node_mish(nc, c):
    io = c.io
    with ExitStack() as ctx:
        sb = lambda n, shape, dt=FP32: ctx.enter_context(nc.sbuf_tensor(f"n_{n}", shape, dt))
        pb = lambda n, shape: ctx.enter_context(nc.psum_tensor(f"n_{n}", shape, FP32))
        sem = ctx.enter_context(Signals(nc, "n_"))
        sem2 = lambda n: [sem(f"{n}{h}") for h in range(2)]
        wd = sb("wd", [P, KD, D])
        bias, parts, ones = bias_buffers(sb)
        ln2 = sb("ln2", [P, 1])
        xn = [sb(f"xn{h}", [P, 2, D]) for h in range(2)]
        xt = [sb(f"xt{h}", [P, KD, 2 * P]) for h in range(2)]
        q = [sb(f"q{h}", [P, 2, D]) for h in range(2)]
        rows = [sb(f"rows{h}", [P, 2, D]) for h in range(2)]
        ps_t = [pb(f"pt{h}", [P, KD, 2 * P]) for h in range(2)]
        ps_y = [pb(f"py{h}", [P, 2, D]) for h in range(2)]
        ps_u = [pb(f"pu{h}", [P, KD, 2 * P]) for h in range(2)]
        w_in, own, act_own, parts_ready = sem("w_in"), sem("own"), sem("act_own"), sem("parts_ready")
        xn_ready, pt_ready, xt_ready, py_ready = sem2("xn_ready"), sem2("pt_ready"), sem2("xt_ready"), sem2("py_ready")
        z_ready, q_ready, rows_ready, rows_pe = sem2("z_ready"), sem2("q_ready"), sem2("rows_ready"), sem2("rows_pe")
        pu_ready, pu_free, rows_out, rows_free = sem2("pu_ready"), sem2("pu_free"), sem2("rows_out"), sem2("rows_free")
        block = ctx.enter_context(nc.Block())

        @block.sync
        def _(sp):
            sp.dma_start(wd[:], io["l_wd"]).then_inc(w_in, 16)
            sp.dma_start(bias[0][:], io["l_bd"]).then_inc(w_in, 16)
            with sp.Fori(0, G) as g:
                for h in range(2):
                    store_rows(sp, c.t3, g, h, rows, rows_ready, rows_out, rows_free)
                for h in range(2):
                    take(sp, rows_out[h], 16)
                    sp.sem_inc(rows_free[h], 1)

        @block.vector
        def _(dve):
            for h in range(2):
                dve.sem_inc(rows_free[h], 1)
            nc.vector.memset(ln2[:], LN2)
            nc.vector.memset(ones[:], 1.0)
            dve.wait_ge(w_in, 32)
            split_bias(dve, nc, c, bias, parts, own)
            dve.sem_inc(parts_ready, 2)
            with dve.Fori(0, G) as g:
                for h in range(2):
                    normalise(dve, nc, c, xn[h], g, h, xn_ready[h])
                for h in range(2):
                    take(dve, py_ready[h])
                    nc.vector.tensor_scalar(q[h][:], ps_y[h][:], ZMAX, None, ALU.min).then_inc(z_ready[h], 1)
                for h in range(2):
                    take(dve, q_ready[h])
                    link(dve, nc.vector.tensor_scalar(q[h][:], q[h][:], -1.0, 1.0, ALU.mult, ALU.add), own)
                    take(dve, rows_free[h])
                    link(dve, nc.vector.tensor_tensor(rows[h][:], q[h][:], ps_y[h][:], ALU.mult), own)
                    dve.sem_inc(rows_ready[h], 1)
                    dve.sem_inc(rows_pe[h], 1)
                    take(dve, pu_ready[h])
                    nc.vector.tensor_copy(tokens(c.feat[:, :, :], g, h), ps_u[h][:])

        @block.scalar
        def _(act):
            act.wait_ge(parts_ready, 1)
            log_exp_table(act)
            with act.Fori(0, G) as g:
                for h in range(2):
                    take(act, pt_ready[h])
                    act.copy(xt[h][:], ps_t[h][:]).then_inc(xt_ready[h], 1)
                for h in range(2):
                    take(act, z_ready[h])
                    mish_factor(act, q[h][:], ln2, act_own, q_ready[h])

        @block.tensor
        def _(pe):
            pe.wait_ge(parts_ready, 1)
            with pe.Fori(0, G) as g:
                for h in range(2):
                    take(pe, xn_ready[h])
                    transpose_half(nc, c, ps_t[h], xn[h]).then_inc(pt_ready[h], 1)
                for h in range(2):
                    take(pe, xt_ready[h])
                    for s in range(2):
                        for k in range(KD):
                            pe.matmul(ps_y[h][:, s, :], xt[h][:, k, s * P:(s + 1) * P], wd[:, k, :], start=k == 0, stop=False)
                        last = pe.matmul(ps_y[h][:, s, :], ones[:], parts[:], start=False, stop=True)
                    last.then_inc(py_ready[h], 1)
                for h in range(2):
                    take(pe, rows_pe[h])
                    transpose_half(nc, c, ps_u[h], rows[h]).then_inc(pu_ready[h], 1)


def stage_edges(nc, c):
    RING = 3
    with ExitStack() as ctx:
        sb = lambda n, shape, dt=FP32: ctx.enter_context(nc.sbuf_tensor(f"x_{n}", shape, dt))
        pb = lambda n, shape: ctx.enter_context(nc.psum_tensor(f"x_{n}", shape, FP32))
        sem = ctx.enter_context(Signals(nc, "x_"))
        idx = sb("idx", [P, 2, SLOTS // 2 * CG], I32)
        rel = sb("rel", [P, C])
        window = sb("window", [1, EG], I32)
        neg = [sb(f"neg{n}", [P, CG, D]) for n in range(RING)]
        node = [sb(f"node{s}", [P, CG, D]) for s in range(SLOTS)]
        hot = [sb(f"hot{n}", [P, CG, W]) for n in range(RING)]
        ps_a = [pb(f"pa{n}", [P, KD, W]) for n in range(RING)]
        own, add_own, idx_ready = sem("own"), sem("add_own"), sem("idx_ready")
        neg_in = [sem(f"neg_in{n}") for n in range(RING)]
        neg_free = [sem(f"neg_free{n}") for n in range(RING)]
        msg_ready, sum_ready = sem("msg_ready"), sem("sum_ready")
        gathered = [nc.alloc_semaphore(f"x_gathered{s}") for s in range(SLOTS)]
        node_free = [sem(f"node_free{s}") for s in range(SLOTS)]
        block = ctx.enter_context(nc.Block())

        def load_passes(eng):
            return eng.value_load(c.passes[0:1, 0:1], min_val=1, max_val=TW // W)

        @block.sync
        def _(sp):
            for n in range(RING):
                sp.sem_inc(neg_free[n], 1)
            with sp.Fori(0, load_passes(sp)) as k:
                with sp.Fori(0, IT) as i:
                    for s in range(SLOTS):
                        take(sp, neg_free[s % RING])
                        sp.dma_start(neg[s % RING][:], c.mish_d[bass.ds(i * SLOTS + s, 1)].rearrange("a p j d -> p (a j) d")
                                     ).then_inc(neg_in[s % RING], 16)

        @block.gpsimd
        def _(pool):
            for s in range(SLOTS):
                pool.sem_inc(node_free[s], 1)
            with pool.Fori(0, load_passes(pool)) as k:
                with pool.Fori(0, IT) as i:
                    for half in range(2):
                        for s in range(half * 3, half * 3 + 3):
                            take(pool, node_free[s])
                        nc.gpsimd.tensor_copy(idx[:, half, :], c.src[:, bass.ds(i * (SLOTS * CG) + half * (SLOTS // 2 * CG), SLOTS // 2 * CG)]).then_inc(idx_ready, 1)
                        take(pool, idx_ready)
                        for s in range(half * 3, half * 3 + 3):
                            for j in range(CG):
                                col = (s - half * 3) * CG + j
                                pool.indirect_dma_start(
                                    node[s][:, j, :], None, c.t3[:, :],
                                    bass.IndirectOffsetOnAxis(ap=idx[:, half, col:col + 1], axis=0),
                                ).then_inc(gathered[s], 16)

        @block.tensor
        def _(pe):
            with pe.Fori(0, load_passes(pe)) as k:
                with pe.Fori(0, IT) as i:
                    for s in range(SLOTS):
                        n = s % RING
                        take(pe, msg_ready)
                        for m in range(KD):
                            for j in range(CG):
                                last = pe.matmul(ps_a[n][:, m, :], node[s][:, j, m * P:(m + 1) * P], hot[n][:, j, :],
                                                 start=j == 0, stop=j == CG - 1)
                        last.then_inc(sum_ready, 1)

        @block.scalar
        def _(act):
            with act.Fori(0, load_passes(act)) as k:
                with act.Fori(0, IT) as i:
                    for s in range(SLOTS):
                        take(act, own)
                        act.activation(node[s][:], node[s][:], ACT.Relu).then_inc(msg_ready, 1)

        @block.vector
        def _(dve):
            def message(k, i, s):
                for j in range(CG):
                    nc.vector.tensor_scalar(hot[s % RING][:, j, :], c.iota[:], rel[:, bass.ds(i * (SLOTS * CG) + s * CG + j, 1)],
                                            None, ALU.is_equal)
                take(dve, neg_in[s % RING], 16)
                dve.wait_ge(gathered[s], k * (IT * CG * 16) + i * (CG * 16) + CG * 16)
                nc.vector.tensor_tensor(node[s][:], node[s][:], neg[s % RING][:], ALU.subtract).then_inc(own, 1)

            def add(i, s):
                at = dve.value_load(window[0:1, bass.ds(i * SLOTS + s, 1)], min_val=0, max_val=NP)
                take(dve, sum_ready)
                dve.sem_inc(neg_free[s % RING], 1)
                dve.sem_inc(node_free[s], 1)
                here = c.feat[:, :, bass.ds(at, W)]
                link(dve, nc.vector.tensor_tensor(here, here, ps_a[s % RING][:], ALU.add), add_own)

            nc.vector.tensor_copy(rel[:], c.dstrel[:])
            link(dve, nc.vector.tensor_copy(window[:], c.base[:]), add_own)
            with dve.Fori(0, load_passes(dve)) as k:
                for s in range(SLOTS):
                    message(k, 0, s)
                    if s:
                        add(0, s - 1)
                with dve.Fori(1, IT) as i:
                    for s in range(SLOTS):
                        message(k, i, s)
                        add(i if s else i - 1, (s - 1) % SLOTS)
                add(IT - 1, SLOTS - 1)
                nc.vector.tensor_scalar(rel[:], rel[:], -float(W), None, ALU.add)
                link(dve, nc.vector.tensor_scalar(window[:], window[:], float(W), float(NP), ALU.add, ALU.min), add_own)


def stage_node_out(nc, c):
    io = c.io
    with ExitStack() as ctx:
        sb = lambda n, shape, dt=FP32: ctx.enter_context(nc.sbuf_tensor(f"o_{n}", shape, dt))
        sem = ctx.enter_context(Signals(nc, "o_"))
        sem2 = lambda n: [sem(f"{n}{h}") for h in range(2)]
        wo = sb("wo", [P, KD, D])
        bias, parts, ones = bias_buffers(sb)
        ln2 = sb("ln2", [P, 1])
        xt = [sb(f"xt{h}", [P, KD, 2 * P]) for h in range(2)]
        q = [sb(f"q{h}", [P, 2, D]) for h in range(2)]
        ps_y = [ctx.enter_context(nc.psum_tensor(f"o_py{h}", [P, 2, D], FP32)) for h in range(2)]
        w_in, own, act_own, parts_ready = sem("w_in"), sem("own"), sem("act_own"), sem("parts_ready")
        xt_ready, xt_free, py_ready, z_ready, q_ready = sem2("xt_ready"), sem2("xt_free"), sem2("py_ready"), sem2("z_ready"), sem2("q_ready")
        block = ctx.enter_context(nc.Block())

        @block.sync
        def _(sp):
            sp.dma_start(wo[:], io["l_wo"]).then_inc(w_in, 16)
            sp.dma_start(bias[0][:], io["l_bo"]).then_inc(w_in, 16)

        @block.gpsimd
        def _(pool):
            for h in range(2):
                pool.sem_inc(xt_free[h], 1)
            with pool.Fori(0, G) as g:
                for h in range(2):
                    take(pool, xt_free[h])
                    nc.gpsimd.tensor_copy(xt[h][:], tokens(c.feat[:, :, :], g, h)).then_inc(xt_ready[h], 1)

        @block.tensor
        def _(pe):
            pe.wait_ge(parts_ready, 1)
            with pe.Fori(0, G) as g:
                for h in range(2):
                    take(pe, xt_ready[h])
                    for s in range(2):
                        for k in range(KD):
                            pe.matmul(ps_y[h][:, s, :], xt[h][:, k, s * P:(s + 1) * P], wo[:, k, :], start=k == 0, stop=False)
                        last = pe.matmul(ps_y[h][:, s, :], ones[:], parts[:], start=False, stop=True)
                    last.then_inc(py_ready[h], 1)

        @block.scalar
        def _(act):
            act.wait_ge(parts_ready, 1)
            log_exp_table(act)
            with act.Fori(0, G) as g:
                for h in range(2):
                    take(act, z_ready[h])
                    mish_factor(act, q[h][:], ln2, act_own, q_ready[h])

        @block.vector
        def _(dve):
            nc.vector.memset(ln2[:], LN2)
            nc.vector.memset(ones[:], 1.0)
            dve.wait_ge(w_in, 32)
            split_bias(dve, nc, c, bias, parts, own)
            dve.sem_inc(parts_ready, 2)
            with dve.Fori(0, G) as g:
                for h in range(2):
                    take(dve, py_ready[h])
                    nc.vector.tensor_scalar(q[h][:], ps_y[h][:], ZMAX, None, ALU.min).then_inc(z_ready[h], 1)
                for h in range(2):
                    x = c.x[:, bass.ds(g * TG + 2 * h, 2), :]
                    take(dve, q_ready[h])
                    link(dve, nc.vector.scalar_tensor_tensor(q[h][:], q[h][:], -1.0, ps_y[h][:], ALU.add, ALU.mult), own)
                    dve.sem_inc(xt_free[h], 1)
                    link(dve, nc.vector.tensor_tensor(x, x, q[h][:], ALU.subtract), own)


def build(nc, io, out):
    with ExitStack() as ctx:
        c = Chip(nc, ctx, io)
        stage_setup(nc, c)
        stage_stats(nc, c, "ln0")
        stage_support(nc, c)
        stage_conv(nc, c, 0, c.t1)
        stage_hidden(nc, c)
        stage_conv(nc, c, 1, c.t2)
        stage_convolved(nc, c)
        stage_stats(nc, c, "ln1")
        stage_route(nc, c, 0)
        stage_last_bias(nc, c, 0)
        stage_experts0(nc, c)
        stage_stats(nc, c, "ln2")
        stage_node_mish(nc, c)
        stage_edges(nc, c)
        stage_node_out(nc, c)
        stage_stats(nc, c, "ln3")
        stage_route(nc, c, 1)
        stage_last_bias(nc, c, 1)
        stage_experts1(nc, c)
        whole = N // P
        with nc.semaphore("stored") as stored, nc.Block() as block:
            @block.sync
            def _(sp):
                sp.dma_start(out[0:whole * P, :].rearrange("(t p) d -> p t d", p=P), c.x[:, 0:whole, :]).then_inc(stored, 16)
                sp.dma_start(out[whole * P:N, :], c.x[0:N - whole * P, whole, :]).then_inc(stored, 16)
                sp.wait_ge(stored, 32)


def kernel(**inp):
    import concourse.bacc as bacc
    from concourse.bass_utils import run_bass_kernel_spmd as run
    nc = bacc.Bacc("TRN2", target_bir_lowering=False, num_devices=1)

    def padded(a, n, value=0):
        return np.concatenate([a, np.full((n - a.shape[0],) + a.shape[1:], value, a.dtype)])

    def blocks(w):
        return w.reshape(-1, P, w.shape[-1]).transpose(1, 0, 2)

    def experts(w):
        return np.stack([blocks(one) for one in w])

    a = {k: np.asarray(v) for k, v in inp.items()}
    dst = padded(a["dst"], C * P, N)
    arrays = {
        "x": padded(a["x"], NP),
        "src_t": padded(a["src"], C * P).reshape(C, P).T,
        "dst_t": dst.reshape(C, P).T,
        "dst_g": dst.reshape(2, EGP, CG * P).transpose(1, 0, 2),
        "weight_t": padded(a["edge_weight"], C * P).reshape(C, P).T,
        "iota": np.broadcast_to(np.arange(W, dtype=np.float32), (P, W)),
        "ident": np.eye(P, dtype=np.float32),
        "iota8": np.broadcast_to(np.arange(8, dtype=np.float32), (P, 8)),
        "edge_t": padded(a["edge_attr_256"], C * P).reshape(EG, CG * P, KD, P).transpose(0, 3, 2, 1),
        "r0_w1": blocks(a["L0_ffn_router_w1"]),
        "r0_b1": a["L0_ffn_router_b1"][:, None],
        "r0_w2": a["L0_ffn_router_w2"],
        "r0_b2": np.broadcast_to(a["L0_ffn_router_b2"], (P, E0)),
        "m0_w1": experts(a["L0_ffn_expert_w1"]),
        "m0_w2": experts(a["L0_ffn_expert_w2"]),
        "m0_w3": experts(a["L0_ffn_expert_w3"]),
        "m0_b1": a["L0_ffn_expert_b1"].reshape(E0, KD, P).transpose(2, 0, 1),
        "m0_b2": a["L0_ffn_expert_b2"].reshape(E0, KD, P).transpose(2, 0, 1),
        "m0_blast": a["L0_ffn_expert_b3"],
        "l_wd": blocks(a["L1_gnn_W_dense"].T),
        "l_bd": np.broadcast_to(a["L1_gnn_b_dense"], (3, D)),
        "l_we": blocks(a["L1_gnn_W_edge"].T),
        "l_be": np.broadcast_to(a["L1_gnn_b_edge"], (3, D)),
        "l_wo": blocks(a["L1_gnn_W_out"].T),
        "l_bo": np.broadcast_to(a["L1_gnn_b_out"], (3, D)),
        "r1_gamma": a["L1_ffn_gamma"].reshape(KD, P).T,
        "r1_beta": a["L1_ffn_beta"].reshape(KD, P).T,
        "r1_w2": blocks(a["L1_ffn_Wr"]),
        "r1_b2": np.broadcast_to(a["L1_ffn_br"], (P, E1)),
        "m1_w1": experts(a["L1_ffn_W1"]),
        "m1_w2": experts(a["L1_ffn_W2"]),
        "m1_b1": a["L1_ffn_b1"].reshape(E1, HM, P).transpose(2, 0, 1),
        "m1_blast": a["L1_ffn_b2"],
        "g_w1": blocks(a["L0_gnn_W1"]),
        "g_b1": a["L0_gnn_b1"][:, None],
        "g_w2": a["L0_gnn_W2"],
        "g_b2": np.broadcast_to(a["L0_gnn_b2"], (P, D)),
    }
    arrays = {k: np.ascontiguousarray(v) for k, v in arrays.items()}
    io = {k: nc.dram_tensor("in_" + k, v.shape, mybir.dt.from_np(v.dtype), kind="ExternalInput").ap() for k, v in arrays.items()}
    out = nc.dram_tensor("out", (N, D), FP32, kind="ExternalOutput").ap()
    build(nc, io, out)
    r = run(nc, [{"in_" + k: v for k, v in arrays.items()}], core_ids=[0])
    return r.results[0]["out"]
```

```python
import concourse.bass as bass
from concourse import mybir
from contextlib import ExitStack
import numpy as np

FP32 = mybir.dt.float32
BF16 = mybir.dt.bfloat16
I32 = mybir.dt.int32
U32 = mybir.dt.uint32
ALU = mybir.AluOpType
ACT = mybir.ActivationFunctionType
AX = mybir.AxisListType

P = 128
D = 256
KD = D // P
HID = 128
N = 6250
T = 52
NP = T * P
TG = 4
G = T // TG
GN = TG * P
E = 106250
C = 840
CG = 4
EG = C // CG
EGP = EG // 2
SLOTS = 6
IT = EG // SLOTS
MISH = SLOTS // 2
W = 64
TW = NP + W
EPS = 1e-5
E0 = 6
E1 = 8
H1 = 512
HM = H1 // P
NT = -(-N // P)
WHOLE = N // P
SLOT = 512
HALF = SLOT // 2
ROWS = (2 * N // SLOT + E1) * SLOT
FILLED = IT * SLOT
SG = 4
ZMAX = 20.0
LN2 = 0.6931471805599453


def take(eng, semaphore, n=1):
    eng.wait_ge(semaphore, n)
    eng.sem_inc(semaphore, -n)


def link(eng, ins, semaphore):
    ins.then_inc(semaphore, 1)
    take(eng, semaphore)


class Signals:

    def __init__(self, nc, prefix=""):
        self.nc, self.prefix, self.made = nc, prefix, []

    def __enter__(self):
        return self

    def __call__(self, name):
        self.made.append(self.nc.alloc_semaphore(self.prefix + name))
        return self.made[-1]

    def __exit__(self, *_):
        self.nc.clear_and_free_semaphores(self.made)
        self.nc.all_engine_barrier()


class Chip:

    def __init__(self, nc, ctx, io):
        self.nc, self.io = nc, io
        sb = lambda name, shape, dt=FP32: ctx.enter_context(nc.sbuf_tensor(name, shape, dt))
        self.x = sb("x_sb", [P, T, D])
        self.src = sb("src_sb", [P, C], I32)
        self.dstrel = sb("dstrel", [P, C])
        self.weight = sb("weight_sb", [P, C])
        self.base = sb("base_row", [1, EG], I32)
        self.window = sb("window_row", [1, EG], I32)
        self.passes = sb("passes", [1, 1], I32)
        self.iota = sb("iota_sb", [P, W])
        self.ident = sb("ident_sb", [P, P])
        self.mv = sb("mv", [P, T, 2])
        self.rstd = sb("rstd", [P, T])
        self.gate = sb("gate", [P, NT, 2])
        self.row = sb("row", [P, NT, 2], I32)
        self.slots = sb("slots", [1, 8], I32)
        self.start = sb("start", [1, 8], I32)
        self.eps = sb("eps_sb", [P, 1])
        dram = lambda name, shape, dt=FP32: nc.dram_tensor(name, shape, dt, kind="Internal").ap()
        self.t1 = dram("support_table", (NP, HID))
        self.t2 = dram("hidden_table", (NP, HID))
        self.t3 = dram("node_table", (NP, D))
        self.mish_d = dram("edge_mish_table", (EG, P, CG, D))
        self.rows_d = dram("expert_rows", (FILLED, D))
        self.outs_d = dram("expert_outs", (FILLED, D))
        self.base_d = dram("base_dram", (EG,))
        self.span_d = dram("span_dram", (EG,))

    def feature_table(self, name):
        return FeatureTable(self, name)


class FeatureTable:
    def __init__(self, c, name):
        self.c, self.name = c, name

    def __enter__(self):
        self.held = self.c.nc.sbuf_tensor(self.name, [P, KD, TW], FP32)
        self.c.feat = self.held.__enter__()

    def __exit__(self, *_):
        self.held.__exit__(None, None, None)


def stage_setup(nc, c):
    io = c.io
    with ExitStack() as ctx:
        sb = lambda name, shape, dt=FP32: ctx.enter_context(nc.sbuf_tensor(name, shape, dt))
        sem = ctx.enter_context(Signals(nc))
        dst_g = sb("dst_g", [EGP, 2, CG * P], I32)
        dst_gf = sb("dst_gf", [EGP, 2, CG * P])
        low = sb("low", [EGP, 2])
        high = sb("high", [EGP, 2])
        span = sb("span", [EGP, 2])
        dst_t = sb("dst_t", [P, C], I32)
        dst_tf = sb("dst_tf", [P, C])
        base_bc = sb("base_bc", [P, EG])
        base_1 = sb("base_1", [1, EG])
        span_1 = sb("span_1", [1, EG])
        widest = sb("widest", [1, 1])
        widest_i = sb("widest_i", [1, 1], I32)
        shifted = sb("shifted", [1, 1], I32)
        x_in, dst_in, edges_in = sem("x_in"), sem("dst_in"), sem("edges_in")
        own, spans_ready, spans_out, spans_in = sem("su_own"), sem("spans_ready"), sem("spans_out"), sem("spans_in")
        block = ctx.enter_context(nc.Block())

        @block.sync
        def _(sp):
            sp.dma_start(dst_g[:], io["dst_g"]).then_inc(dst_in, 16)
            sp.dma_start(dst_t[:], io["dst_t"]).then_inc(edges_in, 16)
            sp.dma_start(c.src[:], io["src_t"]).then_inc(x_in, 16)
            sp.dma_start(c.weight[:], io["weight_t"]).then_inc(x_in, 16)
            sp.dma_start(c.iota[:], io["iota"]).then_inc(x_in, 16)
            sp.dma_start(c.ident[:], io["ident"]).then_inc(x_in, 16)
            sp.dma_start(c.x[:], io["x"].rearrange("(t p) d -> p t d", p=P)).then_inc(x_in, 16)
            sp.wait_ge(spans_ready, 2)
            with nc.allow_non_contiguous_dma(reason="208 words"):
                sp.dma_start(c.base_d.rearrange("(a p) -> p a", p=EGP), low[:]).then_inc(spans_out, 16)
                sp.dma_start(c.span_d.rearrange("(a p) -> p a", p=EGP), span[:]).then_inc(spans_out, 16)
            sp.wait_ge(spans_out, 32)
            sp.dma_start(base_bc[:], c.base_d.partition_broadcast(P)).then_inc(spans_in, 16)
            sp.dma_start(base_1[:], c.base_d.rearrange("(a g) -> a g", a=1)).then_inc(spans_in, 16)
            sp.dma_start(span_1[:], c.span_d.rearrange("(a g) -> a g", a=1)).then_inc(spans_in, 16)
            sp.wait_ge(x_in, 5 * 16)

        @block.vector
        def _(dve):
            nc.vector.memset(c.eps[:], EPS)
            dve.wait_ge(dst_in, 16)
            link(dve, nc.vector.tensor_copy(dst_gf[:], dst_g[:]), own)
            nc.vector.tensor_reduce(low[:], dst_gf[:], AX.X, ALU.min).then_inc(spans_ready, 1)
            link(dve, nc.vector.tensor_reduce(high[:], dst_gf[:], AX.X, ALU.max), own)
            dve.wait_ge(spans_ready, 1)
            nc.vector.tensor_tensor(span[:], high[:], low[:], ALU.subtract).then_inc(spans_ready, 1)
            dve.wait_ge(edges_in, 16)
            link(dve, nc.vector.tensor_copy(dst_tf[:], dst_t[:]), own)
            dve.wait_ge(spans_in, 48)
            by_chunk = lambda a, j: a[:].rearrange("p (g j) -> p j g", j=CG)[:, j, :]
            for j in range(CG):
                nc.vector.tensor_tensor(by_chunk(c.dstrel, j), by_chunk(dst_tf, j), base_bc[:], ALU.subtract)
            nc.vector.tensor_copy(c.base[:], base_1[:])
            link(dve, nc.vector.tensor_reduce(widest[:], span_1[:], AX.X, ALU.max), own)
            link(dve, nc.vector.tensor_copy(widest_i[:], widest[:]), own)
            link(dve, nc.vector.tensor_single_scalar(shifted[:], widest_i[:], W.bit_length() - 1,
                                                     ALU.arith_shift_right), own)
            nc.vector.tensor_scalar_add(c.passes[:], shifted[:], 1.0)


def stage_stats(nc, c, name):
    with ExitStack() as ctx:
        stats = ctx.enter_context(nc.sbuf_tensor(f"{name}_stats", [P, TG, 6], FP32))
        mv4 = ctx.enter_context(nc.sbuf_tensor(f"{name}_mv4", [P, TG, 2], FP32))
        dev = ctx.enter_context(nc.sbuf_tensor(f"{name}_dev", [P, T], FP32))
        sem = ctx.enter_context(Signals(nc, name + "_"))
        stats_done = sem("stats_done")
        mv_done = sem("mv_done")
        all_done = sem("all_done")
        dev_done = sem("dev_done")
        block = ctx.enter_context(nc.Block())

        @block.vector
        def _(dve):
            with dve.Fori(0, G) as g:
                for s in range(TG):
                    nc.vector.bn_stats(stats[:, s, :], c.x[:, bass.ds(g * TG + s, 1), :].rearrange("p a d -> p (a d)")).then_inc(stats_done, 1)
                take(dve, stats_done, TG)
                for s in range(TG):
                    nc.vector.bn_aggr(mv4[:, s, :], stats[:, s, :]).then_inc(mv_done, 1)
                take(dve, mv_done, TG)
                link(dve, nc.vector.tensor_copy(c.mv[:, bass.ds(g * TG, TG), :], mv4[:]), mv_done)
            dve.sem_inc(all_done, 1)
            dve.wait_ge(dev_done, 1)
            link(dve, nc.vector.reciprocal(c.rstd[:], dev[:]), mv_done)
            link(dve, nc.vector.tensor_tensor(dev[:], c.rstd[:], c.rstd[:], ALU.mult), mv_done)
            link(dve, nc.vector.scalar_tensor_tensor(dev[:], c.mv[:, :, 1], EPS, dev[:], ALU.add, ALU.mult), mv_done)
            link(dve, nc.vector.tensor_scalar(dev[:], dev[:], -0.5, 1.5, ALU.mult, ALU.add), mv_done)
            nc.vector.tensor_tensor(c.rstd[:], c.rstd[:], dev[:], ALU.mult)

        @block.scalar
        def _(act):
            act.wait_ge(all_done, 1)
            act.activation(dev[:], c.mv[:, :, 1], ACT.Sqrt, bias=c.eps[:]).then_inc(dev_done, 1)


def tokens(a, g, h):
    return a[..., bass.ds(g * GN + h * (GN // 2), GN // 2)]


def normalise(dve, nc, c, xn, g, h, xn_ready):
    for s in range(2):
        tile = bass.ds(g * TG + 2 * h + s, 1)
        last = nc.vector.tensor_scalar(xn[:, s, :], c.x[:, tile, :].rearrange("p a d -> p (a d)"),
                                       c.mv[:, tile, 0], c.rstd[:, tile], ALU.subtract, ALU.mult)
    last.then_inc(xn_ready, 1)


def transpose_half(nc, c, out, xn):
    for k in range(KD):
        for s in range(2):
            last = nc.tensor.transpose(out[:, k, s * P:(s + 1) * P], xn[:, s, k * P:(k + 1) * P], c.ident[:])
    return last


def store_rows(sp, table, g, h, rows, rows_ready, rows_out, rows_free):
    take(sp, rows_ready[h])
    sp.dma_start(table[bass.ds(g * GN + h * (GN // 2), GN // 2), :].rearrange("(s p) d -> p s d", p=P),
                 rows[h][:]).then_inc(rows_out[h], 16)


def stage_support(nc, c):
    io = c.io
    with ExitStack() as ctx:
        sb = lambda name, shape, dt=FP32: ctx.enter_context(nc.sbuf_tensor(name, shape, dt))
        pb = lambda name, shape: ctx.enter_context(nc.psum_tensor(name, shape, FP32))
        sem = ctx.enter_context(Signals(nc))
        sem2 = lambda name: [sem(f"{name}{h}") for h in range(2)]
        w1 = sb("gw1", [P, KD, HID])
        xn = [sb(f"s_xn{h}", [P, 2, D]) for h in range(2)]
        xt = [sb(f"s_xt{h}", [P, KD, 2 * P]) for h in range(2)]
        rows = [sb(f"s_rows{h}", [P, 2, HID]) for h in range(2)]
        ps_t = [pb(f"s_pt{h}", [P, KD, 2 * P]) for h in range(2)]
        ps_y = [pb(f"s_py{h}", [P, 2, HID]) for h in range(2)]
        w_in = sem("s_w_in")
        xn_ready, pt_ready, xt_ready = sem2("s_xn_ready"), sem2("s_pt_ready"), sem2("s_xt_ready")
        py_ready, rows_ready = sem2("s_py_ready"), sem2("s_rows_ready")
        rows_out, rows_free = sem2("s_rows_out"), sem2("s_rows_free")
        block = ctx.enter_context(nc.Block())

        @block.sync
        def _(sp):
            sp.dma_start(w1[:], io["g_w1"]).then_inc(w_in, 16)
            with sp.Fori(0, G) as g:
                for h in range(2):
                    store_rows(sp, c.t1, g, h, rows, rows_ready, rows_out, rows_free)
                for h in range(2):
                    take(sp, rows_out[h], 16)
                    sp.sem_inc(rows_free[h], 1)

        @block.vector
        def _(dve):
            dve.sem_inc(rows_free[0], 1)
            dve.sem_inc(rows_free[1], 1)
            with dve.Fori(0, G) as g:
                for h in range(2):
                    normalise(dve, nc, c, xn[h], g, h, xn_ready[h])
                for h in range(2):
                    take(dve, py_ready[h])
                    take(dve, rows_free[h])
                    nc.vector.tensor_copy(rows[h][:], ps_y[h][:]).then_inc(rows_ready[h], 1)

        @block.scalar
        def _(act):
            with act.Fori(0, G) as g:
                for h in range(2):
                    take(act, pt_ready[h])
                    act.copy(xt[h][:], ps_t[h][:]).then_inc(xt_ready[h], 1)

        @block.tensor
        def _(pe):
            pe.wait_ge(w_in, 16)
            with pe.Fori(0, G) as g:
                for h in range(2):
                    take(pe, xn_ready[h])
                    transpose_half(nc, c, ps_t[h], xn[h]).then_inc(pt_ready[h], 1)
                for h in range(2):
                    take(pe, xt_ready[h])
                    for s in range(2):
                        for k in range(KD):
                            last = pe.matmul(ps_y[h][:, s, :], xt[h][:, k, s * P:(s + 1) * P], w1[:, k, :],
                                             start=k == 0, stop=k == KD - 1)
                    last.then_inc(py_ready[h], 1)


def stage_conv(nc, c, part, table):
    io, name = c.io, f"conv{part}"
    with ExitStack() as ctx:
        sb = lambda n, shape, dt=FP32: ctx.enter_context(nc.sbuf_tensor(f"{name}_{n}", shape, dt))
        pb = lambda n, shape: ctx.enter_context(nc.psum_tensor(f"{name}_{n}", shape, FP32))
        sem = ctx.enter_context(Signals(nc, name + "_"))
        idx = sb("idx", [P, 2, SLOTS // 2 * CG], I32)
        rel = sb("rel", [P, C])
        window = sb("window", [1, EG], I32)
        gath = [sb(f"gath{s}", [P, CG, HID]) for s in range(SLOTS)]
        hot = [sb(f"hot{s}", [P, CG, W]) for s in range(SLOTS)]
        we = sb("we", [P, KD, D])
        bias, parts, ones = bias_buffers(sb)
        ln2 = sb("ln2", [P, 1])
        edge = [sb(f"edge{r}", [P, KD, CG * P]) for r in range(MISH)]
        q = [sb(f"q{r}", [P, CG, D]) for r in range(MISH)]
        neg = [sb(f"neg{r}", [P, CG, D]) for r in range(MISH)]
        ps = [pb(f"ps{n}", [P, W]) for n in range(2)]
        ps_z = [pb(f"pz{r}", [P, CG, D]) for r in range(MISH)]
        if part == 0:
            zeros, filled = sb("zeros", [P, SLOT // P, D]), sem("filled")
        sums = c.feat[:, 0, :]
        gathered = [nc.alloc_semaphore(f"{name}_gathered{s}") for s in range(SLOTS)]
        slot_free = [sem(f"slot_free{s}") for s in range(SLOTS)]
        hot_ready = [sem(f"hot_ready{s}") for s in range(SLOTS)]
        ps_ready = [sem(f"ps_ready{n}") for n in range(2)]
        ps_free = [sem(f"ps_free{n}") for n in range(2)]
        idx_ready, own, act_own, neg_own = sem("idx_ready"), sem("own"), sem("act_own"), sem("neg_own")
        w_in, parts_ready = sem("w_in"), sem("parts_ready")
        per_r = lambda n: [sem(f"{n}{r}") for r in range(MISH)]
        edge_in, edge_free, z_done, z_free = per_r("edge_in"), per_r("edge_free"), per_r("z_done"), per_r("z_free")
        z_ready, q_ready, neg_ready, neg_out = per_r("z_ready"), per_r("q_ready"), per_r("neg_ready"), per_r("neg_out")
        block = ctx.enter_context(nc.Block())

        def load_passes(eng):
            return eng.value_load(c.passes[0:1, 0:1], min_val=1, max_val=TW // W)

        @block.sync
        def _(sp):
            group = lambda i, r: bass.ds(i * MISH + (part * IT * MISH + r), 1)

            def load(i, r):
                take(sp, edge_free[r])
                sp.dma_start(edge[r][:], io["edge_t"][group(i, r)].rearrange("a p k e -> p (a k) e")).then_inc(edge_in[r], 16)

            def store(i, r):
                take(sp, neg_ready[r])
                sp.dma_start(c.mish_d[group(i, r)].rearrange("a p j d -> p (a j) d"), neg[r][:]).then_inc(neg_out[r], 16)

            sp.dma_start(we[:], io["l_we"]).then_inc(w_in, 16)
            sp.dma_start(bias[0][:], io["l_be"]).then_inc(w_in, 16)
            for r in range(MISH):
                sp.sem_inc(edge_free[r], 1)
            with sp.Fori(0, load_passes(sp)) as k:
                for r in range(MISH):
                    load(0, r)
                with sp.Fori(0, IT - 1) as i:
                    for r in range(MISH):
                        load(i + 1, r)
                        store(i, r)
                for r in range(MISH):
                    store(IT - 1, r)
            for r in range(MISH):
                sp.wait_ge(neg_out[r], 16)

        @block.gpsimd
        def _(pool):
            for s in range(SLOTS):
                pool.sem_inc(slot_free[s], 1)
            with pool.Fori(0, load_passes(pool)) as k:
                with pool.Fori(0, IT) as i:
                    for half in range(2):
                        for s in range(half * 3, half * 3 + 3):
                            take(pool, slot_free[s])
                        nc.gpsimd.tensor_copy(idx[:, half, :], c.src[:, bass.ds(i * (SLOTS * CG) + half * (SLOTS // 2 * CG), SLOTS // 2 * CG)]).then_inc(idx_ready, 1)
                        take(pool, idx_ready)
                        for s in range(half * 3, half * 3 + 3):
                            for j in range(CG):
                                col = (s - half * 3) * CG + j
                                pool.indirect_dma_start(
                                    gath[s][:, j, :], None, table[:, :],
                                    bass.IndirectOffsetOnAxis(ap=idx[:, half, col:col + 1], axis=0),
                                ).then_inc(gathered[s], 16)

        @block.vector
        def _(dve):
            def mish_begin(r):
                take(dve, z_done[r])
                dve.sem_inc(edge_free[r], 1)
                nc.vector.tensor_scalar(q[r][:], ps_z[r][:], ZMAX, None, ALU.min).then_inc(z_ready[r], 1)

            def mish_end(r):
                take(dve, q_ready[r])
                take(dve, neg_out[r], 16)
                link(dve, nc.vector.scalar_tensor_tensor(neg[r][:], q[r][:], -1.0, ps_z[r][:], ALU.add, ALU.mult), neg_own)
                dve.sem_inc(z_free[r], 1)
                dve.sem_inc(neg_ready[r], 1)

            def add(i, s):
                at = dve.value_load(window[0:1, bass.ds(i * SLOTS + s, 1)], min_val=0, max_val=NP)
                take(dve, ps_ready[s % 2])
                here = sums[:, bass.ds(at, W)]
                link(dve, nc.vector.tensor_tensor(here, here, ps[s % 2][:], ALU.add), own)
                dve.sem_inc(ps_free[s % 2], 1)
                dve.sem_inc(slot_free[s], 1)

            def step(i, first):
                for s in range(SLOTS):
                    for j in range(CG):
                        col = bass.ds(i * (SLOTS * CG) + s * CG + j, 1)
                        last = nc.vector.tensor_scalar(hot[s][:, j, :], c.iota[:], rel[:, col], c.weight[:, col],
                                                       ALU.is_equal, ALU.mult)
                    last.then_inc(hot_ready[s], 1)
                for r in range(MISH):
                    add(i, 2 * r)
                    add(i, 2 * r + 1)
                    mish_begin(r)
                    if r or not first:
                        mish_end((r - 1) % MISH)

            for n in range(2):
                dve.sem_inc(ps_free[n], 1)
            for r in range(MISH):
                dve.sem_inc(z_free[r], 1)
                dve.sem_inc(neg_out[r], 16)
            nc.vector.memset(ln2[:], LN2)
            nc.vector.memset(ones[:], 1.0)
            nc.vector.memset(sums, 0.0)
            if part == 0:
                nc.vector.memset(zeros[:], 0.0)
            nc.vector.tensor_copy(rel[:], c.dstrel[:])
            link(dve, nc.vector.tensor_copy(window[:], c.base[:]), own)
            dve.wait_ge(w_in, 32)
            split_bias(dve, nc, c, bias, parts, own)
            dve.sem_inc(parts_ready, 2)
            with dve.Fori(0, load_passes(dve)) as k:
                step(0, True)
                with dve.Fori(1, IT) as i:
                    step(i, False)
                mish_end(MISH - 1)
                nc.vector.tensor_scalar(rel[:], rel[:], -float(W), None, ALU.add)
                link(dve, nc.vector.tensor_scalar(window[:], window[:], float(W), float(NP), ALU.add, ALU.min), own)

        @block.scalar
        def _(act):
            act.wait_ge(parts_ready, 1)
            log_exp_table(act)
            if part == 0:
                act.sem_inc(filled, 32)
            with act.Fori(0, load_passes(act)) as k:
                with act.Fori(0, IT) as i:
                    if part == 0:
                        take(act, filled, 32)
                        for table_d in (c.rows_d, c.outs_d):
                            act.dma_start(table_d[bass.ds(i * SLOT, SLOT), :].rearrange("(t p) d -> p t d", p=P), zeros[:]
                                          ).then_inc(filled, 16)
                    for r in range(MISH):
                        take(act, z_ready[r])
                        mish_factor(act, q[r][:], ln2, act_own, q_ready[r])
            if part == 0:
                act.wait_ge(filled, 32)

        @block.tensor
        def _(pe):
            def segment(k, i, s):
                take(pe, hot_ready[s])
                take(pe, ps_free[s % 2])
                pe.wait_ge(gathered[s], k * (IT * CG * 16) + i * (CG * 16) + CG * 16)
                for j in range(CG):
                    last = pe.matmul(ps[s % 2][:], gath[s][:, j, :], hot[s][:, j, :], start=j == 0, stop=j == CG - 1)
                last.then_inc(ps_ready[s % 2], 1)

            def product(r):
                take(pe, edge_in[r], 16)
                take(pe, z_free[r])
                for j in range(CG):
                    for m in range(KD):
                        pe.matmul(ps_z[r][:, j, :], edge[r][:, m, j * P:(j + 1) * P], we[:, m, :], start=m == 0, stop=False)
                    last = pe.matmul(ps_z[r][:, j, :], ones[:], parts[:], start=False, stop=True)
                last.then_inc(z_done[r], 1)

            pe.wait_ge(parts_ready, 1)
            with pe.Fori(0, load_passes(pe)) as k:
                with pe.Fori(0, IT) as i:
                    for r in range(MISH):
                        segment(k, i, 2 * r)
                        segment(k, i, 2 * r + 1)
                        product(r)


def stage_hidden(nc, c):
    io = c.io
    with ExitStack() as ctx:
        sb = lambda name, shape, dt=FP32: ctx.enter_context(nc.sbuf_tensor(name, shape, dt))
        sem = ctx.enter_context(Signals(nc))
        sem2 = lambda name: [sem(f"{name}{h}") for h in range(2)]
        b1 = sb("gb1", [P, 1])
        hid = [sb(f"h_hid{h}", [P, 2 * P]) for h in range(2)]
        rows = [sb(f"h_rows{h}", [P, 2, HID]) for h in range(2)]
        ps = [ctx.enter_context(nc.psum_tensor(f"h_ps{h}", [P, 2, HID], FP32)) for h in range(2)]
        b_in, own = sem("h_b_in"), sem("h_own")
        hid_ready, ps_ready, ps_free = sem2("h_hid_ready"), sem2("h_ps_ready"), sem2("h_ps_free")
        rows_ready, rows_out, rows_free = sem2("h_rows_ready"), sem2("h_rows_out"), sem2("h_rows_free")
        block = ctx.enter_context(nc.Block())

        @block.sync
        def _(sp):
            sp.dma_start(b1[:], io["g_b1"]).then_inc(b_in, 16)
            with sp.Fori(0, G) as g:
                for h in range(2):
                    store_rows(sp, c.t2, g, h, rows, rows_ready, rows_out, rows_free)
                for h in range(2):
                    take(sp, rows_out[h], 16)
                    sp.sem_inc(rows_free[h], 1)

        @block.scalar
        def _(act):
            act.wait_ge(b_in, 16)
            act.sem_inc(ps_free[0], 1)
            act.sem_inc(ps_free[1], 1)
            with act.Fori(0, G) as g:
                for h in range(2):
                    take(act, ps_free[h])
                    act.activation(hid[h][:], tokens(c.feat[:, 0, :], g, h), ACT.Relu, bias=b1[:]).then_inc(hid_ready[h], 1)

        @block.tensor
        def _(pe):
            with pe.Fori(0, G) as g:
                for h in range(2):
                    take(pe, hid_ready[h])
                    for s in range(2):
                        last = pe.transpose(ps[h][:, s, :], hid[h][:, s * P:(s + 1) * P], c.ident[:])
                    last.then_inc(ps_ready[h], 1)

        @block.vector
        def _(dve):
            dve.sem_inc(rows_free[0], 1)
            dve.sem_inc(rows_free[1], 1)
            with dve.Fori(0, G) as g:
                for h in range(2):
                    take(dve, ps_ready[h])
                    take(dve, rows_free[h])
                    link(dve, nc.vector.tensor_copy(rows[h][:], ps[h][:]), own)
                    dve.sem_inc(rows_ready[h], 1)
                    dve.sem_inc(ps_free[h], 1)


def stage_convolved(nc, c):
    io = c.io
    with ExitStack() as ctx:
        sb = lambda name, shape, dt=FP32: ctx.enter_context(nc.sbuf_tensor(name, shape, dt))
        sem = ctx.enter_context(Signals(nc))
        sem2 = lambda name: [sem(f"{name}{h}") for h in range(2)]
        w2, b2 = sb("gw2", [P, D]), sb("gb2", [P, D])
        sums = [sb(f"c_sums{h}", [P, 2 * P]) for h in range(2)]
        ps = [ctx.enter_context(nc.psum_tensor(f"c_ps{h}", [P, 2, D], FP32)) for h in range(2)]
        w_in = sem("c_w_in")
        own = sem("c_own")
        sums_ready, ps_ready, ps_free = sem2("c_sums_ready"), sem2("c_ps_ready"), sem2("c_ps_free")
        block = ctx.enter_context(nc.Block())

        @block.sync
        def _(sp):
            sp.dma_start(w2[:], io["g_w2"]).then_inc(w_in, 16)
            sp.dma_start(b2[:], io["g_b2"]).then_inc(w_in, 16)

        @block.scalar
        def _(act):
            act.sem_inc(ps_free[0], 1)
            act.sem_inc(ps_free[1], 1)
            with act.Fori(0, G) as g:
                for h in range(2):
                    take(act, ps_free[h])
                    act.copy(sums[h][:], tokens(c.feat[:, 0, :], g, h)).then_inc(sums_ready[h], 1)

        @block.tensor
        def _(pe):
            pe.wait_ge(w_in, 32)
            with pe.Fori(0, G) as g:
                for h in range(2):
                    take(pe, sums_ready[h])
                    for s in range(2):
                        last = pe.matmul(ps[h][:, s, :], sums[h][:, s * P:(s + 1) * P], w2[:], start=True, stop=True)
                    last.then_inc(ps_ready[h], 1)

        @block.vector
        def _(dve):
            dve.wait_ge(w_in, 32)
            with dve.Fori(0, G) as g:
                for h in range(2):
                    x = c.x[:, bass.ds(g * TG + 2 * h, 2), :]
                    link(dve, nc.vector.tensor_tensor(x, x, b2[:].unsqueeze(1).to_broadcast([P, 2, D]), ALU.add), own)
                    take(dve, ps_ready[h])
                    link(dve, nc.vector.tensor_tensor(x, x, ps[h][:], ALU.add), own)
                    dve.sem_inc(ps_free[h], 1)


def stage_route(nc, c, mix):
    io, name = c.io, f"r{mix}"
    experts = (E0, E1)[mix]
    with ExitStack() as ctx:
        sb = lambda n, shape, dt=FP32: ctx.enter_context(nc.sbuf_tensor(f"{name}_{n}", shape, dt))
        pb = lambda n, shape: ctx.enter_context(nc.psum_tensor(f"{name}_{n}", shape, FP32))
        sem = ctx.enter_context(Signals(nc, name + "_"))
        sem2 = lambda n: [sem(f"{n}{h}") for h in range(2)]
        if mix == 0:
            w1, b1 = sb("w1", [P, KD, P]), sb("b1", [P, 1])
            hid = [sb(f"hid{h}", [P, 2 * P]) for h in range(2)]
            w2 = sb("w2", [P, E0])
        else:
            gamma, beta, w2 = sb("gamma", [P, KD]), sb("beta", [P, KD]), sb("w2", [P, KD, E1])
        xt = [sb(f"xt{h}", [P, KD, 2 * P]) for h in range(2)]
        b2 = sb("b2", [P, experts])
        iota8, real, before, ones = sb("iota8", [P, 8]), sb("real", [P, NT]), sb("before", [P, P]), sb("ones", [P, P])
        xn = [sb(f"xn{h}", [P, 2, D]) for h in range(2)]
        logit = sb("logit", [P, T, 8])
        top = sb("top", [P, T])
        total = sb("total", [P, T])
        best = sb("best", [P, NT, 8])
        best_at = sb("best_at", [P, NT, 8], U32)
        at = sb("at", [P, NT, 2])
        gap, share = sb("gap", [P, NT]), sb("share", [P, NT])
        is_nth = [sb(f"is_nth{n}", [P, NT, 8]) for n in range(2)]
        chosen = sb("chosen", [P, NT, 8])
        upto = [sb(f"upto{n}", [P, NT, 8]) for n in range(2)]
        place, picked, row = sb("place", [P, NT, 8]), sb("picked", [P, NT, 8]), sb("row", [P, NT])
        filled, filled_i, slots_i = sb("filled", [P, 8]), sb("filled_i", [P, 8], I32), sb("slots_i", [P, 8], I32)
        slots_f, start_f = sb("slots_f", [P, 8]), sb("start_f", [P, 8])
        slots_upto = [sb(f"slots_upto{n}", [P, 8]) for n in range(2)]
        ps_rank, ps_all = pb("rank", [P, 64, 8]), pb("all", [P, 64, 8])
        ps_t = [pb(f"pt{h}", [P, KD, 2 * P]) for h in range(2)]
        ps_h = [pb(f"ph{h}", [P, 2 * P]) for h in range(2)]
        ps_l = [pb(f"pl{h}", [P, 2, 8]) for h in range(2)]
        w_in, own = sem("w_in"), sem("own")
        xn_ready, pt_ready, xt_ready = sem2("xn_ready"), sem2("pt_ready"), sem2("xt_ready")
        ph_ready, hid_ready, pl_ready = sem2("ph_ready"), sem2("hid_ready"), sem2("pl_ready")
        shifted_ready, exp_ready, gap_ready, gap_exp = sem("shifted_ready"), sem("exp_ready"), sem("gap_ready"), sem("gap_exp")
        chosen_ready, rank_ready = sem("chosen_ready"), sem("rank_ready")
        block = ctx.enter_context(nc.Block())
        loads = ([(w1, "r0_w1"), (b1, "r0_b1"), (w2, "r0_w2"), (b2, "r0_b2")] if mix == 0 else
                 [(gamma, "r1_gamma"), (beta, "r1_beta"), (w2, "r1_w2"), (b2, "r1_b2")])
        loads += [(iota8, "iota8"), (real, "real"), (before, "before")]

        @block.sync
        def _(sp):
            for tile, key in loads:
                sp.dma_start(tile[:], io[key]).then_inc(w_in, 16)

        @block.vector
        def _(dve):
            def running_sum(bufs, size, cut):
                now, step = 0, 1
                while step < size:
                    a, b = bufs[now], bufs[1 - now]
                    nc.vector.tensor_copy(cut(b, 0, step), cut(a, 0, step))
                    link(dve, nc.vector.tensor_tensor(cut(b, step, size), cut(a, step, size), cut(a, 0, size - step), ALU.add), own)
                    now, step = 1 - now, 2 * step
                return bufs[now]

            nc.vector.memset(logit[:], -1e30)
            nc.vector.memset(ones[:], 1.0)
            dve.wait_ge(w_in, 16 * len(loads))
            with dve.Fori(0, G) as g:
                for h in range(2):
                    normalise(dve, nc, c, xn[h], g, h, xn_ready[h])
                for h in range(2):
                    take(dve, pl_ready[h])
                    link(dve, nc.vector.tensor_tensor(logit[:, bass.ds(g * TG + 2 * h, 2), 0:experts], ps_l[h][:, :, 0:experts],
                                                      b2[:].unsqueeze(1).to_broadcast([P, 2, experts]), ALU.add), own)
            if mix == 0:
                some = logit[:, :, 0:experts]
                wide = lambda ap: ap.unsqueeze(2).to_broadcast([P, T, experts])
                link(dve, nc.vector.tensor_reduce(top[:], some, AX.X, ALU.max), own)
                nc.vector.tensor_tensor(some, some, wide(top[:]), ALU.subtract).then_inc(shifted_ready, 1)
                take(dve, exp_ready)
                link(dve, nc.vector.tensor_reduce(total[:], some, AX.X, ALU.add), own)
                link(dve, nc.vector.reciprocal(total[:], total[:]), own)
                link(dve, nc.vector.tensor_tensor(some, some, wide(total[:]), ALU.mult), own)
            for t in range(NT):
                last = nc.vector.max(best[:, t, :], logit[:, t, :])
            link(dve, last, own)
            nc.vector.tensor_tensor(gap[:], best[:, :, 1], best[:, :, 0], ALU.subtract).then_inc(gap_ready, 1)
            for t in range(NT):
                last = nc.vector.max_index(best_at[:, t, :], best[:, t, :], logit[:, t, :])
            link(dve, last, own)
            link(dve, nc.vector.tensor_copy(at[:], best_at[:, :, 0:2]), own)
            every = iota8[:].unsqueeze(1).to_broadcast([P, NT, 8])
            over = lambda ap: ap.unsqueeze(2).to_broadcast([P, NT, 8])
            for n in range(2):
                link(dve, nc.vector.tensor_tensor(is_nth[n][:], every, over(at[:, :, n]), ALU.is_equal), own)
            link(dve, nc.vector.tensor_tensor(chosen[:], is_nth[0][:], is_nth[1][:], ALU.add), own)
            nc.vector.tensor_tensor(chosen[:], chosen[:], over(real[:]), ALU.mult).then_inc(chosen_ready, 1)
            take(dve, gap_exp)
            link(dve, nc.vector.tensor_scalar_add(share[:], gap[:], 1.0), own)
            link(dve, nc.vector.reciprocal(share[:], share[:]), own)
            nc.vector.tensor_copy(c.gate[:, :, 0], share[:])
            nc.vector.tensor_tensor(c.gate[:, :, 1], gap[:], share[:], ALU.mult)
            take(dve, rank_ready)
            link(dve, nc.vector.tensor_copy(upto[0][:], ps_all[:, 0:NT, :]), own)
            upto_t = running_sum(upto, NT, lambda a, i, j: a[:, i:j, :])
            link(dve, nc.vector.tensor_scalar(filled[:], upto_t[:, NT - 1, :], 1.0, float(SLOT - 1), ALU.max, ALU.add), own)
            link(dve, nc.vector.tensor_copy(filled_i[:], filled[:]), own)
            link(dve, nc.vector.tensor_single_scalar(slots_i[:], filled_i[:], SLOT.bit_length() - 1, ALU.arith_shift_right), own)
            nc.vector.tensor_copy(c.slots[:], slots_i[0:1, :])
            nc.vector.tensor_copy(slots_f[:], slots_i[:])
            link(dve, nc.vector.tensor_copy(slots_upto[0][:], slots_i[:]), own)
            slots_e = running_sum(slots_upto, 8, lambda a, i, j: a[:, i:j])
            link(dve, nc.vector.tensor_tensor(start_f[:], slots_e[:], slots_f[:], ALU.subtract), own)
            link(dve, nc.vector.tensor_scalar(start_f[:], start_f[:], float(SLOT), None, ALU.mult), own)
            nc.vector.tensor_copy(c.start[:], start_f[0:1, :])
            link(dve, nc.vector.tensor_tensor(place[:], upto_t[:], ps_all[:, 0:NT, :], ALU.subtract), own)
            link(dve, nc.vector.tensor_tensor(place[:], place[:], ps_rank[:, 0:NT, :], ALU.add), own)
            link(dve, nc.vector.tensor_tensor(place[:], place[:], start_f[:].unsqueeze(1).to_broadcast([P, NT, 8]), ALU.add), own)
            for n in range(2):
                link(dve, nc.vector.tensor_tensor(picked[:], is_nth[n][:], place[:], ALU.mult), own)
                link(dve, nc.vector.tensor_reduce(row[:], picked[:], AX.X, ALU.add), own)
                nc.vector.tensor_copy(c.row[:, :, n], row[:])

        @block.scalar
        def _(act):
            act.wait_ge(w_in, 16 * len(loads))
            with act.Fori(0, G) as g:
                for h in range(2):
                    take(act, pt_ready[h])
                    if mix == 0:
                        last = act.copy(xt[h][:], ps_t[h][:])
                    else:
                        for k in range(KD):
                            last = act.activation(xt[h][:, k, :], ps_t[h][:, k, :], ACT.Identity,
                                                  scale=gamma[:, k:k + 1], bias=beta[:, k:k + 1])
                    last.then_inc(xt_ready[h], 1)
                if mix == 0:
                    for h in range(2):
                        take(act, ph_ready[h])
                        act.activation(hid[h][:], ps_h[h][:], ACT.Relu, bias=b1[:]).then_inc(hid_ready[h], 1)
            if mix == 0:
                take(act, shifted_ready)
                act.activation(logit[:, :, 0:experts], logit[:, :, 0:experts], ACT.Exp).then_inc(exp_ready, 1)
            take(act, gap_ready)
            act.activation(gap[:], gap[:], ACT.Exp).then_inc(gap_exp, 1)

        @block.tensor
        def _(pe):
            pe.wait_ge(w_in, 16 * len(loads))
            with pe.Fori(0, G) as g:
                for h in range(2):
                    take(pe, xn_ready[h])
                    transpose_half(nc, c, ps_t[h], xn[h]).then_inc(pt_ready[h], 1)
                if mix == 0:
                    for h in range(2):
                        take(pe, xt_ready[h])
                        for k in range(KD):
                            last = pe.matmul(ps_h[h][:], w1[:, k, :], xt[h][:, k, :], start=k == 0, stop=k == KD - 1)
                        last.then_inc(ph_ready[h], 1)
                    for h in range(2):
                        take(pe, hid_ready[h])
                        for s in range(2):
                            last = pe.matmul(ps_l[h][:, s, 0:E0], hid[h][:, s * P:(s + 1) * P], w2[:], start=True, stop=True)
                        last.then_inc(pl_ready[h], 1)
                else:
                    for h in range(2):
                        take(pe, xt_ready[h])
                        for s in range(2):
                            for k in range(KD):
                                last = pe.matmul(ps_l[h][:, s, 0:E1], xt[h][:, k, s * P:(s + 1) * P], w2[:, k, :],
                                                 start=k == 0, stop=k == KD - 1)
                        last.then_inc(pl_ready[h], 1)
            take(pe, chosen_ready)
            flat = chosen[:].rearrange("p t e -> p (t e)")
            pe.matmul(ps_rank[:, 0:NT, :].rearrange("p t e -> p (t e)"), before[:], flat, start=True, stop=True)
            pe.matmul(ps_all[:, 0:NT, :].rearrange("p t e -> p (t e)"), ones[:], flat, start=True, stop=True).then_inc(rank_ready, 1)


def stage_scatter(nc, c, mix):
    name = f"sc{mix}"
    steps = WHOLE // (2 * SG)
    with ExitStack() as ctx:
        sb = lambda n, shape, dt=FP32: ctx.enter_context(nc.sbuf_tensor(f"{name}_{n}", shape, dt))
        sem = ctx.enter_context(Signals(nc, name + "_"))
        xn = [sb(f"xn{r}", [P, SG, D]) for r in range(2)]
        idx = [sb(f"idx{r}", [P, SG, 2], I32) for r in range(2)]
        xn_ready, idx_ready = [sem(f"xn_ready{r}") for r in range(2)], sem("idx_ready")
        scattered = [nc.alloc_semaphore(f"{name}_scattered{r}") for r in range(2)]
        block = ctx.enter_context(nc.Block())
        per_step = SG * 2 * 16
        last_rows = N - WHOLE * P

        @block.vector
        def _(dve):
            def rows(i, r):
                for s in range(SG):
                    tile = bass.ds(i * (2 * SG) + r * SG + s, 1)
                    last = nc.vector.tensor_scalar(xn[r][:, s, :], c.x[:, tile, :].rearrange("p a d -> p (a d)"),
                                                   c.mv[:, tile, 0], c.rstd[:, tile], ALU.subtract, ALU.mult)
                last.then_inc(xn_ready[r], 1)

            for r in range(2):
                rows(0, r)
            with dve.Fori(1, steps) as i:
                for r in range(2):
                    dve.wait_ge(scattered[r], i * per_step)
                    rows(i, r)
            dve.wait_ge(scattered[0], steps * per_step)
            nc.vector.tensor_scalar(xn[0][:, 0, :], c.x[:, WHOLE, :], c.mv[:, WHOLE, 0:1], c.rstd[:, WHOLE:WHOLE + 1],
                                    ALU.subtract, ALU.mult).then_inc(xn_ready[0], 1)
            dve.wait_ge(scattered[1], steps * per_step)
            dve.wait_ge(scattered[0], steps * per_step + 32)

        @block.gpsimd
        def _(pool):
            def scatter(r, s, rows):
                for n in range(2):
                    pool.indirect_dma_start(
                        c.rows_d[:, :], bass.IndirectOffsetOnAxis(ap=idx[r][0:rows, s, n:n + 1], axis=0),
                        xn[r][0:rows, s, :], None,
                    ).then_inc(scattered[r], 16)

            with pool.Fori(0, steps) as i:
                for r in range(2):
                    take(pool, xn_ready[r])
                    nc.gpsimd.tensor_copy(idx[r][:], c.row[:, bass.ds(i * (2 * SG) + r * SG, SG), :]).then_inc(idx_ready, 1)
                    take(pool, idx_ready)
                    for s in range(SG):
                        scatter(r, s, P)
            take(pool, xn_ready[0])
            nc.gpsimd.tensor_copy(idx[0][:, 0, :], c.row[:, WHOLE, :]).then_inc(idx_ready, 1)
            take(pool, idx_ready)
            scatter(0, 0, last_rows)


def stage_combine(nc, c, mix):
    name = f"cb{mix}"
    steps = WHOLE // (2 * SG)
    with ExitStack() as ctx:
        sb = lambda n, shape, dt=FP32: ctx.enter_context(nc.sbuf_tensor(f"{name}_{n}", shape, dt))
        sem = ctx.enter_context(Signals(nc, name + "_"))
        outs = [sb(f"outs{r}", [P, SG, 2, D]) for r in range(2)]
        idx = [sb(f"idx{r}", [P, SG, 2], I32) for r in range(2)]
        outs_free, idx_ready, own = [sem(f"outs_free{r}") for r in range(2)], sem("idx_ready"), sem("own")
        gathered = [nc.alloc_semaphore(f"{name}_gathered{r}") for r in range(2)]
        block = ctx.enter_context(nc.Block())
        per_step = SG * 2 * 16
        last_rows = N - WHOLE * P

        @block.gpsimd
        def _(pool):
            def gather(r, s, rows):
                for n in range(2):
                    pool.indirect_dma_start(
                        outs[r][0:rows, s, n, :], None, c.outs_d[:, :],
                        bass.IndirectOffsetOnAxis(ap=idx[r][0:rows, s, n:n + 1], axis=0),
                    ).then_inc(gathered[r], 16)

            for r in range(2):
                pool.sem_inc(outs_free[r], 1)
            with pool.Fori(0, steps) as i:
                for r in range(2):
                    take(pool, outs_free[r])
                    nc.gpsimd.tensor_copy(idx[r][:], c.row[:, bass.ds(i * (2 * SG) + r * SG, SG), :]).then_inc(idx_ready, 1)
                    take(pool, idx_ready)
                    for s in range(SG):
                        gather(r, s, P)
            take(pool, outs_free[0])
            nc.gpsimd.tensor_copy(idx[0][:, 0, :], c.row[:, WHOLE, :]).then_inc(idx_ready, 1)
            take(pool, idx_ready)
            gather(0, 0, last_rows)

        @block.vector
        def _(dve):
            with dve.Fori(0, steps) as i:
                for r in range(2):
                    dve.wait_ge(gathered[r], i * per_step + per_step)
                    for n in range(2):
                        for s in range(SG):
                            tile = bass.ds(i * (2 * SG) + r * SG + s, 1)
                            x = c.x[:, tile, :].rearrange("p a d -> p (a d)")
                            last = nc.vector.scalar_tensor_tensor(x, outs[r][:, s, n, :], c.gate[:, tile, n], x, ALU.mult, ALU.add)
                        link(dve, last, own)
                    dve.sem_inc(outs_free[r], 1)
            dve.wait_ge(gathered[0], steps * per_step + 32)
            x = c.x[0:last_rows, WHOLE, :]
            for n in range(2):
                link(dve, nc.vector.scalar_tensor_tensor(x, outs[0][0:last_rows, 0, n, :], c.gate[0:last_rows, WHOLE, n:n + 1], x,
                                                         ALU.mult, ALU.add), own)


def stage_experts(nc, c, mix):
    io, name = c.io, f"e{mix}"
    experts = (E0, E1)[mix]
    hm = (KD, HM)[mix]
    with ExitStack() as ctx:
        sb = lambda n, shape, dt=FP32: ctx.enter_context(nc.sbuf_tensor(f"{name}_{n}", shape, dt))
        pb = lambda n, shape: ctx.enter_context(nc.psum_tensor(f"{name}_{n}", shape, FP32))
        sem = ctx.enter_context(Signals(nc, name + "_"))
        sem2 = lambda n: [sem(f"{n}{h}") for h in range(2)]
        w_first = [sb(f"w_first{e}", [P, KD, hm * P]) for e in range(experts)]
        w_last = [sb(f"w_last{e}", [P, hm, D]) for e in range(experts)]
        b_first, b_last = sb("b_first", [P, experts, hm]), sb("b_last", [P, experts, D])
        if mix == 0:
            w_mid, b_mid = [sb(f"w_mid{e}", [P, KD, D]) for e in range(E0)], sb("b_mid", [P, E0, KD])
            mid = [sb(f"mid{h}", [P, KD, HALF]) for h in range(2)]
            ps_m = [pb(f"pm{h}", [P, KD, HALF]) for h in range(2)]
        else:
            gamma, beta = sb("gamma", [P, KD]), sb("beta", [P, KD])
        rows = [sb(f"rows{h}", [P, 2, D]) for h in range(2)]
        xt = [sb(f"xt{h}", [P, KD, HALF]) for h in range(2)]
        hid = [sb(f"hid{h}", [P, hm, HALF]) for h in range(2)]
        outs = [sb(f"outs{h}", [P, 2, D]) for h in range(2)]
        ps_t = [pb(f"pt{h}", [P, KD, HALF]) for h in range(2)]
        ps_h = [pb(f"ph{h}", [P, hm, HALF]) for h in range(2)]
        ps_y = [pb(f"py{h}", [P, 2, D]) for h in range(2)]
        b_in = sem("b_in")
        w_in = [sem(f"w_in{e}") for e in range(experts)]
        rows_in, rows_free, pt_ready, xt_ready = sem2("rows_in"), sem2("rows_free"), sem2("pt_ready"), sem2("xt_ready")
        ph_ready, hid_ready, pm_ready, mid_ready = sem2("ph_ready"), sem2("hid_ready"), sem2("pm_ready"), sem2("mid_ready")
        py_ready, outs_ready, outs_out = sem2("py_ready"), sem2("outs_ready"), sem2("outs_out")
        block = ctx.enter_context(nc.Block())
        small = [(b_first, f"m{mix}_b1"), (b_last, f"m{mix}_blast")]
        small += [(b_mid, "m0_b2")] if mix == 0 else [(gamma, "r1_gamma"), (beta, "r1_beta")]
        layers = [(w_first, "m0_w1"), (w_mid, "m0_w2"), (w_last, "m0_w3")] if mix == 0 else [(w_first, "m1_w1"), (w_last, "m1_w2")]

        def slots(eng, e):
            return eng.value_load(c.slots[0:1, e:e + 1], min_val=1, max_val=-(-N // SLOT))

        def half_rows(table, start, j, h):
            at = nc.s_assert_within(start + j * SLOT, 0, ROWS - SLOT, skip_runtime_bounds_check_because="the slots of all experts fit in ROWS")
            return table[bass.ds(at + h * HALF, HALF), :].rearrange("(s p) d -> p s d", p=P)

        @block.gpsimd
        def _(pool):
            for e in range(experts):
                for w, key in layers:
                    pool.dma_start(w[e][:], io[key][e]).then_inc(w_in[e], 16)

        @block.sync
        def _(sp):
            for tile, key in small:
                sp.dma_start(tile[:], io[key]).then_inc(b_in, 16)
            for h in range(2):
                sp.sem_inc(rows_free[h], 1)
            for e in range(experts):
                start = sp.value_load(c.start[0:1, e:e + 1], min_val=0, max_val=ROWS - SLOT)
                with sp.Fori(0, slots(sp, e)) as j:
                    for h in range(2):
                        take(sp, rows_free[h])
                        sp.dma_start(rows[h][:], half_rows(c.rows_d, start, j, h)).then_inc(rows_in[h], 16)

        @block.tensor
        def _(pe):
            def layer(out, w, given, blocks):
                for m in range(blocks):
                    for k in range(KD):
                        last = pe.matmul(out[:, m, :], w[:, k, m * P:(m + 1) * P], given[:, k, :], start=k == 0, stop=k == KD - 1)
                return last

            for e in range(experts):
                pe.wait_ge(w_in[e], 16 * len(layers))
                with pe.Fori(0, slots(pe, e)) as j:
                    for h in range(2):
                        take(pe, rows_in[h], 16)
                        transpose_half(nc, c, ps_t[h], rows[h]).then_inc(pt_ready[h], 1)
                    for h in range(2):
                        take(pe, xt_ready[h])
                        layer(ps_h[h], w_first[e], xt[h], hm).then_inc(ph_ready[h], 1)
                    if mix == 0:
                        for h in range(2):
                            take(pe, hid_ready[h])
                            layer(ps_m[h], w_mid[e], hid[h], KD).then_inc(pm_ready[h], 1)
                    given, ready = (mid, mid_ready) if mix == 0 else (hid, hid_ready)
                    for h in range(2):
                        take(pe, ready[h])
                        for s in range(2):
                            for k in range(hm):
                                last = pe.matmul(ps_y[h][:, s, :], given[h][:, k, s * P:(s + 1) * P], w_last[e][:, k, :],
                                                 start=k == 0, stop=k == hm - 1)
                        last.then_inc(py_ready[h], 1)

        @block.scalar
        def _(act):
            act.wait_ge(b_in, 16 * len(small))
            for e in range(experts):
                start = act.value_load(c.start[0:1, e:e + 1], min_val=0, max_val=ROWS - SLOT)
                with act.Fori(0, slots(act, e)) as j:
                    for h in range(2):
                        take(act, ph_ready[h])
                        for m in range(hm):
                            last = act.activation(hid[h][:, m, :], ps_h[h][:, m, :], (ACT.Relu, ACT.Gelu)[mix], bias=b_first[:, e, m:m + 1])
                        last.then_inc(hid_ready[h], 1)
                    for h in range(2):
                        take(act, outs_ready[h])
                        act.dma_start(half_rows(c.outs_d, start, j, h), outs[h][:]).then_inc(outs_out[h], 16)
            for h in range(2):
                act.wait_ge(outs_out[h], 16)

        @block.vector
        def _(dve):
            for h in range(2):
                dve.sem_inc(outs_out[h], 16)
            dve.wait_ge(b_in, 16 * len(small))
            for e in range(experts):
                with dve.Fori(0, slots(dve, e)) as j:
                    for h in range(2):
                        take(dve, pt_ready[h])
                        dve.sem_inc(rows_free[h], 1)
                        if mix == 0:
                            last = nc.vector.tensor_copy(xt[h][:], ps_t[h][:])
                        else:
                            for k in range(KD):
                                last = nc.vector.tensor_scalar(xt[h][:, k, :], ps_t[h][:, k, :], gamma[:, k:k + 1], beta[:, k:k + 1],
                                                               ALU.mult, ALU.add)
                        last.then_inc(xt_ready[h], 1)
                    if mix == 0:
                        for h in range(2):
                            take(dve, pm_ready[h])
                            for m in range(KD):
                                last = nc.vector.tensor_scalar(mid[h][:, m, :], ps_m[h][:, m, :], b_mid[:, e, m:m + 1], 0.0,
                                                               ALU.add, ALU.max)
                            last.then_inc(mid_ready[h], 1)
                    for h in range(2):
                        take(dve, py_ready[h])
                        take(dve, outs_out[h], 16)
                        nc.vector.tensor_tensor(outs[h][:], ps_y[h][:], b_last[:, e, :].unsqueeze(1).to_broadcast([P, 2, D]),
                                                ALU.add).then_inc(outs_ready[h], 1)


def split_bias(dve, nc, c, bias, parts, own):
    b, high, rest, total = bias
    link(dve, nc.vector.tensor_copy(high[:], b[:]), own)
    link(dve, nc.vector.tensor_scalar(total[:], high[:], c.ident[0:3, 0:1], None, ALU.mult), own)
    link(dve, nc.vector.tensor_tensor(rest[:], b[:], high[:], ALU.subtract), own)
    for row in (1, 2):
        link(dve, nc.vector.tensor_copy(high[:], rest[:]), own)
        link(dve, nc.vector.scalar_tensor_tensor(total[:], high[:], c.ident[0:3, row:row + 1], total[:], ALU.mult, ALU.add), own)
        link(dve, nc.vector.tensor_tensor(rest[:], rest[:], high[:], ALU.subtract), own)
    link(dve, nc.vector.tensor_copy(parts[:], total[:]), own)


def bias_buffers(sb):
    return ((sb("bias", [3, D]), sb("bias_high", [3, D], BF16), sb("bias_rest", [3, D]), sb("bias_total", [3, D])),
            sb("bias_parts", [3, D], BF16), sb("ones3", [3, P], BF16))


def mish_factor(act, q, ln2, own, ready):
    link(act, act.activation(q, q, ACT.Exp), own)
    link(act, act.activation(q, q, ACT.Square, bias=1.0), own)
    link(act, act.activation(q, q, ACT.Ln, bias=1.0), own)
    act.activation(q, q, ACT.Exp, scale=-1.0, bias=ln2[:]).then_inc(ready, 1)


def log_exp_table(act):
    act.preload_act_table_set("natural_log_exp_and_others")


def stage_node_mish(nc, c):
    io = c.io
    with ExitStack() as ctx:
        sb = lambda n, shape, dt=FP32: ctx.enter_context(nc.sbuf_tensor(f"n_{n}", shape, dt))
        pb = lambda n, shape: ctx.enter_context(nc.psum_tensor(f"n_{n}", shape, FP32))
        sem = ctx.enter_context(Signals(nc, "n_"))
        sem2 = lambda n: [sem(f"{n}{h}") for h in range(2)]
        wd = sb("wd", [P, KD, D])
        bias, parts, ones = bias_buffers(sb)
        ln2 = sb("ln2", [P, 1])
        xn = [sb(f"xn{h}", [P, 2, D]) for h in range(2)]
        xt = [sb(f"xt{h}", [P, KD, 2 * P]) for h in range(2)]
        q = [sb(f"q{h}", [P, 2, D]) for h in range(2)]
        rows = [sb(f"rows{h}", [P, 2, D]) for h in range(2)]
        ps_t = [pb(f"pt{h}", [P, KD, 2 * P]) for h in range(2)]
        ps_y = [pb(f"py{h}", [P, 2, D]) for h in range(2)]
        ps_u = [pb(f"pu{h}", [P, KD, 2 * P]) for h in range(2)]
        w_in, own, act_own, parts_ready = sem("w_in"), sem("own"), sem("act_own"), sem("parts_ready")
        xn_ready, pt_ready, xt_ready, py_ready = sem2("xn_ready"), sem2("pt_ready"), sem2("xt_ready"), sem2("py_ready")
        z_ready, q_ready, rows_ready, rows_pe = sem2("z_ready"), sem2("q_ready"), sem2("rows_ready"), sem2("rows_pe")
        pu_ready, pu_free, rows_out, rows_free = sem2("pu_ready"), sem2("pu_free"), sem2("rows_out"), sem2("rows_free")
        block = ctx.enter_context(nc.Block())

        @block.sync
        def _(sp):
            sp.dma_start(wd[:], io["l_wd"]).then_inc(w_in, 16)
            sp.dma_start(bias[0][:], io["l_bd"]).then_inc(w_in, 16)
            with sp.Fori(0, G) as g:
                for h in range(2):
                    store_rows(sp, c.t3, g, h, rows, rows_ready, rows_out, rows_free)
                for h in range(2):
                    take(sp, rows_out[h], 16)
                    sp.sem_inc(rows_free[h], 1)

        @block.vector
        def _(dve):
            for h in range(2):
                dve.sem_inc(rows_free[h], 1)
            nc.vector.memset(ln2[:], LN2)
            nc.vector.memset(ones[:], 1.0)
            dve.wait_ge(w_in, 32)
            split_bias(dve, nc, c, bias, parts, own)
            dve.sem_inc(parts_ready, 2)
            with dve.Fori(0, G) as g:
                for h in range(2):
                    normalise(dve, nc, c, xn[h], g, h, xn_ready[h])
                for h in range(2):
                    take(dve, py_ready[h])
                    nc.vector.tensor_scalar(q[h][:], ps_y[h][:], ZMAX, None, ALU.min).then_inc(z_ready[h], 1)
                for h in range(2):
                    take(dve, q_ready[h])
                    link(dve, nc.vector.tensor_scalar(q[h][:], q[h][:], -1.0, 1.0, ALU.mult, ALU.add), own)
                    take(dve, rows_free[h])
                    link(dve, nc.vector.tensor_tensor(rows[h][:], q[h][:], ps_y[h][:], ALU.mult), own)
                    dve.sem_inc(rows_ready[h], 1)
                    dve.sem_inc(rows_pe[h], 1)
                    take(dve, pu_ready[h])
                    nc.vector.tensor_copy(tokens(c.feat[:, :, :], g, h), ps_u[h][:])

        @block.scalar
        def _(act):
            act.wait_ge(parts_ready, 1)
            log_exp_table(act)
            with act.Fori(0, G) as g:
                for h in range(2):
                    take(act, pt_ready[h])
                    act.copy(xt[h][:], ps_t[h][:]).then_inc(xt_ready[h], 1)
                for h in range(2):
                    take(act, z_ready[h])
                    mish_factor(act, q[h][:], ln2, act_own, q_ready[h])

        @block.tensor
        def _(pe):
            pe.wait_ge(parts_ready, 1)
            with pe.Fori(0, G) as g:
                for h in range(2):
                    take(pe, xn_ready[h])
                    transpose_half(nc, c, ps_t[h], xn[h]).then_inc(pt_ready[h], 1)
                for h in range(2):
                    take(pe, xt_ready[h])
                    for s in range(2):
                        for k in range(KD):
                            pe.matmul(ps_y[h][:, s, :], xt[h][:, k, s * P:(s + 1) * P], wd[:, k, :], start=k == 0, stop=False)
                        last = pe.matmul(ps_y[h][:, s, :], ones[:], parts[:], start=False, stop=True)
                    last.then_inc(py_ready[h], 1)
                for h in range(2):
                    take(pe, rows_pe[h])
                    transpose_half(nc, c, ps_u[h], rows[h]).then_inc(pu_ready[h], 1)


def stage_edges(nc, c):
    RING = 3
    with ExitStack() as ctx:
        sb = lambda n, shape, dt=FP32: ctx.enter_context(nc.sbuf_tensor(f"x_{n}", shape, dt))
        pb = lambda n, shape: ctx.enter_context(nc.psum_tensor(f"x_{n}", shape, FP32))
        sem = ctx.enter_context(Signals(nc, "x_"))
        idx = sb("idx", [P, 2, SLOTS // 2 * CG], I32)
        rel = sb("rel", [P, C])
        window = sb("window", [1, EG], I32)
        neg = [sb(f"neg{n}", [P, CG, D]) for n in range(RING)]
        node = [sb(f"node{s}", [P, CG, D]) for s in range(SLOTS)]
        hot = [sb(f"hot{n}", [P, CG, W]) for n in range(RING)]
        ps_a = [pb(f"pa{n}", [P, KD, W]) for n in range(RING)]
        own, add_own, idx_ready = sem("own"), sem("add_own"), sem("idx_ready")
        neg_in = [sem(f"neg_in{n}") for n in range(RING)]
        neg_free = [sem(f"neg_free{n}") for n in range(RING)]
        msg_ready, sum_ready = sem("msg_ready"), sem("sum_ready")
        gathered = [nc.alloc_semaphore(f"x_gathered{s}") for s in range(SLOTS)]
        node_free = [sem(f"node_free{s}") for s in range(SLOTS)]
        block = ctx.enter_context(nc.Block())

        def load_passes(eng):
            return eng.value_load(c.passes[0:1, 0:1], min_val=1, max_val=TW // W)

        @block.sync
        def _(sp):
            for n in range(RING):
                sp.sem_inc(neg_free[n], 1)
            with sp.Fori(0, load_passes(sp)) as k:
                with sp.Fori(0, IT) as i:
                    for s in range(SLOTS):
                        take(sp, neg_free[s % RING])
                        sp.dma_start(neg[s % RING][:], c.mish_d[bass.ds(i * SLOTS + s, 1)].rearrange("a p j d -> p (a j) d")
                                     ).then_inc(neg_in[s % RING], 16)

        @block.gpsimd
        def _(pool):
            for s in range(SLOTS):
                pool.sem_inc(node_free[s], 1)
            with pool.Fori(0, load_passes(pool)) as k:
                with pool.Fori(0, IT) as i:
                    for half in range(2):
                        for s in range(half * 3, half * 3 + 3):
                            take(pool, node_free[s])
                        nc.gpsimd.tensor_copy(idx[:, half, :], c.src[:, bass.ds(i * (SLOTS * CG) + half * (SLOTS // 2 * CG), SLOTS // 2 * CG)]).then_inc(idx_ready, 1)
                        take(pool, idx_ready)
                        for s in range(half * 3, half * 3 + 3):
                            for j in range(CG):
                                col = (s - half * 3) * CG + j
                                pool.indirect_dma_start(
                                    node[s][:, j, :], None, c.t3[:, :],
                                    bass.IndirectOffsetOnAxis(ap=idx[:, half, col:col + 1], axis=0),
                                ).then_inc(gathered[s], 16)

        @block.tensor
        def _(pe):
            with pe.Fori(0, load_passes(pe)) as k:
                with pe.Fori(0, IT) as i:
                    for s in range(SLOTS):
                        n = s % RING
                        take(pe, msg_ready)
                        for m in range(KD):
                            for j in range(CG):
                                last = pe.matmul(ps_a[n][:, m, :], node[s][:, j, m * P:(m + 1) * P], hot[n][:, j, :],
                                                 start=j == 0, stop=j == CG - 1)
                        last.then_inc(sum_ready, 1)

        @block.scalar
        def _(act):
            with act.Fori(0, load_passes(act)) as k:
                with act.Fori(0, IT) as i:
                    for s in range(SLOTS):
                        take(act, own)
                        act.activation(node[s][:], node[s][:], ACT.Relu).then_inc(msg_ready, 1)

        @block.vector
        def _(dve):
            def message(k, i, s):
                for j in range(CG):
                    nc.vector.tensor_scalar(hot[s % RING][:, j, :], c.iota[:], rel[:, bass.ds(i * (SLOTS * CG) + s * CG + j, 1)],
                                            None, ALU.is_equal)
                take(dve, neg_in[s % RING], 16)
                dve.wait_ge(gathered[s], k * (IT * CG * 16) + i * (CG * 16) + CG * 16)
                nc.vector.tensor_tensor(node[s][:], node[s][:], neg[s % RING][:], ALU.subtract).then_inc(own, 1)

            def add(i, s):
                at = dve.value_load(window[0:1, bass.ds(i * SLOTS + s, 1)], min_val=0, max_val=NP)
                take(dve, sum_ready)
                dve.sem_inc(neg_free[s % RING], 1)
                dve.sem_inc(node_free[s], 1)
                here = c.feat[:, :, bass.ds(at, W)]
                link(dve, nc.vector.tensor_tensor(here, here, ps_a[s % RING][:], ALU.add), add_own)

            nc.vector.tensor_copy(rel[:], c.dstrel[:])
            link(dve, nc.vector.tensor_copy(window[:], c.base[:]), add_own)
            with dve.Fori(0, load_passes(dve)) as k:
                for s in range(SLOTS):
                    message(k, 0, s)
                    if s:
                        add(0, s - 1)
                with dve.Fori(1, IT) as i:
                    for s in range(SLOTS):
                        message(k, i, s)
                        add(i if s else i - 1, (s - 1) % SLOTS)
                add(IT - 1, SLOTS - 1)
                nc.vector.tensor_scalar(rel[:], rel[:], -float(W), None, ALU.add)
                link(dve, nc.vector.tensor_scalar(window[:], window[:], float(W), float(NP), ALU.add, ALU.min), add_own)


def stage_node_out(nc, c):
    io = c.io
    with ExitStack() as ctx:
        sb = lambda n, shape, dt=FP32: ctx.enter_context(nc.sbuf_tensor(f"o_{n}", shape, dt))
        sem = ctx.enter_context(Signals(nc, "o_"))
        sem2 = lambda n: [sem(f"{n}{h}") for h in range(2)]
        wo = sb("wo", [P, KD, D])
        bias, parts, ones = bias_buffers(sb)
        ln2 = sb("ln2", [P, 1])
        xt = [sb(f"xt{h}", [P, KD, 2 * P]) for h in range(2)]
        q = [sb(f"q{h}", [P, 2, D]) for h in range(2)]
        ps_y = [ctx.enter_context(nc.psum_tensor(f"o_py{h}", [P, 2, D], FP32)) for h in range(2)]
        w_in, own, act_own, parts_ready = sem("w_in"), sem("own"), sem("act_own"), sem("parts_ready")
        xt_ready, xt_free, py_ready, z_ready, q_ready = sem2("xt_ready"), sem2("xt_free"), sem2("py_ready"), sem2("z_ready"), sem2("q_ready")
        block = ctx.enter_context(nc.Block())

        @block.sync
        def _(sp):
            sp.dma_start(wo[:], io["l_wo"]).then_inc(w_in, 16)
            sp.dma_start(bias[0][:], io["l_bo"]).then_inc(w_in, 16)

        @block.gpsimd
        def _(pool):
            for h in range(2):
                pool.sem_inc(xt_free[h], 1)
            with pool.Fori(0, G) as g:
                for h in range(2):
                    take(pool, xt_free[h])
                    nc.gpsimd.tensor_copy(xt[h][:], tokens(c.feat[:, :, :], g, h)).then_inc(xt_ready[h], 1)

        @block.tensor
        def _(pe):
            pe.wait_ge(parts_ready, 1)
            with pe.Fori(0, G) as g:
                for h in range(2):
                    take(pe, xt_ready[h])
                    for s in range(2):
                        for k in range(KD):
                            pe.matmul(ps_y[h][:, s, :], xt[h][:, k, s * P:(s + 1) * P], wo[:, k, :], start=k == 0, stop=False)
                        last = pe.matmul(ps_y[h][:, s, :], ones[:], parts[:], start=False, stop=True)
                    last.then_inc(py_ready[h], 1)

        @block.scalar
        def _(act):
            act.wait_ge(parts_ready, 1)
            log_exp_table(act)
            with act.Fori(0, G) as g:
                for h in range(2):
                    take(act, z_ready[h])
                    mish_factor(act, q[h][:], ln2, act_own, q_ready[h])

        @block.vector
        def _(dve):
            nc.vector.memset(ln2[:], LN2)
            nc.vector.memset(ones[:], 1.0)
            dve.wait_ge(w_in, 32)
            split_bias(dve, nc, c, bias, parts, own)
            dve.sem_inc(parts_ready, 2)
            with dve.Fori(0, G) as g:
                for h in range(2):
                    take(dve, py_ready[h])
                    nc.vector.tensor_scalar(q[h][:], ps_y[h][:], ZMAX, None, ALU.min).then_inc(z_ready[h], 1)
                for h in range(2):
                    x = c.x[:, bass.ds(g * TG + 2 * h, 2), :]
                    take(dve, q_ready[h])
                    link(dve, nc.vector.scalar_tensor_tensor(q[h][:], q[h][:], -1.0, ps_y[h][:], ALU.add, ALU.mult), own)
                    dve.sem_inc(xt_free[h], 1)
                    link(dve, nc.vector.tensor_tensor(x, x, q[h][:], ALU.subtract), own)


def build(nc, io, out):
    with ExitStack() as ctx:
        c = Chip(nc, ctx, io)
        stage_setup(nc, c)
        stage_stats(nc, c, "ln0")
        stage_support(nc, c)
        with c.feature_table("sums_table"):
            stage_conv(nc, c, 0, c.t1)
            stage_hidden(nc, c)
            stage_conv(nc, c, 1, c.t2)
            stage_convolved(nc, c)
        stage_stats(nc, c, "ln1")
        stage_route(nc, c, 0)
        stage_scatter(nc, c, 0)
        stage_experts(nc, c, 0)
        stage_combine(nc, c, 0)
        stage_stats(nc, c, "ln2")
        with c.feature_table("messages_table"):
            stage_node_mish(nc, c)
            stage_edges(nc, c)
            stage_node_out(nc, c)
        stage_stats(nc, c, "ln3")
        stage_route(nc, c, 1)
        stage_scatter(nc, c, 1)
        stage_experts(nc, c, 1)
        stage_combine(nc, c, 1)
        with nc.semaphore("stored") as stored, nc.Block() as block:
            @block.sync
            def _(sp):
                sp.dma_start(out[0:WHOLE * P, :].rearrange("(t p) d -> p t d", p=P), c.x[:, 0:WHOLE, :]).then_inc(stored, 16)
                sp.dma_start(out[WHOLE * P:N, :], c.x[0:N - WHOLE * P, WHOLE, :]).then_inc(stored, 16)
                sp.wait_ge(stored, 32)


def kernel(**inp):
    import concourse.bacc as bacc
    from concourse.bass_utils import run_bass_kernel_spmd as run
    nc = bacc.Bacc("TRN2", target_bir_lowering=False, num_devices=1)

    def padded(a, n, value=0):
        return np.concatenate([a, np.full((n - a.shape[0],) + a.shape[1:], value, a.dtype)])

    def blocks(w):
        return w.reshape(-1, P, w.shape[-1]).transpose(1, 0, 2)

    def experts(w):
        return np.stack([blocks(one) for one in w])

    a = {k: np.asarray(v) for k, v in inp.items()}
    dst = padded(a["dst"], C * P, N)
    arrays = {
        "x": padded(a["x"], NP),
        "src_t": padded(a["src"], C * P).reshape(C, P).T,
        "dst_t": dst.reshape(C, P).T,
        "dst_g": dst.reshape(2, EGP, CG * P).transpose(1, 0, 2),
        "weight_t": padded(a["edge_weight"], C * P).reshape(C, P).T,
        "iota": np.broadcast_to(np.arange(W, dtype=np.float32), (P, W)),
        "ident": np.eye(P, dtype=np.float32),
        "real": (np.arange(NT)[None, :] * P + np.arange(P)[:, None] < N).astype(np.float32),
        "before": np.triu(np.ones((P, P), np.float32), 1),
        "iota8": np.broadcast_to(np.arange(8, dtype=np.float32), (P, 8)),
        "edge_t": padded(a["edge_attr_256"], C * P).reshape(EG, CG * P, KD, P).transpose(0, 3, 2, 1),
        "r0_w1": blocks(a["L0_ffn_router_w1"]),
        "r0_b1": a["L0_ffn_router_b1"][:, None],
        "r0_w2": a["L0_ffn_router_w2"],
        "r0_b2": np.broadcast_to(a["L0_ffn_router_b2"], (P, E0)),
        "m0_w1": experts(a["L0_ffn_expert_w1"]),
        "m0_w2": experts(a["L0_ffn_expert_w2"]),
        "m0_w3": experts(a["L0_ffn_expert_w3"]),
        "m0_b1": a["L0_ffn_expert_b1"].reshape(E0, KD, P).transpose(2, 0, 1),
        "m0_b2": a["L0_ffn_expert_b2"].reshape(E0, KD, P).transpose(2, 0, 1),
        "m0_blast": np.broadcast_to(a["L0_ffn_expert_b3"], (P, E0, D)),
        "l_wd": blocks(a["L1_gnn_W_dense"].T),
        "l_bd": np.broadcast_to(a["L1_gnn_b_dense"], (3, D)),
        "l_we": blocks(a["L1_gnn_W_edge"].T),
        "l_be": np.broadcast_to(a["L1_gnn_b_edge"], (3, D)),
        "l_wo": blocks(a["L1_gnn_W_out"].T),
        "l_bo": np.broadcast_to(a["L1_gnn_b_out"], (3, D)),
        "r1_gamma": a["L1_ffn_gamma"].reshape(KD, P).T,
        "r1_beta": a["L1_ffn_beta"].reshape(KD, P).T,
        "r1_w2": blocks(a["L1_ffn_Wr"]),
        "r1_b2": np.broadcast_to(a["L1_ffn_br"], (P, E1)),
        "m1_w1": experts(a["L1_ffn_W1"]),
        "m1_w2": experts(a["L1_ffn_W2"]),
        "m1_b1": a["L1_ffn_b1"].reshape(E1, HM, P).transpose(2, 0, 1),
        "m1_blast": np.broadcast_to(a["L1_ffn_b2"], (P, E1, D)),
        "g_w1": blocks(a["L0_gnn_W1"]),
        "g_b1": a["L0_gnn_b1"][:, None],
        "g_w2": a["L0_gnn_W2"],
        "g_b2": np.broadcast_to(a["L0_gnn_b2"], (P, D)),
    }
    arrays = {k: np.ascontiguousarray(v) for k, v in arrays.items()}
    io = {k: nc.dram_tensor("in_" + k, v.shape, mybir.dt.from_np(v.dtype), kind="ExternalInput").ap() for k, v in arrays.items()}
    out = nc.dram_tensor("out", (N, D), FP32, kind="ExternalOutput").ap()
    build(nc, io, out)
    r = run(nc, [{"in_" + k: v for k, v in arrays.items()}], core_ids=[0])
    return r.results[0]["out"]
```

```python
import concourse.bass as bass
from concourse import mybir
from contextlib import ExitStack
import numpy as np

FP32 = mybir.dt.float32
BF16 = mybir.dt.bfloat16
I32 = mybir.dt.int32
U32 = mybir.dt.uint32
ALU = mybir.AluOpType
ACT = mybir.ActivationFunctionType
AX = mybir.AxisListType

P = 128
D = 256
KD = D // P
HID = 128
N = 6250
T = 52
NP = T * P
TG = 4
G = T // TG
GN = TG * P
E = 106250
C = 840
CG = 4
EG = C // CG
EGP = EG // 2
SLOTS = 6
IT = EG // SLOTS
HALF_COLS = SLOTS // 2 * CG
MISH = SLOTS // 2
BEFORE = ((0, 1), (2, 3), (4, 5))
W = 64
TW = NP + W
EPS = 1e-5
E0 = 6
E1 = 8
H1 = 512
HM = H1 // P
NT = -(-N // P)
WHOLE = N // P
SLOT = 512
HALF = SLOT // 2
ROWS = (2 * N // SLOT + E1) * SLOT
FILLED = IT * SLOT
SG = 4
ZMAX = 20.0
LN2 = 0.6931471805599453


def take(eng, semaphore, n=1):
    eng.wait_ge(semaphore, n)
    eng.sem_inc(semaphore, -n)


def link(eng, ins, semaphore):
    ins.then_inc(semaphore, 1)
    take(eng, semaphore)


class Signals:

    def __init__(self, nc, prefix=""):
        self.nc, self.prefix, self.made = nc, prefix, []

    def __enter__(self):
        return self

    def __call__(self, name):
        self.made.append(self.nc.alloc_semaphore(self.prefix + name))
        return self.made[-1]

    def __exit__(self, *_):
        self.nc.clear_and_free_semaphores(self.made)
        self.nc.all_engine_barrier()


class Chip:

    def __init__(self, nc, ctx, io):
        self.nc, self.io = nc, io
        sb = lambda name, shape, dt=FP32: ctx.enter_context(nc.sbuf_tensor(name, shape, dt))
        self.x = sb("x_sb", [P, T, D])
        self.src = sb("src_sb", [P, C], I32)
        self.dstrel = sb("dstrel", [P, C])
        self.weight = sb("weight_sb", [P, C])
        self.base = sb("base_row", [1, EG], I32)
        self.window = sb("window_row", [1, EG], I32)
        self.passes = sb("passes", [1, 1], I32)
        self.iota = sb("iota_sb", [P, W])
        self.ident = sb("ident_sb", [P, P])
        self.mv = sb("mv", [P, T, 2])
        self.rstd = sb("rstd", [P, T])
        self.gate = sb("gate", [P, NT, 2])
        self.row = sb("row", [P, NT, 2], I32)
        self.slots = sb("slots", [1, 8], I32)
        self.start = sb("start", [1, 8], I32)
        self.eps = sb("eps_sb", [P, 1])
        dram = lambda name, shape, dt=FP32: nc.dram_tensor(name, shape, dt, kind="Internal").ap()
        self.t1 = dram("support_table", (NP, HID))
        self.t2 = dram("hidden_table", (NP, HID))
        self.t3 = dram("node_table", (NP, D))
        self.mish_d = dram("edge_mish_table", (EG, P, CG, D))
        self.rows_d = dram("expert_rows", (FILLED, D))
        self.outs_d = dram("expert_outs", (FILLED, D))
        self.base_d = dram("base_dram", (EG,))
        self.span_d = dram("span_dram", (EG,))

    def feature_table(self, name):
        return FeatureTable(self, name)


class FeatureTable:

    def __init__(self, c, name):
        self.c, self.name = c, name

    def __enter__(self):
        self.held = self.c.nc.sbuf_tensor(self.name, [P, KD, TW], FP32)
        self.c.feat = self.held.__enter__()

    def __exit__(self, *_):
        self.held.__exit__(None, None, None)


class Moments:

    def __init__(self, nc, c, sb, sem):
        self.nc, self.c = nc, c
        self.stats, self.mv = sb("stats", [P, TG, 6]), sb("mv_group", [P, TG, 2])
        self.done = sem("moments_done")

    def of(self, dve, g):
        nc, c = self.nc, self.c
        for s in range(TG):
            last = nc.vector.bn_stats(self.stats[:, s, :], c.x[:, bass.ds(g * TG + s, 1), :].rearrange("p a d -> p (a d)"))
        link(dve, last, self.done)
        for s in range(TG):
            last = nc.vector.bn_aggr(self.mv[:, s, :], self.stats[:, s, :])
        link(dve, last, self.done)
        link(dve, nc.vector.tensor_copy(c.mv[:, bass.ds(g * TG, TG), :], self.mv[:]), self.done)


def stage_setup(nc, c):
    io = c.io
    with ExitStack() as ctx:
        sb = lambda name, shape, dt=FP32: ctx.enter_context(nc.sbuf_tensor(name, shape, dt))
        sem = ctx.enter_context(Signals(nc))
        dst_g = sb("dst_g", [EGP, 2, CG * P], I32)
        dst_gf = sb("dst_gf", [EGP, 2, CG * P])
        low = sb("low", [EGP, 2])
        high = sb("high", [EGP, 2])
        span = sb("span", [EGP, 2])
        dst_t = sb("dst_t", [P, C], I32)
        dst_tf = sb("dst_tf", [P, C])
        base_bc = sb("base_bc", [P, EG])
        base_1 = sb("base_1", [1, EG])
        span_1 = sb("span_1", [1, EG])
        widest = sb("widest", [1, 1])
        widest_i = sb("widest_i", [1, 1], I32)
        shifted = sb("shifted", [1, 1], I32)
        moments = Moments(nc, c, lambda n, shape: sb("su_" + n, shape), lambda n: sem("su_" + n))
        x_in, dst_in, edges_in = sem("x_in"), sem("dst_in"), sem("edges_in")
        own, spans_ready, spans_out, spans_in = sem("su_own"), sem("spans_ready"), sem("spans_out"), sem("spans_in")
        block = ctx.enter_context(nc.Block())

        @block.sync
        def _(sp):
            sp.dma_start(dst_g[:], io["dst_g"]).then_inc(dst_in, 16)
            sp.dma_start(dst_t[:], io["dst_t"]).then_inc(edges_in, 16)
            sp.dma_start(c.x[:], io["x"].rearrange("(t p) d -> p t d", p=P)).then_inc(x_in, 16)
            sp.dma_start(c.src[:], io["src_t"]).then_inc(x_in, 16)
            sp.dma_start(c.weight[:], io["weight_t"]).then_inc(x_in, 16)
            sp.dma_start(c.iota[:], io["iota"]).then_inc(x_in, 16)
            sp.dma_start(c.ident[:], io["ident"]).then_inc(x_in, 16)
            sp.wait_ge(spans_ready, 2)
            with nc.allow_non_contiguous_dma(reason="208 words"):
                sp.dma_start(c.base_d.rearrange("(a p) -> p a", p=EGP), low[:]).then_inc(spans_out, 16)
                sp.dma_start(c.span_d.rearrange("(a p) -> p a", p=EGP), span[:]).then_inc(spans_out, 16)
            sp.wait_ge(spans_out, 32)
            sp.dma_start(base_bc[:], c.base_d.partition_broadcast(P)).then_inc(spans_in, 16)
            sp.dma_start(base_1[:], c.base_d.rearrange("(a g) -> a g", a=1)).then_inc(spans_in, 16)
            sp.dma_start(span_1[:], c.span_d.rearrange("(a g) -> a g", a=1)).then_inc(spans_in, 16)
            sp.wait_ge(x_in, 5 * 16)

        @block.vector
        def _(dve):
            nc.vector.memset(c.eps[:], EPS)
            dve.wait_ge(dst_in, 16)
            link(dve, nc.vector.tensor_copy(dst_gf[:], dst_g[:]), own)
            nc.vector.tensor_reduce(low[:], dst_gf[:], AX.X, ALU.min).then_inc(spans_ready, 1)
            link(dve, nc.vector.tensor_reduce(high[:], dst_gf[:], AX.X, ALU.max), own)
            dve.wait_ge(spans_ready, 1)
            nc.vector.tensor_tensor(span[:], high[:], low[:], ALU.subtract).then_inc(spans_ready, 1)
            dve.wait_ge(edges_in, 16)
            link(dve, nc.vector.tensor_copy(dst_tf[:], dst_t[:]), own)
            dve.wait_ge(x_in, 5 * 16)
            with dve.Fori(0, G) as g:
                moments.of(dve, g)
            dve.wait_ge(spans_in, 48)
            by_chunk = lambda a, j: a[:].rearrange("p (g j) -> p j g", j=CG)[:, j, :]
            for j in range(CG):
                nc.vector.tensor_tensor(by_chunk(c.dstrel, j), by_chunk(dst_tf, j), base_bc[:], ALU.subtract)
            nc.vector.tensor_copy(c.base[:], base_1[:])
            link(dve, nc.vector.tensor_reduce(widest[:], span_1[:], AX.X, ALU.max), own)
            link(dve, nc.vector.tensor_copy(widest_i[:], widest[:]), own)
            link(dve, nc.vector.tensor_single_scalar(shifted[:], widest_i[:], W.bit_length() - 1,
                                                     ALU.arith_shift_right), own)
            nc.vector.tensor_scalar_add(c.passes[:], shifted[:], 1.0)


def stage_deviation(nc, c, name):
    with ExitStack() as ctx:
        sb = lambda n, shape: ctx.enter_context(nc.sbuf_tensor(f"{name}_{n}", shape, FP32))
        sem = ctx.enter_context(Signals(nc, name + "_"))
        dev = sb("dev", [P, T])
        own, dev_done = sem("own"), sem("dev_done")
        block = ctx.enter_context(nc.Block())

        @block.vector
        def _(dve):
            dve.wait_ge(dev_done, 1)
            link(dve, nc.vector.reciprocal(c.rstd[:], dev[:]), own)
            link(dve, nc.vector.tensor_tensor(dev[:], c.rstd[:], c.rstd[:], ALU.mult), own)
            link(dve, nc.vector.scalar_tensor_tensor(dev[:], c.mv[:, :, 1], EPS, dev[:], ALU.add, ALU.mult), own)
            link(dve, nc.vector.tensor_scalar(dev[:], dev[:], -0.5, 1.5, ALU.mult, ALU.add), own)
            nc.vector.tensor_tensor(c.rstd[:], c.rstd[:], dev[:], ALU.mult)

        @block.scalar
        def _(act):
            act.activation(dev[:], c.mv[:, :, 1], ACT.Sqrt, bias=c.eps[:]).then_inc(dev_done, 1)


def tokens(a, g, h):
    return a[..., bass.ds(g * GN + h * (GN // 2), GN // 2)]


def normalise(dve, nc, c, xn, g, h, xn_ready):
    for s in range(2):
        tile = bass.ds(g * TG + 2 * h + s, 1)
        last = nc.vector.tensor_scalar(xn[:, s, :], c.x[:, tile, :].rearrange("p a d -> p (a d)"),
                                       c.mv[:, tile, 0], c.rstd[:, tile], ALU.subtract, ALU.mult)
    last.then_inc(xn_ready, 1)


def transpose_half(nc, c, out, xn):
    for k in range(KD):
        for s in range(2):
            last = nc.tensor.transpose(out[:, k, s * P:(s + 1) * P], xn[:, s, k * P:(k + 1) * P], c.ident[:])
    return last


def store_rows(sp, table, g, h, rows, rows_ready, rows_out):
    take(sp, rows_ready[h])
    sp.dma_start(table[bass.ds(g * GN + h * (GN // 2), GN // 2), :].rearrange("(s p) d -> p s d", p=P),
                 rows[h][:]).then_inc(rows_out[h], 16)


def stage_support(nc, c):
    io = c.io
    with ExitStack() as ctx:
        sb = lambda name, shape, dt=FP32: ctx.enter_context(nc.sbuf_tensor(name, shape, dt))
        pb = lambda name, shape: ctx.enter_context(nc.psum_tensor(name, shape, FP32))
        sem = ctx.enter_context(Signals(nc))
        sem2 = lambda name: [sem(f"{name}{h}") for h in range(2)]
        w1 = sb("gw1", [P, KD, HID])
        xn = [sb(f"s_xn{h}", [P, 2, D]) for h in range(2)]
        xt = [sb(f"s_xt{h}", [P, KD, 2 * P]) for h in range(2)]
        rows = [sb(f"s_rows{h}", [P, 2, HID]) for h in range(2)]
        ps_t = [pb(f"s_pt{h}", [P, KD, 2 * P]) for h in range(2)]
        ps_y = [pb(f"s_py{h}", [P, 2, HID]) for h in range(2)]
        w_in, own = sem("s_w_in"), sem("s_own")
        xn_free, py_free = sem2("s_xn_free"), sem2("s_py_free")
        xn_ready, pt_ready, xt_ready = sem2("s_xn_ready"), sem2("s_pt_ready"), sem2("s_xt_ready")
        py_ready, rows_ready = sem2("s_py_ready"), sem2("s_rows_ready")
        rows_out = sem2("s_rows_out")
        block = ctx.enter_context(nc.Block())

        @block.sync
        def _(sp):
            sp.dma_start(w1[:], io["g_w1"]).then_inc(w_in, 16)
            with sp.Fori(0, G) as g:
                for h in range(2):
                    store_rows(sp, c.t1, g, h, rows, rows_ready, rows_out)
            for h in range(2):
                sp.wait_ge(rows_out[h], 16)

        @block.vector
        def _(dve):
            dve.sem_inc(rows_out[0], 16)
            dve.sem_inc(rows_out[1], 16)

            def copy_rows():
                for h in range(2):
                    take(dve, py_ready[h])
                    take(dve, rows_out[h], 16)
                    link(dve, nc.vector.tensor_copy(rows[h][:], ps_y[h][:]), own)
                    dve.sem_inc(py_free[h], 1)
                    dve.sem_inc(rows_ready[h], 1)

            for h in range(2):
                dve.sem_inc(py_free[h], 1)
                normalise(dve, nc, c, xn[h], 0, h, xn_ready[h])
            with dve.Fori(0, G - 1) as g:
                for h in range(2):
                    take(dve, xn_free[h])
                    normalise(dve, nc, c, xn[h], g + 1, h, xn_ready[h])
                copy_rows()
            copy_rows()

        @block.scalar
        def _(act):
            with act.Fori(0, G) as g:
                for h in range(2):
                    take(act, pt_ready[h])
                    act.sem_inc(xn_free[h], 1)
                    act.copy(xt[h][:], ps_t[h][:]).then_inc(xt_ready[h], 1)

        @block.tensor
        def _(pe):
            pe.wait_ge(w_in, 16)
            with pe.Fori(0, G) as g:
                for h in range(2):
                    take(pe, xn_ready[h])
                    transpose_half(nc, c, ps_t[h], xn[h]).then_inc(pt_ready[h], 1)
                for h in range(2):
                    take(pe, xt_ready[h])
                    take(pe, py_free[h])
                    for s in range(2):
                        for k in range(KD):
                            last = pe.matmul(ps_y[h][:, s, :], xt[h][:, k, s * P:(s + 1) * P], w1[:, k, :],
                                             start=k == 0, stop=k == KD - 1)
                    last.then_inc(py_ready[h], 1)


def stage_conv(nc, c, part, table):
    io, name = c.io, f"conv{part}"
    with ExitStack() as ctx:
        sb = lambda n, shape, dt=FP32: ctx.enter_context(nc.sbuf_tensor(f"{name}_{n}", shape, dt))
        pb = lambda n, shape: ctx.enter_context(nc.psum_tensor(f"{name}_{n}", shape, FP32))
        sem = ctx.enter_context(Signals(nc, name + "_"))
        idx = sb("idx", [P, 2, HALF_COLS], I32)
        rel = sb("rel", [P, C])
        window = sb("window", [1, EG], I32)
        gath = [sb(f"gath{s}", [P, CG, HID]) for s in range(SLOTS)]
        hot = [sb(f"hot{half}", [P, HALF_COLS, W]) for half in range(2)]
        we = sb("we", [P, KD, D])
        bias, parts, ones = bias_buffers(sb)
        ln2 = sb("ln2", [P, 1])
        edge = [sb(f"edge{r}", [P, KD, CG * P]) for r in range(MISH)]
        q = [sb(f"q{r}", [P, CG, D]) for r in range(MISH)]
        neg = [sb(f"neg{r}", [P, CG, D]) for r in range(MISH)]
        ps = [pb(f"ps{n}", [P, W]) for n in range(2)]
        ps_z = [pb(f"pz{r}", [P, CG, D]) for r in range(MISH)]
        if part == 0:
            zeros, filled = sb("zeros", [P, SLOT // P, D]), sem("filled")
        sums = c.feat[:, 0, :]
        gathered = [nc.alloc_semaphore(f"{name}_gathered{s}") for s in range(SLOTS)]
        hot_ready = [sem(f"hot_ready{half}") for half in range(2)]
        ps_ready = [sem(f"ps_ready{n}") for n in range(2)]
        ps_free = [sem(f"ps_free{n}") for n in range(2)]
        idx_ready = [sem(f"idx_ready{half}") for half in range(2)]
        own, act_own, neg_own = sem("own"), sem("act_own"), sem("neg_own")
        w_in, parts_ready = sem("w_in"), sem("parts_ready")
        per_r = lambda n: [sem(f"{n}{r}") for r in range(MISH)]
        edge_in, edge_free, z_done, z_free = per_r("edge_in"), per_r("edge_free"), per_r("z_done"), per_r("z_free")
        z_ready, q_ready, neg_ready, neg_out = per_r("z_ready"), per_r("q_ready"), per_r("neg_ready"), per_r("neg_out")
        block = ctx.enter_context(nc.Block())

        def load_passes(eng):
            return eng.value_load(c.passes[0:1, 0:1], min_val=1, max_val=TW // W)

        @block.sync
        def _(sp):
            group = lambda i, r: bass.ds(i * MISH + (part * IT * MISH + r), 1)

            def load(i, r):
                take(sp, edge_free[r])
                sp.dma_start(edge[r][:], io["edge_t"][group(i, r)].rearrange("a p k e -> p (a k) e")).then_inc(edge_in[r], 16)

            def store(i, r):
                take(sp, neg_ready[r])
                sp.dma_start(c.mish_d[group(i, r)].rearrange("a p j d -> p (a j) d"), neg[r][:]).then_inc(neg_out[r], 16)

            sp.dma_start(we[:], io["l_we"]).then_inc(w_in, 16)
            sp.dma_start(bias[0][:], io["l_be"]).then_inc(w_in, 16)
            for r in range(MISH):
                sp.sem_inc(edge_free[r], 1)
            with sp.Fori(0, load_passes(sp)) as k:
                for r in range(MISH):
                    load(0, r)
                with sp.Fori(0, IT - 1) as i:
                    for r in range(MISH):
                        load(i + 1, r)
                        store(i, r)
                for r in range(MISH):
                    store(IT - 1, r)
            for r in range(MISH):
                sp.wait_ge(neg_out[r], 16)

        @block.gpsimd
        def _(pool):
            with pool.Fori(0, load_passes(pool)) as k:
                with pool.Fori(0, IT) as i:
                    for half in range(2):
                        take(pool, idx_ready[half])
                        for s in range(half * 3, half * 3 + 3):
                            for j in range(CG):
                                col = (s - half * 3) * CG + j
                                pool.indirect_dma_start(
                                    gath[s][:, j, :], None, table[:, :],
                                    bass.IndirectOffsetOnAxis(ap=idx[:, half, col:col + 1], axis=0),
                                ).then_inc(gathered[s], 16)

        @block.vector
        def _(dve):
            def mish_begin(r):
                take(dve, z_done[r])
                dve.sem_inc(edge_free[r], 1)
                nc.vector.tensor_scalar(q[r][:], ps_z[r][:], ZMAX, None, ALU.min).then_inc(z_ready[r], 1)

            def mish_end(r):
                take(dve, q_ready[r])
                take(dve, neg_out[r], 16)
                link(dve, nc.vector.scalar_tensor_tensor(neg[r][:], q[r][:], -1.0, ps_z[r][:], ALU.add, ALU.mult), neg_own)
                dve.sem_inc(z_free[r], 1)
                dve.sem_inc(neg_ready[r], 1)

            def add(i, s):
                at = dve.value_load(window[0:1, bass.ds(i * SLOTS + s, 1)], min_val=0, max_val=NP)
                take(dve, ps_ready[s % 2])
                here = sums[:, bass.ds(at, W)]
                link(dve, nc.vector.tensor_tensor(here, here, ps[s % 2][:], ALU.add), own)
                dve.sem_inc(ps_free[s % 2], 1)

            def indices(i, half):
                nc.vector.tensor_copy(idx[:, half, :], c.src[:, bass.ds(i * (SLOTS * CG) + half * HALF_COLS, HALF_COLS)]
                                      ).then_inc(idx_ready[half], 1)

            def one_hots(i, half):
                part_of = lambda a: a[:, bass.ds(i * (SLOTS * CG) + half * HALF_COLS, HALF_COLS)].unsqueeze(2).to_broadcast([P, HALF_COLS, W])
                link(dve, nc.vector.tensor_tensor(hot[half][:], c.iota[:].unsqueeze(1).to_broadcast([P, HALF_COLS, W]), part_of(rel), ALU.is_equal), own)
                nc.vector.tensor_tensor(hot[half][:], hot[half][:], part_of(c.weight), ALU.mult).then_inc(hot_ready[half], 1)

            def step(i, first, final):
                for r in range(MISH):
                    for s in BEFORE[r]:
                        add(i, s)
                        if s % 3 == 2 and not final:
                            indices(i + 1, s // 3)
                    mish_begin(r)
                    if r and not final:
                        one_hots(i + 1, r - 1)
                    if r or not first:
                        mish_end((r - 1) % MISH)

            for n in range(2):
                dve.sem_inc(ps_free[n], 1)
            for r in range(MISH):
                dve.sem_inc(z_free[r], 1)
                dve.sem_inc(neg_out[r], 16)
            nc.vector.memset(ln2[:], LN2)
            nc.vector.memset(ones[:], 1.0)
            nc.vector.memset(sums, 0.0)
            if part == 0:
                nc.vector.memset(zeros[:], 0.0)
            nc.vector.tensor_copy(rel[:], c.dstrel[:])
            link(dve, nc.vector.tensor_copy(window[:], c.base[:]), own)
            dve.wait_ge(w_in, 32)
            split_bias(dve, nc, c, bias, parts, own)
            dve.sem_inc(parts_ready, 2)
            with dve.Fori(0, load_passes(dve)) as k:
                for half in range(2):
                    indices(0, half)
                    one_hots(0, half)
                step(0, True, False)
                with dve.Fori(1, IT - 1) as i:
                    step(i, False, False)
                step(IT - 1, False, True)
                mish_end(MISH - 1)
                nc.vector.tensor_scalar(rel[:], rel[:], -float(W), None, ALU.add)
                link(dve, nc.vector.tensor_scalar(window[:], window[:], float(W), float(NP), ALU.add, ALU.min), own)

        @block.scalar
        def _(act):
            act.wait_ge(parts_ready, 1)
            log_exp_table(act)
            if part == 0:
                act.sem_inc(filled, 32)
            with act.Fori(0, load_passes(act)) as k:
                with act.Fori(0, IT) as i:
                    if part == 0:
                        take(act, filled, 32)
                        for table_d in (c.rows_d, c.outs_d):
                            act.dma_start(table_d[bass.ds(i * SLOT, SLOT), :].rearrange("(t p) d -> p t d", p=P), zeros[:]
                                          ).then_inc(filled, 16)
                    for r in range(MISH):
                        take(act, z_ready[r])
                        mish_factor(act, q[r][:], ln2, act_own, q_ready[r])
            if part == 0:
                act.wait_ge(filled, 32)

        @block.tensor
        def _(pe):
            def segment(k, i, s):
                half, at = s // 3, s % 3 * CG
                if at == 0:
                    take(pe, hot_ready[half])
                take(pe, ps_free[s % 2])
                pe.wait_ge(gathered[s], k * (IT * CG * 16) + i * (CG * 16) + CG * 16)
                for j in range(CG):
                    last = pe.matmul(ps[s % 2][:], gath[s][:, j, :], hot[half][:, at + j, :], start=j == 0, stop=j == CG - 1)
                last.then_inc(ps_ready[s % 2], 1)

            def product(r):
                take(pe, edge_in[r], 16)
                take(pe, z_free[r])
                for j in range(CG):
                    for m in range(KD):
                        pe.matmul(ps_z[r][:, j, :], edge[r][:, m, j * P:(j + 1) * P], we[:, m, :], start=m == 0, stop=False)
                    last = pe.matmul(ps_z[r][:, j, :], ones[:], parts[:], start=False, stop=True)
                last.then_inc(z_done[r], 1)

            pe.wait_ge(parts_ready, 1)
            with pe.Fori(0, load_passes(pe)) as k:
                with pe.Fori(0, IT) as i:
                    for r in range(MISH):
                        for s in BEFORE[r]:
                            segment(k, i, s)
                        product(r)


def stage_hidden(nc, c):
    io = c.io
    with ExitStack() as ctx:
        sb = lambda name, shape, dt=FP32: ctx.enter_context(nc.sbuf_tensor(name, shape, dt))
        sem = ctx.enter_context(Signals(nc))
        sem2 = lambda name: [sem(f"{name}{h}") for h in range(2)]
        b1 = sb("gb1", [P, 1])
        hid = [sb(f"h_hid{h}", [P, 2 * P]) for h in range(2)]
        rows = [sb(f"h_rows{h}", [P, 2, HID]) for h in range(2)]
        ps = [ctx.enter_context(nc.psum_tensor(f"h_ps{h}", [P, 2, HID], FP32)) for h in range(2)]
        b_in, own = sem("h_b_in"), sem("h_own")
        hid_ready, ps_ready, ps_free = sem2("h_hid_ready"), sem2("h_ps_ready"), sem2("h_ps_free")
        rows_ready, rows_out = sem2("h_rows_ready"), sem2("h_rows_out")
        block = ctx.enter_context(nc.Block())

        @block.sync
        def _(sp):
            sp.dma_start(b1[:], io["g_b1"]).then_inc(b_in, 16)
            with sp.Fori(0, G) as g:
                for h in range(2):
                    store_rows(sp, c.t2, g, h, rows, rows_ready, rows_out)
            for h in range(2):
                sp.wait_ge(rows_out[h], 16)

        @block.scalar
        def _(act):
            act.wait_ge(b_in, 16)
            act.sem_inc(ps_free[0], 1)
            act.sem_inc(ps_free[1], 1)
            with act.Fori(0, G) as g:
                for h in range(2):
                    take(act, ps_free[h])
                    act.activation(hid[h][:], tokens(c.feat[:, 0, :], g, h), ACT.Relu, bias=b1[:]).then_inc(hid_ready[h], 1)

        @block.tensor
        def _(pe):
            with pe.Fori(0, G) as g:
                for h in range(2):
                    take(pe, hid_ready[h])
                    for s in range(2):
                        last = pe.transpose(ps[h][:, s, :], hid[h][:, s * P:(s + 1) * P], c.ident[:])
                    last.then_inc(ps_ready[h], 1)

        @block.vector
        def _(dve):
            dve.sem_inc(rows_out[0], 16)
            dve.sem_inc(rows_out[1], 16)
            with dve.Fori(0, G) as g:
                for h in range(2):
                    take(dve, ps_ready[h])
                    take(dve, rows_out[h], 16)
                    link(dve, nc.vector.tensor_copy(rows[h][:], ps[h][:]), own)
                    dve.sem_inc(rows_ready[h], 1)
                    dve.sem_inc(ps_free[h], 1)


def stage_convolved(nc, c):
    io = c.io
    with ExitStack() as ctx:
        sb = lambda name, shape, dt=FP32: ctx.enter_context(nc.sbuf_tensor(name, shape, dt))
        sem = ctx.enter_context(Signals(nc))
        sem2 = lambda name: [sem(f"{name}{h}") for h in range(2)]
        w2, b2 = sb("gw2", [P, D]), sb("gb2", [P, D])
        sums = [sb(f"c_sums{h}", [P, 2 * P]) for h in range(2)]
        ps = [ctx.enter_context(nc.psum_tensor(f"c_ps{h}", [P, 2, D], FP32)) for h in range(2)]
        w_in = sem("c_w_in")
        own = sem("c_own")
        moments = Moments(nc, c, lambda n, shape: sb("c_" + n, shape), sem)
        sums_ready, ps_ready, ps_free = sem2("c_sums_ready"), sem2("c_ps_ready"), sem2("c_ps_free")
        block = ctx.enter_context(nc.Block())

        @block.sync
        def _(sp):
            sp.dma_start(w2[:], io["g_w2"]).then_inc(w_in, 16)
            sp.dma_start(b2[:], io["g_b2"]).then_inc(w_in, 16)

        @block.scalar
        def _(act):
            act.sem_inc(ps_free[0], 1)
            act.sem_inc(ps_free[1], 1)
            with act.Fori(0, G) as g:
                for h in range(2):
                    take(act, ps_free[h])
                    act.copy(sums[h][:], tokens(c.feat[:, 0, :], g, h)).then_inc(sums_ready[h], 1)

        @block.tensor
        def _(pe):
            pe.wait_ge(w_in, 32)
            with pe.Fori(0, G) as g:
                for h in range(2):
                    take(pe, sums_ready[h])
                    for s in range(2):
                        last = pe.matmul(ps[h][:, s, :], sums[h][:, s * P:(s + 1) * P], w2[:], start=True, stop=True)
                    last.then_inc(ps_ready[h], 1)

        @block.vector
        def _(dve):
            dve.wait_ge(w_in, 32)
            with dve.Fori(0, G) as g:
                for h in range(2):
                    x = c.x[:, bass.ds(g * TG + 2 * h, 2), :]
                    link(dve, nc.vector.tensor_tensor(x, x, b2[:].unsqueeze(1).to_broadcast([P, 2, D]), ALU.add), own)
                    take(dve, ps_ready[h])
                    link(dve, nc.vector.tensor_tensor(x, x, ps[h][:], ALU.add), own)
                    dve.sem_inc(ps_free[h], 1)
                moments.of(dve, g)


def stage_route(nc, c, mix):
    io, name = c.io, f"r{mix}"
    experts = (E0, E1)[mix]
    with ExitStack() as ctx:
        sb = lambda n, shape, dt=FP32: ctx.enter_context(nc.sbuf_tensor(f"{name}_{n}", shape, dt))
        pb = lambda n, shape: ctx.enter_context(nc.psum_tensor(f"{name}_{n}", shape, FP32))
        sem = ctx.enter_context(Signals(nc, name + "_"))
        sem2 = lambda n: [sem(f"{n}{h}") for h in range(2)]
        if mix == 0:
            w1, b1 = sb("w1", [P, KD, P]), sb("b1", [P, 1])
            hid = [sb(f"hid{h}", [P, 2 * P]) for h in range(2)]
            w2 = sb("w2", [P, E0])
        else:
            gamma, beta, w2 = sb("gamma", [P, KD]), sb("beta", [P, KD]), sb("w2", [P, KD, E1])
        xt = [[sb(f"xt{n}{h}", [P, KD, 2 * P]) for h in range(2)] for n in range(2)]
        b2 = sb("b2", [P, experts])
        iota8, real, before, ones = sb("iota8", [P, 8]), sb("real", [P, NT]), sb("before", [P, P]), sb("ones", [P, P])
        xn = [sb(f"xn{h}", [P, 2, D]) for h in range(2)]
        logit = sb("logit", [P, T, 8])
        top = sb("top", [P, T])
        total = sb("total", [P, T])
        best = sb("best", [P, NT, 8])
        best_at = sb("best_at", [P, NT, 8], U32)
        at = sb("at", [P, NT, 2])
        gap, share = sb("gap", [P, NT]), sb("share", [P, NT])
        is_nth = [sb(f"is_nth{n}", [P, NT, 8]) for n in range(2)]
        chosen = sb("chosen", [P, NT, 8])
        upto = [sb(f"upto{n}", [P, NT, 8]) for n in range(2)]
        place, picked, row = sb("place", [P, NT, 8]), sb("picked", [P, NT, 8]), sb("row", [P, NT])
        filled, filled_i, slots_i = sb("filled", [P, 8]), sb("filled_i", [P, 8], I32), sb("slots_i", [P, 8], I32)
        slots_f, start_f = sb("slots_f", [P, 8]), sb("start_f", [P, 8])
        slots_upto = [sb(f"slots_upto{n}", [P, 8]) for n in range(2)]
        ps_rank, ps_all = pb("rank", [P, 64, 8]), pb("all", [P, 64, 8])
        ps_t = [pb(f"pt{h}", [P, KD, 2 * P]) for h in range(2)]
        ps_h = [pb(f"ph{h}", [P, 2 * P]) for h in range(2)]
        ps_l = [pb(f"pl{h}", [P, 2, 8]) for h in range(2)]
        w_in, own = sem("w_in"), sem("own")
        xn_ready, pt_ready, xt_ready = sem2("xn_ready"), sem2("pt_ready"), sem2("xt_ready")
        xn_free, pl_free = sem2("xn_free"), sem2("pl_free")
        ph_ready, hid_ready, pl_ready = sem2("ph_ready"), sem2("hid_ready"), sem2("pl_ready")
        shifted_ready, exp_ready, gap_ready, gap_exp = sem("shifted_ready"), sem("exp_ready"), sem("gap_ready"), sem("gap_exp")
        chosen_ready, rank_ready = sem("chosen_ready"), sem("rank_ready")
        block = ctx.enter_context(nc.Block())
        loads = ([(w1, "r0_w1"), (b1, "r0_b1"), (w2, "r0_w2"), (b2, "r0_b2")] if mix == 0 else
                 [(gamma, "r1_gamma"), (beta, "r1_beta"), (w2, "r1_w2"), (b2, "r1_b2")])
        loads += [(iota8, "iota8"), (real, "real"), (before, "before")]

        @block.sync
        def _(sp):
            for tile, key in loads:
                sp.dma_start(tile[:], io[key]).then_inc(w_in, 16)

        @block.vector
        def _(dve):
            def running_sum(bufs, size, cut):
                now, step = 0, 1
                while step < size:
                    a, b = bufs[now], bufs[1 - now]
                    nc.vector.tensor_copy(cut(b, 0, step), cut(a, 0, step))
                    link(dve, nc.vector.tensor_tensor(cut(b, step, size), cut(a, step, size), cut(a, 0, size - step), ALU.add), own)
                    now, step = 1 - now, 2 * step
                return bufs[now]

            nc.vector.memset(logit[:], -1e30)
            nc.vector.memset(ones[:], 1.0)
            dve.wait_ge(w_in, 16 * len(loads))

            def logits(g):
                for h in range(2):
                    take(dve, pl_ready[h])
                    link(dve, nc.vector.tensor_tensor(logit[:, bass.ds(g * TG + 2 * h, 2), 0:experts], ps_l[h][:, :, 0:experts],
                                                      b2[:].unsqueeze(1).to_broadcast([P, 2, experts]), ALU.add), own)
                    dve.sem_inc(pl_free[h], 1)

            for h in range(2):
                dve.sem_inc(pl_free[h], 1)
                normalise(dve, nc, c, xn[h], 0, h, xn_ready[h])
            with dve.Fori(0, G - 1) as g:
                for h in range(2):
                    take(dve, xn_free[h])
                    normalise(dve, nc, c, xn[h], g + 1, h, xn_ready[h])
                logits(g)
            logits(G - 1)
            if mix == 0:
                some = logit[:, :, 0:experts]
                wide = lambda ap: ap.unsqueeze(2).to_broadcast([P, T, experts])
                link(dve, nc.vector.tensor_reduce(top[:], some, AX.X, ALU.max), own)
                nc.vector.tensor_tensor(some, some, wide(top[:]), ALU.subtract).then_inc(shifted_ready, 1)
                take(dve, exp_ready)
                link(dve, nc.vector.tensor_reduce(total[:], some, AX.X, ALU.add), own)
                link(dve, nc.vector.reciprocal(total[:], total[:]), own)
                link(dve, nc.vector.tensor_tensor(some, some, wide(total[:]), ALU.mult), own)
            for t in range(NT):
                last = nc.vector.max(best[:, t, :], logit[:, t, :])
            link(dve, last, own)
            nc.vector.tensor_tensor(gap[:], best[:, :, 1], best[:, :, 0], ALU.subtract).then_inc(gap_ready, 1)
            for t in range(NT):
                last = nc.vector.max_index(best_at[:, t, :], best[:, t, :], logit[:, t, :])
            link(dve, last, own)
            link(dve, nc.vector.tensor_copy(at[:], best_at[:, :, 0:2]), own)
            every = iota8[:].unsqueeze(1).to_broadcast([P, NT, 8])
            over = lambda ap: ap.unsqueeze(2).to_broadcast([P, NT, 8])
            for n in range(2):
                link(dve, nc.vector.tensor_tensor(is_nth[n][:], every, over(at[:, :, n]), ALU.is_equal), own)
            link(dve, nc.vector.tensor_tensor(chosen[:], is_nth[0][:], is_nth[1][:], ALU.add), own)
            nc.vector.tensor_tensor(chosen[:], chosen[:], over(real[:]), ALU.mult).then_inc(chosen_ready, 1)
            take(dve, gap_exp)
            link(dve, nc.vector.tensor_scalar_add(share[:], gap[:], 1.0), own)
            link(dve, nc.vector.reciprocal(share[:], share[:]), own)
            nc.vector.tensor_copy(c.gate[:, :, 0], share[:])
            nc.vector.tensor_tensor(c.gate[:, :, 1], gap[:], share[:], ALU.mult)
            take(dve, rank_ready)
            link(dve, nc.vector.tensor_copy(upto[0][:], ps_all[:, 0:NT, :]), own)
            upto_t = running_sum(upto, NT, lambda a, i, j: a[:, i:j, :])
            link(dve, nc.vector.tensor_scalar(filled[:], upto_t[:, NT - 1, :], 1.0, float(SLOT - 1), ALU.max, ALU.add), own)
            link(dve, nc.vector.tensor_copy(filled_i[:], filled[:]), own)
            link(dve, nc.vector.tensor_single_scalar(slots_i[:], filled_i[:], SLOT.bit_length() - 1, ALU.arith_shift_right), own)
            nc.vector.tensor_copy(c.slots[:], slots_i[0:1, :])
            nc.vector.tensor_copy(slots_f[:], slots_i[:])
            link(dve, nc.vector.tensor_copy(slots_upto[0][:], slots_i[:]), own)
            slots_e = running_sum(slots_upto, 8, lambda a, i, j: a[:, i:j])
            link(dve, nc.vector.tensor_tensor(start_f[:], slots_e[:], slots_f[:], ALU.subtract), own)
            link(dve, nc.vector.tensor_scalar(start_f[:], start_f[:], float(SLOT), None, ALU.mult), own)
            nc.vector.tensor_copy(c.start[:], start_f[0:1, :])
            link(dve, nc.vector.tensor_tensor(place[:], upto_t[:], ps_all[:, 0:NT, :], ALU.subtract), own)
            link(dve, nc.vector.tensor_tensor(place[:], place[:], ps_rank[:, 0:NT, :], ALU.add), own)
            link(dve, nc.vector.tensor_tensor(place[:], place[:], start_f[:].unsqueeze(1).to_broadcast([P, NT, 8]), ALU.add), own)
            for n in range(2):
                link(dve, nc.vector.tensor_tensor(picked[:], is_nth[n][:], place[:], ALU.mult), own)
                link(dve, nc.vector.tensor_reduce(row[:], picked[:], AX.X, ALU.add), own)
                nc.vector.tensor_copy(c.row[:, :, n], row[:])

        @block.scalar
        def _(act):
            def evacuate(n):
                for h in range(2):
                    take(act, pt_ready[h])
                    act.sem_inc(xn_free[h], 1)
                    if mix == 0:
                        last = act.copy(xt[n][h][:], ps_t[h][:])
                    else:
                        for k in range(KD):
                            last = act.activation(xt[n][h][:, k, :], ps_t[h][:, k, :], ACT.Identity,
                                                  scale=gamma[:, k:k + 1], bias=beta[:, k:k + 1])
                    last.then_inc(xt_ready[h], 1)

            def hidden():
                for h in range(2):
                    take(act, ph_ready[h])
                    act.activation(hid[h][:], ps_h[h][:], ACT.Relu, bias=b1[:]).then_inc(hid_ready[h], 1)

            act.wait_ge(w_in, 16 * len(loads))
            evacuate(0)
            with act.Fori(0, G // 2) as i:
                for n in (1, 0):
                    if mix == 0:
                        hidden()
                    evacuate(n)
            if mix == 0:
                hidden()
                take(act, shifted_ready)
                act.activation(logit[:, :, 0:experts], logit[:, :, 0:experts], ACT.Exp).then_inc(exp_ready, 1)
            take(act, gap_ready)
            act.activation(gap[:], gap[:], ACT.Exp).then_inc(gap_exp, 1)

        @block.tensor
        def _(pe):
            def turn():
                for h in range(2):
                    take(pe, xn_ready[h])
                    transpose_half(nc, c, ps_t[h], xn[h]).then_inc(pt_ready[h], 1)

            def step(n, final):
                for h in range(2):
                    take(pe, xt_ready[h])
                    if mix == 0:
                        for k in range(KD):
                            last = pe.matmul(ps_h[h][:], w1[:, k, :], xt[n][h][:, k, :], start=k == 0, stop=k == KD - 1)
                        last.then_inc(ph_ready[h], 1)
                if not final:
                    turn()
                for h in range(2):
                    if mix == 0:
                        take(pe, hid_ready[h])
                    take(pe, pl_free[h])
                    for s in range(2):
                        if mix == 0:
                            last = pe.matmul(ps_l[h][:, s, 0:E0], hid[h][:, s * P:(s + 1) * P], w2[:], start=True, stop=True)
                        else:
                            for k in range(KD):
                                last = pe.matmul(ps_l[h][:, s, 0:E1], xt[n][h][:, k, s * P:(s + 1) * P], w2[:, k, :],
                                                 start=k == 0, stop=k == KD - 1)
                    last.then_inc(pl_ready[h], 1)

            pe.wait_ge(w_in, 16 * len(loads))
            turn()
            with pe.Fori(0, G // 2) as i:
                for n in range(2):
                    step(n, False)
            step(0, True)
            take(pe, chosen_ready)
            flat = chosen[:].rearrange("p t e -> p (t e)")
            pe.matmul(ps_rank[:, 0:NT, :].rearrange("p t e -> p (t e)"), before[:], flat, start=True, stop=True)
            pe.matmul(ps_all[:, 0:NT, :].rearrange("p t e -> p (t e)"), ones[:], flat, start=True, stop=True).then_inc(rank_ready, 1)


def stage_scatter(nc, c, mix):
    name = f"sc{mix}"
    steps = WHOLE // (2 * SG)
    with ExitStack() as ctx:
        sb = lambda n, shape, dt=FP32: ctx.enter_context(nc.sbuf_tensor(f"{name}_{n}", shape, dt))
        sem = ctx.enter_context(Signals(nc, name + "_"))
        xn = [sb(f"xn{r}", [P, SG, D]) for r in range(2)]
        idx = [sb(f"idx{r}", [P, SG, 2], I32) for r in range(2)]
        xn_ready, idx_ready = [sem(f"xn_ready{r}") for r in range(2)], sem("idx_ready")
        scattered = [nc.alloc_semaphore(f"{name}_scattered{r}") for r in range(2)]
        block = ctx.enter_context(nc.Block())
        per_step = SG * 2 * 16
        last_rows = N - WHOLE * P

        @block.vector
        def _(dve):
            def rows(i, r):
                for s in range(SG):
                    tile = bass.ds(i * (2 * SG) + r * SG + s, 1)
                    last = nc.vector.tensor_scalar(xn[r][:, s, :], c.x[:, tile, :].rearrange("p a d -> p (a d)"),
                                                   c.mv[:, tile, 0], c.rstd[:, tile], ALU.subtract, ALU.mult)
                last.then_inc(xn_ready[r], 1)

            for r in range(2):
                rows(0, r)
            with dve.Fori(1, steps) as i:
                for r in range(2):
                    dve.wait_ge(scattered[r], i * per_step)
                    rows(i, r)
            dve.wait_ge(scattered[0], steps * per_step)
            nc.vector.tensor_scalar(xn[0][:, 0, :], c.x[:, WHOLE, :], c.mv[:, WHOLE, 0:1], c.rstd[:, WHOLE:WHOLE + 1],
                                    ALU.subtract, ALU.mult).then_inc(xn_ready[0], 1)
            dve.wait_ge(scattered[1], steps * per_step)
            dve.wait_ge(scattered[0], steps * per_step + 32)

        @block.gpsimd
        def _(pool):
            def scatter(r, s, rows):
                for n in range(2):
                    pool.indirect_dma_start(
                        c.rows_d[:, :], bass.IndirectOffsetOnAxis(ap=idx[r][0:rows, s, n:n + 1], axis=0),
                        xn[r][0:rows, s, :], None,
                    ).then_inc(scattered[r], 16)

            with pool.Fori(0, steps) as i:
                for r in range(2):
                    take(pool, xn_ready[r])
                    nc.gpsimd.tensor_copy(idx[r][:], c.row[:, bass.ds(i * (2 * SG) + r * SG, SG), :]).then_inc(idx_ready, 1)
                    take(pool, idx_ready)
                    for s in range(SG):
                        scatter(r, s, P)
            take(pool, xn_ready[0])
            nc.gpsimd.tensor_copy(idx[0][:, 0, :], c.row[:, WHOLE, :]).then_inc(idx_ready, 1)
            take(pool, idx_ready)
            scatter(0, 0, last_rows)


def stage_combine(nc, c, mix):
    name = f"cb{mix}"
    steps = WHOLE // (2 * SG)
    with ExitStack() as ctx:
        sb = lambda n, shape, dt=FP32: ctx.enter_context(nc.sbuf_tensor(f"{name}_{n}", shape, dt))
        sem = ctx.enter_context(Signals(nc, name + "_"))
        outs = [sb(f"outs{r}", [P, SG, 2, D]) for r in range(2)]
        idx = [sb(f"idx{r}", [P, SG, 2], I32) for r in range(2)]
        moments = Moments(nc, c, sb, sem) if mix == 0 else None
        outs_free, idx_ready, own = [sem(f"outs_free{r}") for r in range(2)], sem("idx_ready"), sem("own")
        gathered = [nc.alloc_semaphore(f"{name}_gathered{r}") for r in range(2)]
        block = ctx.enter_context(nc.Block())
        per_step = SG * 2 * 16
        last_rows = N - WHOLE * P

        @block.gpsimd
        def _(pool):
            def gather(r, s, rows):
                for n in range(2):
                    pool.indirect_dma_start(
                        outs[r][0:rows, s, n, :], None, c.outs_d[:, :],
                        bass.IndirectOffsetOnAxis(ap=idx[r][0:rows, s, n:n + 1], axis=0),
                    ).then_inc(gathered[r], 16)

            for r in range(2):
                pool.sem_inc(outs_free[r], 1)
            with pool.Fori(0, steps) as i:
                for r in range(2):
                    take(pool, outs_free[r])
                    nc.gpsimd.tensor_copy(idx[r][:], c.row[:, bass.ds(i * (2 * SG) + r * SG, SG), :]).then_inc(idx_ready, 1)
                    take(pool, idx_ready)
                    for s in range(SG):
                        gather(r, s, P)
            take(pool, outs_free[0])
            nc.gpsimd.tensor_copy(idx[0][:, 0, :], c.row[:, WHOLE, :]).then_inc(idx_ready, 1)
            take(pool, idx_ready)
            gather(0, 0, last_rows)

        @block.vector
        def _(dve):
            with dve.Fori(0, steps) as i:
                for r in range(2):
                    dve.wait_ge(gathered[r], i * per_step + per_step)
                    for n in range(2):
                        for s in range(SG):
                            tile = bass.ds(i * (2 * SG) + r * SG + s, 1)
                            x = c.x[:, tile, :].rearrange("p a d -> p (a d)")
                            last = nc.vector.scalar_tensor_tensor(x, outs[r][:, s, n, :], c.gate[:, tile, n], x, ALU.mult, ALU.add)
                        link(dve, last, own)
                    dve.sem_inc(outs_free[r], 1)
                    if mix == 0:
                        moments.of(dve, i * 2 + r)
            dve.wait_ge(gathered[0], steps * per_step + 32)
            x = c.x[0:last_rows, WHOLE, :]
            for n in range(2):
                link(dve, nc.vector.scalar_tensor_tensor(x, outs[0][0:last_rows, 0, n, :], c.gate[0:last_rows, WHOLE, n:n + 1], x,
                                                         ALU.mult, ALU.add), own)
            if mix == 0:
                moments.of(dve, G - 1)


def stage_experts(nc, c, mix):
    io, name = c.io, f"e{mix}"
    experts = (E0, E1)[mix]
    hm = (KD, HM)[mix]
    with ExitStack() as ctx:
        sb = lambda n, shape, dt=FP32: ctx.enter_context(nc.sbuf_tensor(f"{name}_{n}", shape, dt))
        pb = lambda n, shape: ctx.enter_context(nc.psum_tensor(f"{name}_{n}", shape, FP32))
        sem = ctx.enter_context(Signals(nc, name + "_"))
        sem2 = lambda n: [sem(f"{n}{h}") for h in range(2)]
        w_first = [sb(f"w_first{e}", [P, KD, hm * P]) for e in range(experts)]
        w_last = [sb(f"w_last{e}", [P, hm, D]) for e in range(experts)]
        b_first, b_last = sb("b_first", [P, experts, hm]), sb("b_last", [P, experts, D])
        if mix == 0:
            w_mid, b_mid = [sb(f"w_mid{e}", [P, KD, D]) for e in range(E0)], sb("b_mid", [P, E0, KD])
            mid = [sb(f"mid{h}", [P, KD, HALF]) for h in range(2)]
            ps_m = [pb(f"pm{h}", [P, KD, HALF]) for h in range(2)]
        else:
            gamma, beta = sb("gamma", [P, KD]), sb("beta", [P, KD])
        rows = [sb(f"rows{h}", [P, 2, D]) for h in range(2)]
        xt = [sb(f"xt{h}", [P, KD, HALF]) for h in range(2)]
        hid = [sb(f"hid{h}", [P, hm, HALF]) for h in range(2)]
        outs = [sb(f"outs{h}", [P, 2, D]) for h in range(2)]
        ps_t = [pb(f"pt{h}", [P, KD, HALF]) for h in range(2)]
        ps_h = [pb(f"ph{h}", [P, hm, HALF]) for h in range(2)]
        ps_y = [pb(f"py{h}", [P, 2, D]) for h in range(2)]
        b_in = sem("b_in")
        w_in = [sem(f"w_in{e}") for e in range(experts)]
        rows_in, rows_free, pt_ready, xt_ready = sem2("rows_in"), sem2("rows_free"), sem2("pt_ready"), sem2("xt_ready")
        ph_ready, hid_ready, pm_ready, mid_ready = sem2("ph_ready"), sem2("hid_ready"), sem2("pm_ready"), sem2("mid_ready")
        py_ready, outs_ready, outs_out = sem2("py_ready"), sem2("outs_ready"), sem2("outs_out")
        block = ctx.enter_context(nc.Block())
        small = [(b_first, f"m{mix}_b1"), (b_last, f"m{mix}_blast")]
        small += [(b_mid, "m0_b2")] if mix == 0 else [(gamma, "r1_gamma"), (beta, "r1_beta")]
        layers = [(w_first, "m0_w1"), (w_mid, "m0_w2"), (w_last, "m0_w3")] if mix == 0 else [(w_first, "m1_w1"), (w_last, "m1_w2")]

        def slots(eng, e):
            return eng.value_load(c.slots[0:1, e:e + 1], min_val=1, max_val=-(-N // SLOT))

        def half_rows(table, start, j, h):
            at = nc.s_assert_within(start + j * SLOT, 0, ROWS - SLOT, skip_runtime_bounds_check_because="the slots of all experts fit in ROWS")
            return table[bass.ds(at + h * HALF, HALF), :].rearrange("(s p) d -> p s d", p=P)

        @block.gpsimd
        def _(pool):
            for e in range(experts):
                for w, key in layers:
                    pool.dma_start(w[e][:], io[key][e]).then_inc(w_in[e], 16)

        @block.sync
        def _(sp):
            for tile, key in small:
                sp.dma_start(tile[:], io[key]).then_inc(b_in, 16)
            for h in range(2):
                sp.sem_inc(rows_free[h], 1)
            for e in range(experts):
                start = sp.value_load(c.start[0:1, e:e + 1], min_val=0, max_val=ROWS - SLOT)
                with sp.Fori(0, slots(sp, e)) as j:
                    for h in range(2):
                        take(sp, rows_free[h])
                        sp.dma_start(rows[h][:], half_rows(c.rows_d, start, j, h)).then_inc(rows_in[h], 16)

        @block.tensor
        def _(pe):
            def layer(out, w, given, blocks):
                for m in range(blocks):
                    for k in range(KD):
                        last = pe.matmul(out[:, m, :], w[:, k, m * P:(m + 1) * P], given[:, k, :], start=k == 0, stop=k == KD - 1)
                return last

            for e in range(experts):
                pe.wait_ge(w_in[e], 16 * len(layers))
                with pe.Fori(0, slots(pe, e)) as j:
                    for h in range(2):
                        take(pe, rows_in[h], 16)
                        transpose_half(nc, c, ps_t[h], rows[h]).then_inc(pt_ready[h], 1)
                    for h in range(2):
                        take(pe, xt_ready[h])
                        layer(ps_h[h], w_first[e], xt[h], hm).then_inc(ph_ready[h], 1)
                    if mix == 0:
                        for h in range(2):
                            take(pe, hid_ready[h])
                            layer(ps_m[h], w_mid[e], hid[h], KD).then_inc(pm_ready[h], 1)
                    given, ready = (mid, mid_ready) if mix == 0 else (hid, hid_ready)
                    for h in range(2):
                        take(pe, ready[h])
                        for s in range(2):
                            for k in range(hm):
                                last = pe.matmul(ps_y[h][:, s, :], given[h][:, k, s * P:(s + 1) * P], w_last[e][:, k, :],
                                                 start=k == 0, stop=k == hm - 1)
                        last.then_inc(py_ready[h], 1)

        @block.scalar
        def _(act):
            act.wait_ge(b_in, 16 * len(small))
            for e in range(experts):
                start = act.value_load(c.start[0:1, e:e + 1], min_val=0, max_val=ROWS - SLOT)
                with act.Fori(0, slots(act, e)) as j:
                    for h in range(2):
                        take(act, ph_ready[h])
                        for m in range(hm):
                            last = act.activation(hid[h][:, m, :], ps_h[h][:, m, :], (ACT.Relu, ACT.Gelu)[mix], bias=b_first[:, e, m:m + 1])
                        last.then_inc(hid_ready[h], 1)
                    for h in range(2):
                        take(act, outs_ready[h])
                        act.dma_start(half_rows(c.outs_d, start, j, h), outs[h][:]).then_inc(outs_out[h], 16)
            for h in range(2):
                act.wait_ge(outs_out[h], 16)

        @block.vector
        def _(dve):
            for h in range(2):
                dve.sem_inc(outs_out[h], 16)
            dve.wait_ge(b_in, 16 * len(small))
            for e in range(experts):
                with dve.Fori(0, slots(dve, e)) as j:
                    for h in range(2):
                        take(dve, pt_ready[h])
                        dve.sem_inc(rows_free[h], 1)
                        if mix == 0:
                            last = nc.vector.tensor_copy(xt[h][:], ps_t[h][:])
                        else:
                            for k in range(KD):
                                last = nc.vector.tensor_scalar(xt[h][:, k, :], ps_t[h][:, k, :], gamma[:, k:k + 1], beta[:, k:k + 1],
                                                               ALU.mult, ALU.add)
                        last.then_inc(xt_ready[h], 1)
                    if mix == 0:
                        for h in range(2):
                            take(dve, pm_ready[h])
                            for m in range(KD):
                                last = nc.vector.tensor_scalar(mid[h][:, m, :], ps_m[h][:, m, :], b_mid[:, e, m:m + 1], 0.0,
                                                               ALU.add, ALU.max)
                            last.then_inc(mid_ready[h], 1)
                    for h in range(2):
                        take(dve, py_ready[h])
                        take(dve, outs_out[h], 16)
                        nc.vector.tensor_tensor(outs[h][:], ps_y[h][:], b_last[:, e, :].unsqueeze(1).to_broadcast([P, 2, D]),
                                                ALU.add).then_inc(outs_ready[h], 1)


def split_bias(dve, nc, c, bias, parts, own):
    b, high, rest, total = bias
    link(dve, nc.vector.tensor_copy(high[:], b[:]), own)
    link(dve, nc.vector.tensor_scalar(total[:], high[:], c.ident[0:3, 0:1], None, ALU.mult), own)
    link(dve, nc.vector.tensor_tensor(rest[:], b[:], high[:], ALU.subtract), own)
    for row in (1, 2):
        link(dve, nc.vector.tensor_copy(high[:], rest[:]), own)
        link(dve, nc.vector.scalar_tensor_tensor(total[:], high[:], c.ident[0:3, row:row + 1], total[:], ALU.mult, ALU.add), own)
        link(dve, nc.vector.tensor_tensor(rest[:], rest[:], high[:], ALU.subtract), own)
    link(dve, nc.vector.tensor_copy(parts[:], total[:]), own)


def bias_buffers(sb):
    return ((sb("bias", [3, D]), sb("bias_high", [3, D], BF16), sb("bias_rest", [3, D]), sb("bias_total", [3, D])),
            sb("bias_parts", [3, D], BF16), sb("ones3", [3, P], BF16))


def mish_factor(act, q, ln2, own, ready):
    link(act, act.activation(q, q, ACT.Exp), own)
    link(act, act.activation(q, q, ACT.Square, bias=1.0), own)
    link(act, act.activation(q, q, ACT.Ln, bias=1.0), own)
    act.activation(q, q, ACT.Exp, scale=-1.0, bias=ln2[:]).then_inc(ready, 1)


def log_exp_table(act):
    act.preload_act_table_set("natural_log_exp_and_others")


def stage_node_mish(nc, c):
    io = c.io
    with ExitStack() as ctx:
        sb = lambda n, shape, dt=FP32: ctx.enter_context(nc.sbuf_tensor(f"n_{n}", shape, dt))
        pb = lambda n, shape: ctx.enter_context(nc.psum_tensor(f"n_{n}", shape, FP32))
        sem = ctx.enter_context(Signals(nc, "n_"))
        sem2 = lambda n: [sem(f"{n}{h}") for h in range(2)]
        wd = sb("wd", [P, KD, D])
        bias, parts, ones = bias_buffers(sb)
        ln2 = sb("ln2", [P, 1])
        xn = [sb(f"xn{h}", [P, 2, D]) for h in range(2)]
        xt = [sb(f"xt{h}", [P, KD, 2 * P]) for h in range(2)]
        q = [sb(f"q{h}", [P, 2, D]) for h in range(2)]
        rows = [sb(f"rows{h}", [P, 2, D]) for h in range(2)]
        ps_t = [pb(f"pt{h}", [P, KD, 2 * P]) for h in range(2)]
        ps_y = [pb(f"py{h}", [P, 2, D]) for h in range(2)]
        ps_u = [pb(f"pu{h}", [P, KD, 2 * P]) for h in range(2)]
        w_in, own, act_own, parts_ready = sem("w_in"), sem("own"), sem("act_own"), sem("parts_ready")
        xn_ready, pt_ready, xt_ready, py_ready = sem2("xn_ready"), sem2("pt_ready"), sem2("xt_ready"), sem2("py_ready")
        z_ready, q_ready, rows_ready, rows_pe = sem2("z_ready"), sem2("q_ready"), sem2("rows_ready"), sem2("rows_pe")
        pu_ready, rows_out, py_free = sem2("pu_ready"), sem2("rows_out"), sem2("py_free")
        block = ctx.enter_context(nc.Block())

        @block.sync
        def _(sp):
            sp.dma_start(wd[:], io["l_wd"]).then_inc(w_in, 16)
            sp.dma_start(bias[0][:], io["l_bd"]).then_inc(w_in, 16)
            with sp.Fori(0, G) as g:
                for h in range(2):
                    store_rows(sp, c.t3, g, h, rows, rows_ready, rows_out)
            for h in range(2):
                sp.wait_ge(rows_out[h], 16)

        @block.vector
        def _(dve):
            def finish(h):
                take(dve, q_ready[h])
                link(dve, nc.vector.tensor_scalar(q[h][:], q[h][:], -1.0, 1.0, ALU.mult, ALU.add), own)
                take(dve, rows_out[h], 16)
                link(dve, nc.vector.tensor_tensor(rows[h][:], q[h][:], ps_y[h][:], ALU.mult), own)
                dve.sem_inc(py_free[h], 1)
                dve.sem_inc(rows_ready[h], 1)
                dve.sem_inc(rows_pe[h], 1)

            def keep(g, h):
                take(dve, pu_ready[h])
                nc.vector.tensor_copy(tokens(c.feat[:, :, :], g, h), ps_u[h][:])

            def step(g, h, first, final):
                take(dve, py_ready[h])
                nc.vector.tensor_scalar(q[h][:], ps_y[h][:], ZMAX, None, ALU.min).then_inc(z_ready[h], 1)
                if not final:
                    normalise(dve, nc, c, xn[h], g + 1, h, xn_ready[h])
                if h or not first:
                    finish(1 - h)
                if not first:
                    keep(g - 1, h)

            for h in range(2):
                dve.sem_inc(rows_out[h], 16)
                dve.sem_inc(py_free[h], 1)
            nc.vector.memset(ln2[:], LN2)
            nc.vector.memset(ones[:], 1.0)
            dve.wait_ge(w_in, 32)
            split_bias(dve, nc, c, bias, parts, own)
            dve.sem_inc(parts_ready, 2)
            for h in range(2):
                normalise(dve, nc, c, xn[h], 0, h, xn_ready[h])
            for h in range(2):
                step(0, h, True, False)
            with dve.Fori(1, G - 1) as g:
                for h in range(2):
                    step(g, h, False, False)
            for h in range(2):
                step(G - 1, h, False, True)
            finish(1)
            keep(G - 1, 0)
            keep(G - 1, 1)

        @block.scalar
        def _(act):
            def evacuate(h):
                take(act, pt_ready[h])
                act.copy(xt[h][:], ps_t[h][:]).then_inc(xt_ready[h], 1)

            def step(h, final):
                if not (final and h):
                    evacuate(1 - h)
                take(act, z_ready[h])
                mish_factor(act, q[h][:], ln2, act_own, q_ready[h])

            act.wait_ge(parts_ready, 1)
            log_exp_table(act)
            evacuate(0)
            with act.Fori(0, G - 1) as g:
                for h in range(2):
                    step(h, False)
            for h in range(2):
                step(h, True)

        @block.tensor
        def _(pe):
            def turn(h):
                take(pe, xn_ready[h])
                transpose_half(nc, c, ps_t[h], xn[h]).then_inc(pt_ready[h], 1)

            def turn_back(h):
                take(pe, rows_pe[h])
                transpose_half(nc, c, ps_u[h], rows[h]).then_inc(pu_ready[h], 1)

            def step(h, first, final):
                if not (final and h):
                    turn(1 - h)
                take(pe, xt_ready[h])
                take(pe, py_free[h])
                for s in range(2):
                    for k in range(KD):
                        pe.matmul(ps_y[h][:, s, :], xt[h][:, k, s * P:(s + 1) * P], wd[:, k, :], start=k == 0, stop=False)
                    last = pe.matmul(ps_y[h][:, s, :], ones[:], parts[:], start=False, stop=True)
                last.then_inc(py_ready[h], 1)
                if not first:
                    turn_back(h)

            pe.wait_ge(parts_ready, 1)
            turn(0)
            for h in range(2):
                step(h, True, False)
            with pe.Fori(1, G - 1) as g:
                for h in range(2):
                    step(h, False, False)
            for h in range(2):
                step(h, False, True)
            turn_back(0)
            turn_back(1)


def stage_edges(nc, c):
    RING = 3
    with ExitStack() as ctx:
        sb = lambda n, shape, dt=FP32: ctx.enter_context(nc.sbuf_tensor(f"x_{n}", shape, dt))
        pb = lambda n, shape: ctx.enter_context(nc.psum_tensor(f"x_{n}", shape, FP32))
        sem = ctx.enter_context(Signals(nc, "x_"))
        idx = sb("idx", [P, 2, HALF_COLS], I32)
        rel = sb("rel", [P, C])
        window = sb("window", [1, EG], I32)
        neg = [sb(f"neg{n}", [P, CG, D]) for n in range(RING)]
        node = [sb(f"node{s}", [P, CG, D]) for s in range(SLOTS)]
        hot = [sb(f"hot{n}", [P, CG, W]) for n in range(RING)]
        ps_a = [pb(f"pa{n}", [P, KD, W]) for n in range(RING)]
        own, add_own = sem("own"), sem("add_own")
        idx_ready = [sem(f"idx_ready{half}") for half in range(2)]
        neg_in = [sem(f"neg_in{n}") for n in range(RING)]
        neg_free = [sem(f"neg_free{n}") for n in range(RING)]
        msg_ready, sum_ready = sem("msg_ready"), sem("sum_ready")
        gathered = [nc.alloc_semaphore(f"x_gathered{s}") for s in range(SLOTS)]
        block = ctx.enter_context(nc.Block())

        def load_passes(eng):
            return eng.value_load(c.passes[0:1, 0:1], min_val=1, max_val=TW // W)

        @block.sync
        def _(sp):
            for n in range(RING):
                sp.sem_inc(neg_free[n], 1)
            with sp.Fori(0, load_passes(sp)) as k:
                with sp.Fori(0, IT) as i:
                    for s in range(SLOTS):
                        take(sp, neg_free[s % RING])
                        sp.dma_start(neg[s % RING][:], c.mish_d[bass.ds(i * SLOTS + s, 1)].rearrange("a p j d -> p (a j) d")
                                     ).then_inc(neg_in[s % RING], 16)

        @block.gpsimd
        def _(pool):
            with pool.Fori(0, load_passes(pool)) as k:
                with pool.Fori(0, IT) as i:
                    for half in range(2):
                        take(pool, idx_ready[half])
                        for s in range(half * 3, half * 3 + 3):
                            for j in range(CG):
                                col = (s - half * 3) * CG + j
                                pool.indirect_dma_start(
                                    node[s][:, j, :], None, c.t3[:, :],
                                    bass.IndirectOffsetOnAxis(ap=idx[:, half, col:col + 1], axis=0),
                                ).then_inc(gathered[s], 16)

        @block.tensor
        def _(pe):
            with pe.Fori(0, load_passes(pe)) as k:
                with pe.Fori(0, IT) as i:
                    for s in range(SLOTS):
                        n = s % RING
                        take(pe, msg_ready)
                        for m in range(KD):
                            for j in range(CG):
                                last = pe.matmul(ps_a[n][:, m, :], node[s][:, j, m * P:(m + 1) * P], hot[n][:, j, :],
                                                 start=j == 0, stop=j == CG - 1)
                        last.then_inc(sum_ready, 1)

        @block.scalar
        def _(act):
            with act.Fori(0, load_passes(act)) as k:
                with act.Fori(0, IT) as i:
                    for s in range(SLOTS):
                        take(act, own)
                        act.activation(node[s][:], node[s][:], ACT.Relu).then_inc(msg_ready, 1)

        @block.vector
        def _(dve):
            def message(k, i, s):
                nc.vector.tensor_tensor(hot[s % RING][:], c.iota[:].unsqueeze(1).to_broadcast([P, CG, W]),
                                        rel[:, bass.ds(i * (SLOTS * CG) + s * CG, CG)].unsqueeze(2).to_broadcast([P, CG, W]),
                                        ALU.is_equal)
                take(dve, neg_in[s % RING], 16)
                dve.wait_ge(gathered[s], k * (IT * CG * 16) + i * (CG * 16) + CG * 16)
                nc.vector.tensor_tensor(node[s][:], node[s][:], neg[s % RING][:], ALU.subtract).then_inc(own, 1)

            def add(i, s):
                at = dve.value_load(window[0:1, bass.ds(i * SLOTS + s, 1)], min_val=0, max_val=NP)
                take(dve, sum_ready)
                dve.sem_inc(neg_free[s % RING], 1)
                here = c.feat[:, :, bass.ds(at, W)]
                link(dve, nc.vector.tensor_tensor(here, here, ps_a[s % RING][:], ALU.add), add_own)

            def indices(i, half):
                nc.vector.tensor_copy(idx[:, half, :], c.src[:, bass.ds(i * (SLOTS * CG) + half * HALF_COLS, HALF_COLS)]
                                      ).then_inc(idx_ready[half], 1)

            def step(k, i, final):
                for s in range(SLOTS):
                    message(k, i, s)
                    add(i if s else i - 1, (s - 1) % SLOTS)
                    if s == 0:
                        indices(i, 1)
                    if s == 3 and not final:
                        indices(i + 1, 0)

            nc.vector.tensor_copy(rel[:], c.dstrel[:])
            link(dve, nc.vector.tensor_copy(window[:], c.base[:]), add_own)
            with dve.Fori(0, load_passes(dve)) as k:
                indices(0, 0)
                indices(0, 1)
                for s in range(SLOTS):
                    message(k, 0, s)
                    if s:
                        add(0, s - 1)
                    if s == 3:
                        indices(1, 0)
                with dve.Fori(1, IT - 1) as i:
                    step(k, i, False)
                step(k, IT - 1, True)
                add(IT - 1, SLOTS - 1)
                nc.vector.tensor_scalar(rel[:], rel[:], -float(W), None, ALU.add)
                link(dve, nc.vector.tensor_scalar(window[:], window[:], float(W), float(NP), ALU.add, ALU.min), add_own)


def stage_node_out(nc, c):
    io = c.io
    with ExitStack() as ctx:
        sb = lambda n, shape, dt=FP32: ctx.enter_context(nc.sbuf_tensor(f"o_{n}", shape, dt))
        sem = ctx.enter_context(Signals(nc, "o_"))
        sem2 = lambda name: [sem(f"{name}{n}") for n in range(2)]
        wo = sb("wo", [P, KD, D])
        bias, parts, ones = bias_buffers(sb)
        ln2 = sb("ln2", [P, 1])
        xt = [sb(f"xt{n}", [P, KD, GN]) for n in range(2)]
        q = [sb(f"q{n}", [P, TG, D]) for n in range(2)]
        ps_y = [ctx.enter_context(nc.psum_tensor(f"o_py{n}", [P, TG, D], FP32)) for n in range(2)]
        w_in, own, act_own, parts_ready = sem("w_in"), sem("own"), sem("act_own"), sem("parts_ready")
        moments = Moments(nc, c, sb, sem)
        py_free = sem2("py_free")
        xt_ready, xt_free, py_ready, z_ready, q_ready = sem2("xt_ready"), sem2("xt_free"), sem2("py_ready"), sem2("z_ready"), sem2("q_ready")
        block = ctx.enter_context(nc.Block())

        @block.sync
        def _(sp):
            sp.dma_start(wo[:], io["l_wo"]).then_inc(w_in, 16)
            sp.dma_start(bias[0][:], io["l_bo"]).then_inc(w_in, 16)

        @block.gpsimd
        def _(pool):
            def copy(g, n):
                take(pool, xt_free[n])
                nc.gpsimd.tensor_copy(xt[n][:], c.feat[:, :, bass.ds(g * GN, GN)]).then_inc(xt_ready[n], 1)

            for n in range(2):
                pool.sem_inc(xt_free[n], 1)
            with pool.Fori(0, G // 2) as i:
                for n in range(2):
                    copy(i * 2 + n, n)
            copy(G - 1, 0)

        @block.tensor
        def _(pe):
            def product(n):
                take(pe, xt_ready[n])
                take(pe, py_free[n])
                for s in range(TG):
                    for k in range(KD):
                        pe.matmul(ps_y[n][:, s, :], xt[n][:, k, s * P:(s + 1) * P], wo[:, k, :], start=k == 0, stop=False)
                    last = pe.matmul(ps_y[n][:, s, :], ones[:], parts[:], start=False, stop=True)
                last.then_inc(py_ready[n], 1)

            pe.wait_ge(parts_ready, 1)
            with pe.Fori(0, G // 2) as i:
                for n in range(2):
                    product(n)
            product(0)

        @block.scalar
        def _(act):
            def factor(n):
                take(act, z_ready[n])
                mish_factor(act, q[n][:], ln2, act_own, q_ready[n])

            act.wait_ge(parts_ready, 1)
            log_exp_table(act)
            with act.Fori(0, G // 2) as i:
                for n in range(2):
                    factor(n)
            factor(0)

        @block.vector
        def _(dve):
            def begin(n):
                take(dve, py_ready[n])
                dve.sem_inc(xt_free[n], 1)
                nc.vector.tensor_scalar(q[n][:], ps_y[n][:], ZMAX, None, ALU.min).then_inc(z_ready[n], 1)

            def finish(g, n):
                x = c.x[:, bass.ds(g * TG, TG), :]
                take(dve, q_ready[n])
                link(dve, nc.vector.scalar_tensor_tensor(q[n][:], q[n][:], -1.0, ps_y[n][:], ALU.add, ALU.mult), own)
                dve.sem_inc(py_free[n], 1)
                link(dve, nc.vector.tensor_tensor(x, x, q[n][:], ALU.subtract), own)
                moments.of(dve, g)

            for n in range(2):
                dve.sem_inc(py_free[n], 1)
            nc.vector.memset(ln2[:], LN2)
            nc.vector.memset(ones[:], 1.0)
            dve.wait_ge(w_in, 32)
            split_bias(dve, nc, c, bias, parts, own)
            dve.sem_inc(parts_ready, 2)
            begin(0)
            begin(1)
            finish(0, 0)
            with dve.Fori(1, G // 2) as i:
                begin(0)
                finish(i * 2 - 1, 1)
                begin(1)
                finish(i * 2, 0)
            begin(0)
            finish(G - 2, 1)
            finish(G - 1, 0)


def build(nc, io, out):
    with ExitStack() as ctx:
        c = Chip(nc, ctx, io)
        stage_setup(nc, c)
        stage_deviation(nc, c, "ln0")
        stage_support(nc, c)
        with c.feature_table("sums_table"):
            stage_conv(nc, c, 0, c.t1)
            stage_hidden(nc, c)
            stage_conv(nc, c, 1, c.t2)
            stage_convolved(nc, c)
        stage_deviation(nc, c, "ln1")
        stage_route(nc, c, 0)
        stage_scatter(nc, c, 0)
        stage_experts(nc, c, 0)
        stage_combine(nc, c, 0)
        stage_deviation(nc, c, "ln2")
        with c.feature_table("messages_table"):
            stage_node_mish(nc, c)
            stage_edges(nc, c)
            stage_node_out(nc, c)
        stage_deviation(nc, c, "ln3")
        stage_route(nc, c, 1)
        stage_scatter(nc, c, 1)
        stage_experts(nc, c, 1)
        stage_combine(nc, c, 1)
        with nc.semaphore("stored") as stored, nc.Block() as block:
            @block.sync
            def _(sp):
                sp.dma_start(out[0:WHOLE * P, :].rearrange("(t p) d -> p t d", p=P), c.x[:, 0:WHOLE, :]).then_inc(stored, 16)
                sp.dma_start(out[WHOLE * P:N, :], c.x[0:N - WHOLE * P, WHOLE, :]).then_inc(stored, 16)
                sp.wait_ge(stored, 32)


def kernel(**inp):
    import concourse.bacc as bacc
    from concourse.bass_utils import run_bass_kernel_spmd as run
    nc = bacc.Bacc("TRN2", target_bir_lowering=False, num_devices=1)

    def padded(a, n, value=0):
        return np.concatenate([a, np.full((n - a.shape[0],) + a.shape[1:], value, a.dtype)])

    def blocks(w):
        return w.reshape(-1, P, w.shape[-1]).transpose(1, 0, 2)

    def experts(w):
        return np.stack([blocks(one) for one in w])

    a = {k: np.asarray(v) for k, v in inp.items()}
    dst = padded(a["dst"], C * P, N)
    arrays = {
        "x": padded(a["x"], NP),
        "src_t": padded(a["src"], C * P).reshape(C, P).T,
        "dst_t": dst.reshape(C, P).T,
        "dst_g": dst.reshape(2, EGP, CG * P).transpose(1, 0, 2),
        "weight_t": padded(a["edge_weight"], C * P).reshape(C, P).T,
        "iota": np.broadcast_to(np.arange(W, dtype=np.float32), (P, W)),
        "ident": np.eye(P, dtype=np.float32),
        "real": (np.arange(NT)[None, :] * P + np.arange(P)[:, None] < N).astype(np.float32),
        "before": np.triu(np.ones((P, P), np.float32), 1),
        "iota8": np.broadcast_to(np.arange(8, dtype=np.float32), (P, 8)),
        "edge_t": padded(a["edge_attr_256"], C * P).reshape(EG, CG * P, KD, P).transpose(0, 3, 2, 1),
        "r0_w1": blocks(a["L0_ffn_router_w1"]),
        "r0_b1": a["L0_ffn_router_b1"][:, None],
        "r0_w2": a["L0_ffn_router_w2"],
        "r0_b2": np.broadcast_to(a["L0_ffn_router_b2"], (P, E0)),
        "m0_w1": experts(a["L0_ffn_expert_w1"]),
        "m0_w2": experts(a["L0_ffn_expert_w2"]),
        "m0_w3": experts(a["L0_ffn_expert_w3"]),
        "m0_b1": a["L0_ffn_expert_b1"].reshape(E0, KD, P).transpose(2, 0, 1),
        "m0_b2": a["L0_ffn_expert_b2"].reshape(E0, KD, P).transpose(2, 0, 1),
        "m0_blast": np.broadcast_to(a["L0_ffn_expert_b3"], (P, E0, D)),
        "l_wd": blocks(a["L1_gnn_W_dense"].T),
        "l_bd": np.broadcast_to(a["L1_gnn_b_dense"], (3, D)),
        "l_we": blocks(a["L1_gnn_W_edge"].T),
        "l_be": np.broadcast_to(a["L1_gnn_b_edge"], (3, D)),
        "l_wo": blocks(a["L1_gnn_W_out"].T),
        "l_bo": np.broadcast_to(a["L1_gnn_b_out"], (3, D)),
        "r1_gamma": a["L1_ffn_gamma"].reshape(KD, P).T,
        "r1_beta": a["L1_ffn_beta"].reshape(KD, P).T,
        "r1_w2": blocks(a["L1_ffn_Wr"]),
        "r1_b2": np.broadcast_to(a["L1_ffn_br"], (P, E1)),
        "m1_w1": experts(a["L1_ffn_W1"]),
        "m1_w2": experts(a["L1_ffn_W2"]),
        "m1_b1": a["L1_ffn_b1"].reshape(E1, HM, P).transpose(2, 0, 1),
        "m1_blast": np.broadcast_to(a["L1_ffn_b2"], (P, E1, D)),
        "g_w1": blocks(a["L0_gnn_W1"]),
        "g_b1": a["L0_gnn_b1"][:, None],
        "g_w2": a["L0_gnn_W2"],
        "g_b2": np.broadcast_to(a["L0_gnn_b2"], (P, D)),
    }
    arrays = {k: np.ascontiguousarray(v) for k, v in arrays.items()}
    io = {k: nc.dram_tensor("in_" + k, v.shape, mybir.dt.from_np(v.dtype), kind="ExternalInput").ap() for k, v in arrays.items()}
    out = nc.dram_tensor("out", (N, D), FP32, kind="ExternalOutput").ap()
    build(nc, io, out)
    r = run(nc, [{"in_" + k: v for k, v in arrays.items()}], core_ids=[0])
    return r.results[0]["out"]
```
